# Optimizing a Trainium2 kernel written in Bass

```python
import numpy as np
import jax
import jax.numpy as jnp

def _softmax(x, axis=-1):
    return jax.nn.softmax(x, axis=axis)

def _gelu(x):
    return jax.nn.gelu(x, approximate=True)

def _silu(x):
    return jax.nn.silu(x)

def _sigmoid(x):
    return jax.nn.sigmoid(x)

def _layernorm(x, axis=-1, eps=1e-05):
    m = jnp.mean(x, axis=axis, keepdims=True)
    v = jnp.var(x, axis=axis, keepdims=True)
    return (x - m) / jnp.sqrt(v + eps)

def _scatter_add(tgt, idx, src, axis=0):
    return tgt.at[idx].add(src)

def _segment_sum(src, seg, n):
    return jax.ops.segment_sum(src, seg, n)
kernel_name = 'mk_lm_tower_d2_tok_ids1024_r4_ac0129'

def setup_inputs(seed: int=0):
    np.random.seed(seed)
    _w = jnp.asarray

    def _rec_inputs():
        import jax
        import jax.numpy as jnp
        _rk = jax.random.key(seed)
        x = jax.random.randint(jax.random.fold_in(_rk, 1), (16, 256), 0, 64, jnp.int32)
        return x
    x = _rec_inputs()

    def _L0_tok_setup():
        import jax, jax.numpy as jnp
        import numpy as np
        N_FFT = 64
        HOP = 64
        NUM_FREQ = N_FFT // 2 + 1

        def _stft_mag(sig, window):
            L = sig.shape[1]
            pad = N_FFT // 2
            x = jnp.pad(sig, ((0, 0), (pad, pad)), mode='reflect')
            n_frames = 1 + L // HOP
            idx = jnp.arange(n_frames)[:, None] * HOP + jnp.arange(N_FFT)[None, :]
            frames = x[:, idx] * window
            spec = jnp.fft.rfft(frames, axis=-1)
            r, im = (spec.real, spec.imag)
            m2 = r * r + im * im
            mag = jnp.where(m2 == 0, 0.0, jnp.sqrt(jnp.where(m2 == 0, 1.0, m2)))
            return (mag, n_frames)

        def _linear_interp_last(feat, out_len):
            in_len = feat.shape[-1]
            coord = jnp.clip((jnp.arange(out_len) + 0.5) * (in_len / out_len) - 0.5, 0.0, in_len - 1.0)
            i0 = jnp.floor(coord).astype(jnp.int32)
            i1 = jnp.minimum(i0 + 1, in_len - 1)
            w = (coord - i0).astype(feat.dtype)
            return feat[..., i0] * (1.0 - w) + feat[..., i1] * w
        key = jax.random.key(seed)
        k0, k1, k2 = jax.random.split(key, 3)
        B, L, V, d_model = (2, 256, 64, 256)
        d_emb = int(d_model * 0.7)
        d_stft = d_model - d_emb
        input_ids = jax.random.randint(k0, (B, L), 0, V)
        emb_table = jax.random.normal(k1, (V, d_emb), jnp.float32) * 0.02
        proj_w = jax.random.normal(k2, (d_stft, V * NUM_FREQ), jnp.float32) * 0.02
        proj_b = jnp.zeros((d_stft,), jnp.float32)
        n = jnp.arange(N_FFT, dtype=jnp.float32)
        window = 0.5 * (1.0 - jnp.cos(2.0 * jnp.pi * n / N_FFT))
        return {'input_ids': input_ids, 'emb_table': emb_table, 'proj_w': proj_w, 'proj_b': proj_b, 'window': window}
    _L0_tok_all = _L0_tok_setup()
    _L0_tok_in = {k: v for k, v in _L0_tok_all.items() if k in ('emb_table', 'proj_w', 'proj_b', 'window')}
    del _L0_tok_all

    def _L0_attn_setup():
        import math
        import jax, jax.numpy as jnp
        import numpy as np
        B, L, D_MODEL, N_HEADS = (4, 1024, 256, 16)
        HEAD_DIM = D_MODEL // N_HEADS
        NUM_LANDMARKS = 128

        def _split_heads(t):
            b, l, _ = t.shape
            return t.reshape(b, l, N_HEADS, HEAD_DIM).transpose(0, 2, 1, 3)

        def _iterative_inv(mat, n_iter=6):
            I = jnp.eye(mat.shape[-1], dtype=mat.dtype)
            K = mat
            V = K.swapaxes(-1, -2) / jnp.max(jnp.sum(K, axis=-2))
            for _ in range(n_iter):
                KV = jnp.matmul(K, V)
                V = jnp.matmul(0.25 * V, 13.0 * I - jnp.matmul(KV, 15.0 * I - jnp.matmul(KV, 7.0 * I - KV)))
            return V
        key = jax.random.key(seed)
        ks = jax.random.split(key, 7)
        s = 1.0 / math.sqrt(D_MODEL)
        return {'x': jax.random.normal(ks[0], (B, L, D_MODEL), dtype=jnp.float32), 'Wq': jax.random.uniform(ks[1], (D_MODEL, D_MODEL), jnp.float32, -s, s), 'bq': jax.random.uniform(ks[2], (D_MODEL,), jnp.float32, -s, s), 'Wk': jax.random.uniform(ks[3], (D_MODEL, D_MODEL), jnp.float32, -s, s), 'bk': jax.random.uniform(ks[4], (D_MODEL,), jnp.float32, -s, s), 'Wv': jax.random.uniform(ks[5], (D_MODEL, D_MODEL), jnp.float32, -s, s), 'bv': jax.random.uniform(ks[6], (D_MODEL,), jnp.float32, -s, s)}
    _L0_attn_all = _L0_attn_setup()
    _L0_attn_in = {k: v for k, v in _L0_attn_all.items() if k in ('Wq', 'bq', 'Wk', 'bk', 'Wv', 'bv')}
    del _L0_attn_all

    def _L0_ffn_setup():
        import jax, jax.numpy as jnp
        import numpy as np
        EPS = 1e-05

        @jax.custom_vjp
        def ste_quantize(w):
            scale = jnp.maximum(jnp.mean(jnp.abs(w)), EPS)
            return jnp.clip(jnp.round(w / scale), -1.0, 1.0)

        def _ste_fwd(w):
            return (ste_quantize(w), None)

        def _ste_bwd(_, g):
            return (g,)
        ste_quantize.defvjp(_ste_fwd, _ste_bwd)
        key = jax.random.key(seed)
        k1, k2 = jax.random.split(key)
        x = jax.random.normal(k1, (8, 2048, 256), dtype=jnp.float32)
        weight = jax.random.normal(k2, (256, 256), dtype=jnp.float32) * 0.02
        return {'x': x, 'weight': weight}
    _L0_ffn_all = _L0_ffn_setup()
    _L0_ffn_in = {k: v for k, v in _L0_ffn_all.items() if k in ('weight',)}
    del _L0_ffn_all

    def _L1_attn_setup():
        import math
        import jax, jax.numpy as jnp
        import numpy as np
        B, S, E, H = (4, 512, 256, 16)
        HD = E // H
        key = jax.random.key(seed)
        ks = jax.random.split(key, 7)
        scale = 1.0 / math.sqrt(E)
        return {'x': jax.random.normal(ks[0], (B, S, E), dtype=jnp.float32), 'Wq': jax.random.normal(ks[1], (H, HD, E), dtype=jnp.float32) * scale, 'bq': jax.random.normal(ks[2], (H, HD), dtype=jnp.float32) * 0.01, 'Wk': jax.random.normal(ks[3], (H, HD, E), dtype=jnp.float32) * scale, 'bk': jax.random.normal(ks[4], (H, HD), dtype=jnp.float32) * 0.01, 'Wv': jax.random.normal(ks[5], (H, HD, E), dtype=jnp.float32) * scale, 'bv': jax.random.normal(ks[6], (H, HD), dtype=jnp.float32) * 0.01}
    _L1_attn_all = _L1_attn_setup()
    _L1_attn_in = {k: v for k, v in _L1_attn_all.items() if k in ('Wq', 'bq', 'Wk', 'bk', 'Wv', 'bv')}
    del _L1_attn_all

    def _L1_ffn_setup():
        import jax, jax.numpy as jnp
        import numpy as np
        B, N, D = (4, 512, 256)
        SPARSITY = 0.01
        key = jax.random.key(seed)
        k1, k2, k3 = jax.random.split(key, 3)
        x = jax.random.normal(k1, (B, N, D), dtype=jnp.float32)
        spatial = jax.random.normal(k2, (D, D), dtype=jnp.float32) * 0.02
        freq = jnp.fft.fft(spatial, axis=-1)
        k = int(D * SPARSITY)
        mag = jnp.abs(freq)
        kth = jax.lax.top_k(mag, k)[0][:, -1:]
        w_sparse = jnp.where(mag >= kth, freq, 0.0 + 0j)
        bias = jax.random.normal(k3, (D,), dtype=jnp.float32) * 0.01
        return {'x': x, 'w_freq_real': jnp.real(w_sparse).astype(jnp.float32), 'w_freq_imag': jnp.imag(w_sparse).astype(jnp.float32), 'bias': bias}
    _L1_ffn_all = _L1_ffn_setup()
    _L1_ffn_in = {k: v for k, v in _L1_ffn_all.items() if k in ('w_freq_real', 'w_freq_imag', 'bias')}
    del _L1_ffn_all
    return {'x': x, 'L0_tok_emb_table': _L0_tok_in['emb_table'], 'L0_tok_proj_w': _L0_tok_in['proj_w'], 'L0_tok_proj_b': _L0_tok_in['proj_b'], 'L0_tok_window': _L0_tok_in['window'], 'L0_attn_Wq': _L0_attn_in['Wq'], 'L0_attn_bq': _L0_attn_in['bq'], 'L0_attn_Wk': _L0_attn_in['Wk'], 'L0_attn_bk': _L0_attn_in['bk'], 'L0_attn_Wv': _L0_attn_in['Wv'], 'L0_attn_bv': _L0_attn_in['bv'], 'L0_ffn_weight': _L0_ffn_in['weight'], 'L1_attn_Wq': _L1_attn_in['Wq'], 'L1_attn_bq': _L1_attn_in['bq'], 'L1_attn_Wk': _L1_attn_in['Wk'], 'L1_attn_bk': _L1_attn_in['bk'], 'L1_attn_Wv': _L1_attn_in['Wv'], 'L1_attn_bv': _L1_attn_in['bv'], 'L1_ffn_w_freq_real': _L1_ffn_in['w_freq_real'], 'L1_ffn_w_freq_imag': _L1_ffn_in['w_freq_imag'], 'L1_ffn_bias': _L1_ffn_in['bias']}

def reference(x, L0_tok_emb_table, L0_tok_proj_w, L0_tok_proj_b, L0_tok_window, L0_attn_Wq, L0_attn_bq, L0_attn_Wk, L0_attn_bk, L0_attn_Wv, L0_attn_bv, L0_ffn_weight, L1_attn_Wq, L1_attn_bq, L1_attn_Wk, L1_attn_bk, L1_attn_Wv, L1_attn_bv, L1_ffn_w_freq_real, L1_ffn_w_freq_imag, L1_ffn_bias):
    import jax
    import jax.numpy as jnp

    def _L0_tok_ref(input_ids, emb_table, proj_w, proj_b, window):
        import jax, jax.numpy as jnp
        import numpy as np
        N_FFT = 64
        HOP = 64
        NUM_FREQ = N_FFT // 2 + 1

        def _stft_mag(sig, window):
            L = sig.shape[1]
            pad = N_FFT // 2
            x = jnp.pad(sig, ((0, 0), (pad, pad)), mode='reflect')
            n_frames = 1 + L // HOP
            idx = jnp.arange(n_frames)[:, None] * HOP + jnp.arange(N_FFT)[None, :]
            frames = x[:, idx] * window
            spec = jnp.fft.rfft(frames, axis=-1)
            r, im = (spec.real, spec.imag)
            m2 = r * r + im * im
            mag = jnp.where(m2 == 0, 0.0, jnp.sqrt(jnp.where(m2 == 0, 1.0, m2)))
            return (mag, n_frames)

        def _linear_interp_last(feat, out_len):
            in_len = feat.shape[-1]
            coord = jnp.clip((jnp.arange(out_len) + 0.5) * (in_len / out_len) - 0.5, 0.0, in_len - 1.0)
            i0 = jnp.floor(coord).astype(jnp.int32)
            i1 = jnp.minimum(i0 + 1, in_len - 1)
            w = (coord - i0).astype(feat.dtype)
            return feat[..., i0] * (1.0 - w) + feat[..., i1] * w
        B, L = input_ids.shape
        V = emb_table.shape[0]
        word_embeds = emb_table[input_ids]
        sig = jax.nn.one_hot(input_ids, V, dtype=jnp.float32)
        sig = jnp.transpose(sig, (0, 2, 1)).reshape(B * V, L)
        mag, T = _stft_mag(sig, window)
        feat = mag.reshape(B, V, T, NUM_FREQ).transpose(0, 3, 1, 2)
        feat = feat.reshape(B, NUM_FREQ * V, T)
        up = _linear_interp_last(feat, L)
        stft_feat = jnp.transpose(up, (0, 2, 1))
        stft_enc = stft_feat @ proj_w.T + proj_b
        return jnp.concatenate([word_embeds, stft_enc], axis=-1)

    def _L0_attn_ref(x, Wq, bq, Wk, bk, Wv, bv):
        import math
        import jax, jax.numpy as jnp
        import numpy as np
        B, L, D_MODEL, N_HEADS = (4, 1024, 256, 16)
        HEAD_DIM = D_MODEL // N_HEADS
        NUM_LANDMARKS = 128

        def _split_heads(t):
            b, l, _ = t.shape
            return t.reshape(b, l, N_HEADS, HEAD_DIM).transpose(0, 2, 1, 3)

        def _iterative_inv(mat, n_iter=6):
            I = jnp.eye(mat.shape[-1], dtype=mat.dtype)
            K = mat
            V = K.swapaxes(-1, -2) / jnp.max(jnp.sum(K, axis=-2))
            for _ in range(n_iter):
                KV = jnp.matmul(K, V)
                V = jnp.matmul(0.25 * V, 13.0 * I - jnp.matmul(KV, 15.0 * I - jnp.matmul(KV, 7.0 * I - KV)))
            return V
        Q = _split_heads(x @ Wq.T + bq)
        K = _split_heads(x @ Wk.T + bk)
        V = _split_heads(x @ Wv.T + bv)
        b, h, l, d = Q.shape
        scale = 1.0 / math.sqrt(math.sqrt(HEAD_DIM))
        Q = Q * scale
        K = K * scale
        seg = l // NUM_LANDMARKS
        Q_lm = Q.reshape(b, h, NUM_LANDMARKS, seg, d).mean(axis=-2)
        K_lm = K.reshape(b, h, NUM_LANDMARKS, seg, d).mean(axis=-2)
        kernel_1 = jax.nn.softmax(jnp.einsum('bhld,bhmd->bhlm', Q, K_lm), axis=-1)
        kernel_2 = jax.nn.softmax(jnp.einsum('bhmd,bhnd->bhmn', Q_lm, K_lm), axis=-1)
        kernel_3 = jax.nn.softmax(jnp.einsum('bhmd,bhld->bhml', Q_lm, K), axis=-1)
        X = jnp.matmul(jnp.matmul(kernel_1, _iterative_inv(kernel_2)), jnp.matmul(kernel_3, V))
        out = X.transpose(0, 2, 1, 3).reshape(b, l, h * d)
        return out

    def _L0_ffn_ref(x, weight):
        import jax, jax.numpy as jnp
        import numpy as np
        EPS = 1e-05

        @jax.custom_vjp
        def ste_quantize(w):
            scale = jnp.maximum(jnp.mean(jnp.abs(w)), EPS)
            return jnp.clip(jnp.round(w / scale), -1.0, 1.0)

        def _ste_fwd(w):
            return (ste_quantize(w), None)

        def _ste_bwd(_, g):
            return (g,)
        ste_quantize.defvjp(_ste_fwd, _ste_bwd)
        w_ternary = ste_quantize(weight)
        scale = jnp.maximum(jnp.mean(jnp.abs(weight)), EPS)
        return jnp.einsum('bsi,oi->bso', x, w_ternary * scale)

    def _L1_attn_ref(x, Wq, bq, Wk, bk, Wv, bv):
        import math
        import jax, jax.numpy as jnp
        import numpy as np
        B, S, E, H = (4, 512, 256, 16)
        HD = E // H
        b, s, e = x.shape
        h, hd, _ = Wq.shape
        inv_scale = 1.0 / math.sqrt(hd)
        q = jnp.einsum('bse,hde->bshd', x, Wq) + bq
        k = jnp.einsum('bse,hde->bshd', x, Wk) + bk
        v = jnp.einsum('bse,hde->bshd', x, Wv) + bv
        mask = jnp.triu(jnp.full((s, s), -jnp.inf, dtype=x.dtype), k=1)
        scores = (jnp.einsum('bqhd,bkhd->bhqk', q, k) + mask) * inv_scale
        attn = jax.nn.softmax(scores, axis=-1)
        out = jnp.einsum('bhqk,bkhd->bqhd', attn, v)
        return out.reshape(b, s, h * hd)

    def _L1_ffn_ref(x, w_freq_real, w_freq_imag, bias):
        import jax, jax.numpy as jnp
        import numpy as np
        B, N, D = (4, 512, 256)
        SPARSITY = 0.01
        w = jax.lax.complex(w_freq_real, w_freq_imag)
        x_freq = jnp.fft.fft(x, axis=-1)
        y_freq = jnp.einsum('bnd,do->bno', x_freq, w)
        y = jnp.real(jnp.fft.ifft(y_freq, axis=-1))
        return y + bias
    h = _L0_tok_ref(x, L0_tok_emb_table, L0_tok_proj_w, L0_tok_proj_b, L0_tok_window)
    h = h + _L0_attn_ref(_layernorm(h, axis=-1), L0_attn_Wq, L0_attn_bq, L0_attn_Wk, L0_attn_bk, L0_attn_Wv, L0_attn_bv)
    h = h + _L0_ffn_ref(_layernorm(h, axis=-1), L0_ffn_weight)
    h = h + _L1_attn_ref(_layernorm(h, axis=-1), L1_attn_Wq, L1_attn_bq, L1_attn_Wk, L1_attn_bk, L1_attn_Wv, L1_attn_bv)
    h = h + _L1_ffn_ref(_layernorm(h, axis=-1), L1_ffn_w_freq_real, L1_ffn_w_freq_imag, L1_ffn_bias)
    return h

_drawn_inputs = setup_inputs


def setup_inputs(seed=0):
    import zlib

    import numpy as np

    out = dict(_drawn_inputs(seed))
    spreads = {'L0_tok_proj_b': (0.0, 0.1)}
    factors = {'L0_tok_emb_table': 2.947,
     'L0_attn_bq': 8.0,
     'L0_attn_bk': 64.0,
     'L1_attn_bq': 64.0,
     'L1_attn_bk': 64.0,
     'L1_attn_bv': 6.838,
     'L1_ffn_bias': 8.0}
    for name, (base, spread) in spreads.items():
        noise = np.random.default_rng([zlib.crc32(name.encode()), seed]).standard_normal(out[name].shape)
        drawn = base * np.exp(spread * noise) if base else spread * noise
        out[name] = jnp.asarray(drawn.astype(out[name].dtype))
    for name, factor in factors.items():
        out[name] = (out[name] * factor).astype(out[name].dtype)
    return out
```

```python
from contextlib import ExitStack

import numpy as np
import concourse.bass as bass
from concourse import mybir

F32 = mybir.dt.float32
BF16 = mybir.dt.bfloat16
I32 = mybir.dt.int32
ALU = mybir.AluOpType
ACT = mybir.ActivationFunctionType
AX = mybir.AxisListType

P = 128
NB, L, D = 16, 256, 256
NT = L // P
NK = D // P
H, HD = 16, 16
SLOT = 32
J = P // SLOT
G = H // J
ONE = HD
M = 128
V, NFFT = 64, 64
NFR = L // NFFT + 1
NFQ = NFFT // 2 + 1
PAIRS = NB * NFR // 2
DE = 179
DS = D - DE
EPS = 1e-5
ITERS = 6
U, NU = 2, 4
EW = P + HD
NEG = -1e30


def build(nc, t):
    ctx = ExitStack()
    with ctx:
        def sb(name, shape, dt=F32, where=None):
            return (where or ctx).enter_context(nc.sbuf_tensor(name, shape, dt))

        def sem(name):
            return ctx.enter_context(nc.semaphore(name))

        k2_dram = nc.dram_tensor("k2_scratch", [NB, P, H * M], F32, kind="Internal").ap()

        h = sb("h", [P, NB * NT, D])
        ident = sb("ident", [P, P])
        pairing = sb("pairing", [P, P // 2])
        half = sb("half", [P, 4])
        passed = sb("passed", [P, 4])
        wq = [sb(f"wq{n}", [P, NK, G * P]) for n in range(2)]
        wk = [sb(f"wk{n}", [P, NK, G * P]) for n in range(2)]
        wv = [sb(f"wv{n}", [P, NK, D]) for n in range(2)]
        bq = [sb(f"bq{n}", [P, G]) for n in range(2)]
        bk = [sb(f"bk{n}", [P, G]) for n in range(2)]
        bv = [sb(f"bv{n}", [P, D]) for n in range(2)]
        wt = sb("wt", [P, NK, D])
        wf = sb("wf", [P, NK, D])
        bf = sb("bf", [P, D])
        mask = sb("mask", [P, 2, 2 * P], BF16)
        identb = sb("identb", [P, P], BF16)
        minv = sb("minv", [P, 2])
        stats = sb("stats", [P, NT, 6])
        mv = sb("mv", [P, NT, 2])
        rstd = sb("rstd", [P, NT])
        y = sb("y", [P, NT, D])
        yT = sb("yT", [P, NK, L])

        ps = ctx.enter_context(nc.psum_tensor("ps", [P, 8, 512], F32))

        def bank(n, k=1):
            return ps[:, n, :] if k == 1 else ps[:, n:n + k, :]

        class Steps:

            def __init__(self, per):
                self.per, self.n = per, 0

            def next(self, b=0):
                self.n += 1
                return b * self.per + self.n

            def end(self):
                assert self.n == self.per, self.n

        with ExitStack() as tmp:
            ids_all = sb("ids_all", [V, NB * L], I32, tmp)
            ids_fr = sb("ids_fr", [NFFT, 2 * PAIRS], I32, tmp)
            iota_c = sb("iota_c", [V, 1], F32, tmp)
            iota_r = sb("iota_r", [NFFT, V], F32, tmp)
            hotT = sb("hotT", [V, NB * L], F32, tmp)
            hot_fr = sb("hot_fr", [NFFT, PAIRS * 2, V], F32, tmp)
            dft = sb("dft", [NFFT, 2, NFQ], F32, tmp)
            dftw = sb("dftw", [NFFT, 2 * NFQ], F32, tmp)
            window = sb("window", [NFFT, 1], F32, tmp)
            sq = sb("sq", [P, PAIRS, 2 * NFQ], F32, tmp)
            mag = sb("mag", [P, PAIRS, NFQ], F32, tmp)
            live = sb("live", [P, PAIRS, NFQ], F32, tmp)
            wp = sb("wp", [P, NFQ, DS], F32, tmp)
            emb = sb("emb", [V, DE], F32, tmp)
            interp = sb("interp", [PAIRS + 1, 2, NB * L], F32, tmp)
            proj = sb("proj", [PAIRS + 1, 2, DS], F32, tmp)
            mask32 = sb("mask32", [P, 2, 2 * P], F32, tmp)
            fw = sb("fw", [P, NK, D], F32, tmp)
            habs = sb("habs", [P, 1], F32, tmp)
            hsum = sb("hsum", [P, 1], F32, tmp)
            hs = sb("hs", [P, 3], F32, tmp)
            neg = sb("neg", [P, NK, D], F32, tmp)
            cs = sb("cs", [P, 3, NK, D], F32, tmp)
            wri = sb("wri", [P, 2, NK, D], F32, tmp)
            prT = sb("prT", [P, 2, NK, D], F32, tmp)

            in_ids, in_tok, in_fft, in_ffn, in_rest = (sem(s) for s in (
                "in_ids", "in_tok", "in_fft", "in_ffn", "in_rest"))
            hot_fr_ready, hotT_ready, dft_ready = sem("hot_fr_ready"), sem("hotT_ready"), sem("dft_ready")
            spec_ready, sq_ready, m2_ready, mag_ready = (sem(s) for s in (
                "spec_ready", "sq_ready", "m2_ready", "mag_ready"))
            root_ready, proj_ps, proj_ready, tok_ps, tok_done = (sem(s) for s in (
                "root_ready", "proj_ps", "proj_ready", "tok_ps", "tok_done"))
            habs_ready, hsum_ready, ffn_step = sem("habs_ready"), sem("hsum_ready"), sem("ffn_step")
            pr_ps, pr_ready, wf_ps, wf_done = sem("pr_ps"), sem("pr_ready"), sem("wf_ps"), sem("wf_done")
            FPB = PAIRS // 8
            NTILE = NB * NT

            with nc.Block() as block:
                @block.sync
                def _(sp):
                    for dst, src in ((ids_fr[:], t["ids_fr"]), (iota_r[:], t["iota"].partition_broadcast(NFFT)),
                                     (iota_c[:], t["iota_c"]), (dft[:], t["dft"]), (window[:], t["window"])):
                        sp.dma_start(dst, src).then_inc(in_ids, 16)
                    for dst, src in ((wp[:], t["wp"]), (emb[:], t["emb"]), (interp[:], t["interp"]),
                                     (proj[PAIRS:PAIRS + 1, 0, :], t["proj_b"]), (proj[PAIRS:PAIRS + 1, 1, :], t["zero"])):
                        sp.dma_start(dst, src).then_inc(in_tok, 16)
                    for dst, src in ((ident[:], t["ident"]), (pairing[:], t["pairing"]), (half[:], t["half"]),
                                     (mask32[:], t["mask"])):
                        sp.dma_start(dst, src).then_inc(in_rest, 16)
                    sp.wait_ge(in_rest, 16 * (4 + 6 * 2 + 1))

                @block.gpsimd
                def _(pool):
                    pool.wait_ge(habs_ready, 1)
                    pool.partition_all_reduce(hsum[:], habs[:], P, bass.bass_isa.ReduceOp.add).then_inc(hsum_ready, 1)

                @block.scalar
                def _(act):
                    act.dma_start(ids_all[:], t["ids"].partition_broadcast(V)).then_inc(in_ids, 16)
                    act.dma_start(fw[:], t["fw"]).then_inc(in_ffn, 16)
                    act.dma_start(cs[:], t["cs"]).then_inc(in_fft, 16)
                    act.dma_start(wri[:], t["wri"]).then_inc(in_fft, 16)
                    for n in range(2):
                        for dst, name in ((wq, "wq"), (wk, "wk"), (wv, "wv"), (bq, "bq"), (bk, "bk")):
                            act.dma_start(dst[n][:], t[f"{name}{n}"]).then_inc(in_rest, 16)
                        act.dma_start(bv[n][:], t[f"bv{n}"].partition_broadcast(P)).then_inc(in_rest, 16)
                    act.dma_start(bf[:], t["bf"].partition_broadcast(P)).then_inc(in_rest, 16)
                    for n in range(8):
                        act.wait_ge(spec_ready, n + 1)
                        act.activation(sq[:, n * FPB:(n + 1) * FPB, :],
                                       bank(n)[:, 0:FPB * 2 * NFQ].rearrange("p (a f) -> p a f", a=FPB),
                                       ACT.Square).then_inc(sq_ready, 1)
                    act.wait_ge(m2_ready, 1)
                    act.activation(mag[:], mag[:], ACT.Sqrt).then_inc(root_ready, 1)
                    act.wait_ge(pr_ps, 1)
                    act.activation(prT[:], bank(0, 4).rearrange("p (a k) n -> p a k n", a=2)[:, :, :, 0:D],
                                   ACT.Copy).then_inc(pr_ready, 1)
                    act.wait_ge(wf_ps, 1)
                    act.activation(wf[:], bank(4, 2)[:, :, 0:D], ACT.Copy, scale=1.0 / D).then_inc(wf_done, 1)

                @block.vector
                def _(dve):
                    s = Steps(7)
                    dve.wait_ge(in_ids, 16 * 6)
                    dve.tensor_scalar(dftw[:], dft[:].rearrange("n a f -> n (a f)"), window[:, 0:1], None,
                                      ALU.mult).then_inc(dft_ready, 1)
                    dve.tensor_tensor(hot_fr[:], ids_fr[:].unsqueeze(2).to_broadcast([NFFT, 2 * PAIRS, V]),
                                      iota_r[:].unsqueeze(1).to_broadcast([NFFT, 2 * PAIRS, V]),
                                      ALU.is_equal).then_inc(hot_fr_ready, 1)
                    dve.tensor_scalar(hotT[:], ids_all[:], iota_c[:, 0:1], None, ALU.is_equal).then_inc(hotT_ready, 1)
                    dve.wait_ge(in_ffn, 16)
                    dve.tensor_reduce(habs[:], fw[:].rearrange("p k n -> p (k n)"), axis=AX.X, op=ALU.add,
                                      apply_absolute_value=True).then_inc(habs_ready, 1)
                    dve.wait_ge(sq_ready, 8)
                    dve.tensor_tensor(mag[:], sq[:, :, 0:NFQ], sq[:, :, NFQ:2 * NFQ], ALU.add).then_inc(ffn_step, 1)
                    dve.wait_ge(ffn_step, s.next())
                    dve.tensor_scalar(live[:], mag[:], 0.0, None, ALU.is_gt).then_inc(ffn_step, 1)
                    dve.wait_ge(ffn_step, s.next())
                    dve.tensor_scalar(mag[:], mag[:], 1e-34, None, ALU.max).then_inc(m2_ready, 1)
                    dve.wait_ge(root_ready, 1)
                    dve.tensor_tensor(mag[:], mag[:], live[:], ALU.mult).then_inc(mag_ready, 1)
                    dve.wait_ge(proj_ps, 1)
                    dve.tensor_copy(proj[0:PAIRS, :, :], bank(0, 2)[0:PAIRS, :, 0:DS]).then_inc(proj_ready, 1)
                    dve.wait_ge(hsum_ready, 1)
                    dve.tensor_scalar(hs[:, 0:1], hsum[:], 1.0 / (D * D), EPS, ALU.mult, ALU.max).then_inc(ffn_step, 1)
                    dve.wait_ge(ffn_step, s.next())
                    dve.tensor_scalar(hs[:, 1:2], hs[:, 0:1], 0.5, None, ALU.mult).then_inc(ffn_step, 1)
                    dve.wait_ge(ffn_step, s.next())
                    dve.tensor_scalar(hs[:, 2:3], hs[:, 0:1], -0.5, None, ALU.mult).then_inc(ffn_step, 1)
                    dve.wait_ge(ffn_step, s.next())
                    dve.tensor_scalar(wt[:], fw[:], hs[:, 1:2], hs[:, 0:1], ALU.is_gt, ALU.mult).then_inc(ffn_step, 1)
                    dve.wait_ge(ffn_step, s.next())
                    dve.tensor_scalar(neg[:], fw[:], hs[:, 2:3], hs[:, 0:1], ALU.is_lt, ALU.mult).then_inc(ffn_step, 1)
                    dve.wait_ge(ffn_step, s.next())
                    dve.tensor_tensor(wt[:], wt[:], neg[:], ALU.subtract)
                    dve.wait_ge(in_rest, 16 * (4 + 6 * 2 + 1))
                    dve.tensor_copy(mask[:], mask32[:])
                    dve.tensor_copy(identb[:], ident[:])
                    for n in range(NTILE // 4):
                        dve.wait_ge(tok_ps, n + 1)
                        b0 = 2 * (n % 2)
                        dve.tensor_copy(h[:, 4 * n:4 * n + 4, :].rearrange("p (a c) d -> p a (c d)", a=2),
                                        bank(4 + b0, 2)).then_inc(tok_done, 1)
                    s.end()

                @block.tensor
                def _(pe):
                    pe.wait_ge(hot_fr_ready, 1)
                    pe.wait_ge(dft_ready, 1)
                    for n in range(8):
                        for i in range(FPB):
                            pair = n * FPB + i
                            last = pe.matmul(bank(n)[:, i * 2 * NFQ:(i + 1) * 2 * NFQ],
                                             hot_fr[:, 2 * pair:2 * pair + 2, :].rearrange("n a v -> n (a v)"),
                                             dftw[:], start=True, stop=True)
                        last.then_inc(spec_ready, 1)
                    pe.wait_ge(mag_ready, 1)
                    pe.wait_ge(in_tok, 16 * 5)
                    for a in range(2):
                        rows = slice(V * a, V * a + V)
                        for f in range(NFQ):
                            last = pe.matmul(bank(a)[0:PAIRS, 0:DS], mag[rows, :, f], wp[rows, f, :],
                                             start=f == 0, stop=f == NFQ - 1)
                    last.then_inc(proj_ps, 1)
                    pe.wait_ge(proj_ready, 1)
                    pe.wait_ge(hotT_ready, 1)
                    for n in range(NTILE // 4):
                        if n >= 2:
                            pe.wait_ge(tok_done, n - 1)
                        for i in range(4):
                            tok = slice((4 * n + i) * P, (4 * n + i + 1) * P)
                            out = bank(4 + 2 * (n % 2) + i // 2)[:, (i % 2) * D:(i % 2 + 1) * D]
                            pe.matmul(out[:, 0:DE], hotT[:, tok], emb[:], start=True, stop=True)
                            for a in range(2):
                                last = pe.matmul(out[:, DE:D], interp[:, a, tok], proj[:, a, :],
                                                 start=a == 0, stop=a == 1)
                        last.then_inc(tok_ps, 1)
                    pe.wait_ge(in_fft, 32)
                    for a in range(2):
                        for o in range(NK):
                            cols = slice(o * P, o * P + P)
                            for k in range(NK):
                                pe.matmul(bank(2 * a + o)[:, 0:D], wri[:, a, k, cols], cs[:, 0, k, :],
                                          start=k == 0, stop=False)
                                last = pe.matmul(bank(2 * a + o)[:, 0:D], wri[:, 1 - a, k, cols],
                                                 cs[:, 1 + a, k, :], start=False, stop=k == NK - 1)
                    last.then_inc(pr_ps, 1)
                    pe.wait_ge(pr_ready, 1)
                    pe.wait_ge(tok_done, NTILE // 4)
                    for o in range(NK):
                        cols = slice(o * P, o * P + P)
                        for k in range(NK):
                            pe.matmul(bank(4 + o)[:, 0:D], prT[:, 0, k, cols], cs[:, 0, k, :],
                                      start=k == 0, stop=False)
                            last = pe.matmul(bank(4 + o)[:, 0:D], prT[:, 1, k, cols], cs[:, 2, k, :],
                                             start=False, stop=k == NK - 1)
                    last.then_inc(wf_ps, 1)

        def ln_statistics(dve, b, chain, s, ready):
            for i in range(NT):
                dve.bn_stats(stats[:, i, :], h[:, b * NT + i, :]).then_inc(chain, 1)
                n = s.next(b)
            dve.wait_ge(chain, n)
            dve.tensor_copy(passed[:], half[:])
            for i in range(NT):
                dve.bn_aggr(mv[:, i, :], stats[:, i, :]).then_inc(ready, 1)

        def ln_rstd(pool, q, statistics, chain, ready):
            pool.wait_ge(statistics, q * NT + NT)
            pool.tensor_tensor(rstd[:], mv[:, :, 1], half[:, 2:4], ALU.add).then_inc(chain, 1)
            pool.wait_ge(chain, q + 1)
            pool.tensor_tensor(rstd[:], rstd[:], half[:, 0:2], ALU.pow).then_inc(ready, 1)

        def ln_scale(dve, b, q, rstd_ready, ready):
            dve.wait_ge(rstd_ready, q + 1)
            for i in range(NT):
                dve.tensor_scalar(y[:, i, :], h[:, b * NT + i, :], mv[:, i, 0:1], rstd[:, i:i + 1],
                                  ALU.subtract, ALU.mult).then_inc(ready, 1)

        def slotted(ap, width):
            return ap.rearrange("p (h w) -> p h w", w=width)


        xT = sb("xT", [P, G, L])
        xden = sb("xden", [P, NT, H])
        xo = sb("xo", [P, NT, D])
        va = sb("va", [P, NT, H, SLOT])
        qT = sb("qT", [P, G, L])
        kT = sb("kT", [P, G, L])

        def transpose_y(pe, ready):
            for k in range(NK):
                for i in range(NT):
                    last = pe.transpose(bank(4)[:, k * L + i * P:k * L + (i + 1) * P], y[:, i, k * P:(k + 1) * P],
                                        ident[:])
            last.then_inc(ready, 1)

        def project(pe, n, ready):
            for first, w in ((0, wq[n]), (2, wk[n])):
                for g in range(G):
                    for k in range(NK):
                        last = pe.matmul(bank(first + g // 2)[:, (g % 2) * L:(g % 2 + 1) * L],
                                         w[:, k, g * P:(g + 1) * P], yT[:, k, :], start=k == 0, stop=k == NK - 1)
                last.then_inc(ready, 1)
            for i in range(NT):
                for k in range(NK):
                    last = pe.matmul(bank(5)[:, i * D:(i + 1) * D], yT[:, k, i * P:(i + 1) * P], wv[n][:, k, :],
                                     start=k == 0, stop=k == NK - 1)
            last.then_inc(ready, 1)

        def attention_out(dve, b, xo_ps, chain, s, done):
            dve.wait_ge(xo_ps, b + 1)
            out = bank(2, 2).rearrange("p t (h s) -> p t h s", s=SLOT)
            dve.reciprocal(xden[:], out[:, :, :, ONE]).then_inc(chain, 1)
            dve.wait_ge(chain, s.next(b))
            dve.tensor_tensor(xo[:].rearrange("p t (h d) -> p t h d", d=HD), out[:, :, :, 0:HD],
                              xden[:].unsqueeze(3).to_broadcast([P, NT, H, HD]), ALU.mult).then_inc(chain, 1)
            dve.wait_ge(chain, s.next(b))
            dve.tensor_tensor(h[:, bass.ds(b * NT, NT), :], h[:, bass.ds(b * NT, NT), :], xo[:],
                              ALU.add).then_inc(done, 1)

        def heads_to_tokens(pe, ready):
            for i in range(NT):
                for g in range(G):
                    last = pe.transpose(bank(2 + i)[:, g * P:(g + 1) * P], xT[:, g, i * P:(i + 1) * P], ident[:])
            last.then_inc(ready, 1)

        def values(dve, n, done):
            for i in range(NT):
                dve.tensor_tensor(va[:, i, :, 0:HD], slotted(bank(5)[:, i * D:(i + 1) * D], HD),
                                  slotted(bv[n][:], HD), ALU.add).then_inc(done, 1)

        with ExitStack() as tmp:
            yTm = sb("yTm", [P, NK, M], F32, tmp)
            qlm = sb("qlm", [P, G, M], F32, tmp)
            klm = sb("klm", [P, G, M], F32, tmp)
            nmax = sb("nmax", [P, H], F32, tmp)
            nbias = sb("nbias", [P, H], F32, tmp)
            rsum = sb("rsum", [P, H], F32, tmp)
            rinv = sb("rinv", [P, H], F32, tmp)
            pe2 = sb("pe2", [P, H, M], F32, tmp)
            k2 = sb("k2", [P, H, M], F32, tmp)
            cmax = sb("cmax", [P, NB], F32, tmp)
            msum = sb("msum", [P, 1], F32, tmp)
            ones = sb("ones", [P, P], F32, tmp)
            names = ("ln_stat", "ln_rstd_done", "y_done", "dve_step", "pool_step", "yTm_ps", "yTm_done", "q_ps",
                     "k_ps", "q_done", "k_done", "s_ps", "max_done", "exp_done", "rinv_done", "k2_done",
                     "k2_stored", "col_ps", "col_done", "ones_done")
            (ln_stat, ln_rstd_done, y_done, dve_step, pool_step, yTm_ps, yTm_done, q_ps, k_ps, q_done, k_done,
             s_ps, max_done, exp_done, rinv_done, k2_done, k2_stored, col_ps, col_done, ones_done) = (
                sem("lm_" + n) for n in names)
            with nc.Block() as block:
                @block.vector
                def _(dve):
                    dve.memset(ones[:], 1.0).then_inc(ones_done, 1)
                    with dve.Fori(0, NB) as b:
                        s = Steps(3)
                        ln_statistics(dve, b, dve_step, s, ln_stat)
                        ln_scale(dve, b, b, ln_rstd_done, y_done)
                        for ps_ready, n, out, bias, done in ((q_ps, 5, qlm, bq[0], q_done), (k_ps, 6, klm, bk[0], k_done)):
                            dve.wait_ge(ps_ready, b + 1)
                            dve.tensor_tensor(out[:], bank(n).rearrange("p (g m) -> p g m", g=G),
                                              bias[:].unsqueeze(2).to_broadcast([P, G, M]), ALU.add).then_inc(done, 1)
                        dve.wait_ge(s_ps, b + 1)
                        dve.tensor_reduce(nmax[:], bank(0, 4).rearrange("p j (g m) -> p (j g) m", m=M), axis=AX.X,
                                          op=ALU.max, negate=True).then_inc(dve_step, 1)
                        dve.wait_ge(dve_step, s.next(b))
                        dve.tensor_scalar(nbias[:], nmax[:], 0.25, None, ALU.mult).then_inc(max_done, 1)
                        dve.wait_ge(exp_done, b * H + H + 1)
                        dve.reciprocal(rinv[:], rsum[:]).then_inc(rinv_done, 1)
                        dve.wait_ge(col_ps, b + 1)
                        dve.tensor_reduce(cmax[:, bass.ds(b, 1)], bank(4, 4).rearrange("p j n -> p (j n)"), axis=AX.X,
                                          op=ALU.max).then_inc(col_done, 1)
                        s.end()
                    dve.wait_ge(col_done, NB + 1)
                    dve.tensor_reduce(msum[:], cmax[:], axis=AX.X, op=ALU.max).then_inc(dve_step, 1)
                    dve.wait_ge(dve_step, 3 * NB + 1)
                    dve.reciprocal(minv[:, 1:2], msum[:]).then_inc(dve_step, 1)
                    dve.wait_ge(dve_step, 3 * NB + 2)
                    dve.tensor_scalar(minv[:, 0:1], minv[:, 1:2], -1.0, None, ALU.mult)

                @block.gpsimd
                def _(pool):
                    with pool.Fori(0, NB) as b:
                        ln_rstd(pool, b, ln_stat, pool_step, ln_rstd_done)
                        pool.wait_ge(rinv_done, b + 1)
                        pool.wait_ge(k2_stored, b * 16 + 16)
                        pool.tensor_tensor(k2[:], pe2[:], rinv[:].unsqueeze(2).to_broadcast([P, H, M]),
                                           ALU.mult).then_inc(k2_done, 1)

                @block.scalar
                def _(act):
                    with act.Fori(0, NB) as b:
                        act.wait_ge(yTm_ps, b + 1)
                        act.activation(yTm[:].rearrange("p k m -> p (k m)"), bank(4)[:, 0:NK * M], ACT.Copy).then_inc(yTm_done, 1)
                        act.wait_ge(max_done, b + 1)
                        for i in range(H):
                            act.activation(pe2[:, i, :], bank(i // G)[:, (i % G) * M:(i % G + 1) * M], ACT.Exp,
                                           bias=nbias[:, i:i + 1], scale=0.25,
                                           accum_out=rsum[:, i:i + 1]).then_inc(exp_done, 1)

                @block.sync
                def _(sp):
                    sp.sem_inc(k2_stored, 16)
                    with sp.Fori(0, NB) as b:
                        sp.wait_ge(k2_done, b + 1)
                        sp.dma_start(k2_dram[b], k2[:].rearrange("p h m -> p (h m)")).then_inc(k2_stored, 16)
                    sp.wait_ge(k2_stored, 16 * NB + 16)

                @block.tensor
                def _(pe):
                    pe.wait_ge(ones_done, 1)
                    pe.sem_inc(col_done, 1)
                    pe.sem_inc(exp_done, 1)
                    with pe.Fori(0, NB) as b:
                        pe.wait_ge(y_done, b * NT + NT)
                        pe.wait_ge(col_done, b + 1)
                        for k in range(NK):
                            for i in range(NT):
                                last = pe.matmul(bank(4)[:, k * M + i * P // 2:k * M + (i + 1) * P // 2],
                                                 y[:, i, k * P:(k + 1) * P], pairing[:], start=True, stop=True)
                        last.then_inc(yTm_ps, 1)
                        pe.wait_ge(yTm_done, b + 1)
                        for n, w, done in ((5, wq[0], q_ps), (6, wk[0], k_ps)):
                            for g in range(G):
                                for k in range(NK):
                                    last = pe.matmul(bank(n)[:, g * M:(g + 1) * M], w[:, k, g * P:(g + 1) * P],
                                                     yTm[:, k, :], start=k == 0, stop=k == NK - 1)
                            last.then_inc(done, 1)
                        pe.wait_ge(q_done, b + 1)
                        pe.wait_ge(k_done, b + 1)
                        pe.wait_ge(exp_done, b * H + 1)
                        for g in range(G):
                            for j in range(J):
                                rows = slice(SLOT * j, SLOT * (j + 1))
                                last = pe.matmul(bank(j)[:, g * M:(g + 1) * M], qlm[rows, g, :], klm[rows, g, :],
                                                 start=True, stop=True)
                        last.then_inc(s_ps, 1)
                        pe.wait_ge(k2_done, b + 1)
                        for j in range(J):
                            last = pe.matmul(bank(4 + j), ones[:], k2[:, j * G:(j + 1) * G, :].rearrange("p g m -> p (g m)"),
                                             start=True, stop=True)
                        last.then_inc(col_ps, 1)

        with ExitStack() as tmp:
            qs = sb("qs", [P, G, M], F32, tmp)
            ks = sb("ks", [P, G, M], F32, tmp)
            mcol = sb("mcol", [P, 2, 3, P], F32, tmp)
            p3 = sb("p3", [P, 2, J, L], F32, tmp)
            p1 = sb("p1", [P, H, L], F32, tmp)
            yn = sb("yn", [P, H, HD], F32, tmp)
            den = sb("den", [P, H], F32, tmp)
            k2 = sb("k2n", [P, H, M], F32, tmp)
            k2T = sb("k2T", [P, H, M], F32, tmp)
            ey = sb("ey", [P, NU, U, EW], F32, tmp)
            gu = sb("gu", [P, NU, U, EW], F32, tmp)
            e2 = sb("e2", [P, NU, U, EW], F32, tmp)
            ya = sb("ya", [P, NU, U, HD], F32, tmp)
            zc = sb("zc", [P, H, SLOT], F32, tmp)
            names = ("thin_copied", "ln_stat", "ln_rstd_done", "y_done", "dve_step", "pool_step", "yT_ps", "yT_done", "qkv_ps",
                     "q_done", "k_done", "v_done", "qs_done", "ks_done", "s_ps", "mcol_done", "mrow_ps", "aug_done",
                     "st_ps", "exp_done", "yn_ps", "yn_done", "k2_loaded", "k2T_ps", "k2T_done", "kk_ps",
                     "e0_done", "sq_ps", "sq_act", "sq_dve", "cu_ps", "cu_act", "cu_dve", "thin_ps", "thin_done",
                     "z_ps", "z_done", "x_ps", "xT_done", "xo_ps", "h_done", "clear")
            (thin_copied, ln_stat, ln_rstd_done, y_done, dve_step, pool_step, yT_ps, yT_done, qkv_ps, q_done, k_done, v_done,
             qs_done, ks_done, s_ps, mcol_done, mrow_ps, aug_done, st_ps, exp_done, yn_ps, yn_done, k2_loaded,
             k2T_ps, k2T_done, kk_ps, e0_done, sq_ps, sq_act, sq_dve, cu_ps, cu_act, cu_dve, thin_ps, thin_done,
             z_ps, z_done, x_ps, xT_done, xo_ps, h_done, clear) = (sem("ny_" + n) for n in names)
            LAST = ITERS - 1

            def norm_y(dve, b, g, s):
                dve.wait_ge(yn_ps, b * G + g + 1)
                out = slotted(bank(4 * (g % 2) + 1)[:, 0:J * SLOT], SLOT)
                dve.reciprocal(den[:, g * J:(g + 1) * J], out[:, :, ONE]).then_inc(dve_step, 1)
                dve.wait_ge(dve_step, s.next(b))
                dve.tensor_tensor(yn[:, g * J:(g + 1) * J, :], out[:, :, 0:HD],
                                  den[:, g * J:(g + 1) * J].unsqueeze(2).to_broadcast([P, J, HD]),
                                  ALU.mult).then_inc(yn_done, 1)

            def prod(a):
                return bank(4 + a).rearrange("p (i n) -> p i n", i=U)

            def turn(b, half_, k=0):
                return (b * 2 + half_) * (LAST * NU) + k * NU

            with nc.Block() as block:
                @block.sync
                def _(sp):
                    sp.sem_inc(z_ps, 1)
                    with sp.Fori(0, NB) as b:
                        sp.wait_ge(z_ps, b + 1)
                        sp.dma_start(k2[:].rearrange("p h m -> p (h m)"), k2_dram[b]).then_inc(k2_loaded, 16)
                    sp.wait_ge(k2_loaded, 16 * NB)

                @block.gpsimd
                def _(pool):
                    pool.memset(mcol[:], 0.0).then_inc(clear, 1)
                    pool.memset(va[:], 0.0).then_inc(clear, 1)
                    pool.memset(zc[:], 0.0).then_inc(clear, 1)
                    pool.wait_ge(clear, 3)
                    pool.memset(va[:, :, :, ONE:ONE + 1], 1.0).then_inc(clear, 1)
                    pool.memset(zc[:, :, ONE:ONE + 1], 1.0).then_inc(clear, 1)
                    with pool.Fori(0, NB) as b:
                        ln_rstd(pool, b, ln_stat, pool_step, ln_rstd_done)
                        pool.wait_ge(k_done, b * G + G)
                        pair = kT[:].rearrange("p g (m two) -> p g m two", two=2)
                        pool.tensor_tensor(ks[:], pair[:, :, :, 0], pair[:, :, :, 1], ALU.add).then_inc(ks_done, 1)

                @block.scalar
                def _(act):
                    with act.Fori(0, NB) as b:
                        act.wait_ge(yT_ps, b + 1)
                        act.activation(yT[:].rearrange("p k m -> p (k m)"), bank(4), ACT.Copy).then_inc(yT_done, 1)
                        act.wait_ge(qkv_ps, b * 3 + 2)
                        for g in range(G):
                            act.activation(kT[:, g, :], bank(2 + g // 2)[:, (g % 2) * L:(g % 2 + 1) * L], ACT.Identity,
                                           bias=bk[0][:, g:g + 1]).then_inc(k_done, 1)
                        for g in range(G):
                            act.wait_ge(st_ps, b * G + g + 1)
                            act.activation(p3[:, g % 2], bank(4 * (g % 2), 4)[:, :, 0:L], ACT.Exp, scale=0.125).then_inc(exp_done, 1)
                            act.activation(p1[:, g * J:(g + 1) * J, :], bank(4 * (g % 2), 4)[:, :, L:2 * L], ACT.Exp,
                                           scale=0.125).then_inc(exp_done, 1)
                        for n in range(2):
                            act.wait_ge(k2T_ps, b * 2 + n + 1)
                            act.activation(k2T[:, 8 * n:8 * n + 8, :], bank(2 * n, 2).rearrange("p a (i m) -> p (a i) m", m=M),
                                           ACT.Copy).then_inc(k2T_done, 1)
                        for half_ in range(2):
                            for k in range(LAST):
                                for a in range(NU):
                                    act.wait_ge(sq_ps, turn(b, half_, k) + a + 1)
                                    act.activation(e2[:, a], prod(a)[:, :, 0:EW], ACT.Copy).then_inc(sq_act, 1)
                                for a in range(NU):
                                    act.wait_ge(cu_ps, turn(b, half_, k) + a + 1)
                                    act.activation(ey[:, a], prod(a)[:, :, 0:EW], ACT.Copy, scale=0.25).then_inc(cu_act, 1)
                        act.wait_ge(x_ps, b + 1)
                        act.activation(xT[:], bank(0, 2).rearrange("p a (i n) -> p (a i) n", i=2), ACT.Copy).then_inc(xT_done, 1)

                @block.vector
                def _(dve):
                    dve.wait_ge(clear, 5)
                    with dve.Fori(0, NB) as b:
                        s = Steps(NT + G + 2)
                        ln_statistics(dve, b, dve_step, s, ln_stat)
                        ln_scale(dve, b, b, ln_rstd_done, y_done)
                        dve.wait_ge(qkv_ps, b * 3 + 1)
                        dve.tensor_tensor(qT[:], bank(0, 2).rearrange("p a (i n) -> p (a i) n", i=2),
                                          bq[0][:].unsqueeze(2).to_broadcast([P, G, L]), ALU.add).then_inc(q_done, 1)
                        dve.wait_ge(qkv_ps, b * 3 + 3)
                        values(dve, 0, v_done)
                        dve.wait_ge(q_done, b + 1)
                        pair = qT[:].rearrange("p g (m two) -> p g m two", two=2)
                        dve.tensor_tensor(qs[:], pair[:, :, :, 0], pair[:, :, :, 1], ALU.add).then_inc(qs_done, 1)
                        for g in range(G):
                            a = g % 2
                            dve.wait_ge(s_ps, b * G + g + 1)
                            cols = mcol[:, a].rearrange("p c (j s) -> p j c s", s=SLOT)[:, :, :, ONE]
                            dve.tensor_reduce(cols[:, :, 0], bank(4 * a, 4)[:, :, 0:L], axis=AX.X, op=ALU.max,
                                              negate=True)
                            dve.tensor_reduce(cols[:, :, 1:3], bank(4 * a, 4)[:, :, L:2 * L].rearrange("p j (c n) -> p j c n", c=2),
                                              axis=AX.X, op=ALU.max, negate=True).then_inc(mcol_done, 1)
                            dve.wait_ge(mrow_ps, b * G + g + 1)
                            dve.tensor_tensor(qs[:, g, :], bank(4 * a)[:, 0:M], qs[:, g, :], ALU.add).then_inc(aug_done, 1)
                            dve.scalar_tensor_tensor(qT[:, g, :], bank(4 * a)[:, M:M + L], 0.5, qT[:, g, :],
                                                     ALU.mult, ALU.add).then_inc(aug_done, 1)
                            if g >= 1:
                                norm_y(dve, b, g - 1, s)
                        norm_y(dve, b, G - 1, s)
                        for half_ in range(2):
                            for a in range(NU):
                                heads = slice((half_ * NU + a) * U, (half_ * NU + a + 1) * U)
                                dve.wait_ge(kk_ps, (b * 2 + half_) * NU + a + 1)
                                dve.scalar_tensor_tensor(ey[:, a, :, 0:P], prod(a)[:, :, 0:P], minv[:, 0:1],
                                                         ident[:].unsqueeze(1).to_broadcast([P, U, P]), ALU.mult, ALU.add)
                                dve.tensor_copy(ey[:, a, :, P:EW], yn[:, heads, :]).then_inc(e0_done, 1)
                            for k in range(LAST):
                                for a in range(NU):
                                    dve.wait_ge(sq_act, turn(b, half_, k) + a + 1)
                                    dve.tensor_tensor(ya[:, a], ey[:, a, :, P:EW], e2[:, a, :, P:EW], ALU.add)
                                    dve.scalar_tensor_tensor(gu[:, a, :, P:EW], e2[:, a, :, P:EW], 0.25, ey[:, a, :, P:EW],
                                                             ALU.mult, ALU.add)
                                    dve.scalar_tensor_tensor(gu[:, a, :, 0:P], ey[:, a, :, 0:P], 3.0, e2[:, a, :, 0:P],
                                                             ALU.mult, ALU.add).then_inc(sq_dve, 1)
                                for a in range(NU):
                                    dve.wait_ge(cu_act, turn(b, half_, k) + a + 1)
                                    dve.wait_ge(sq_dve, turn(b, half_, k) + a + 1)
                                    dve.scalar_tensor_tensor(ey[:, a, :, P:EW], ey[:, a, :, P:EW], 4.0, ya[:, a],
                                                             ALU.mult, ALU.add).then_inc(cu_dve, 1)
                            for r, c in ((0, 1.0), (1, 1.0), (2, 0.25)):
                                for a in range(NU):
                                    acc = yn[:, (half_ * NU + a) * U:(half_ * NU + a + 1) * U, :]
                                    dve.wait_ge(thin_ps, ((b * 2 + half_) * 3 + r) * NU + a + 1)
                                    if r < 2:
                                        dve.tensor_copy(gu[:, a, :, r * HD:(r + 1) * HD],
                                                        prod(a)[:, :, r * HD:(r + 1) * HD]).then_inc(thin_copied, 1)
                                    dve.scalar_tensor_tensor(acc, prod(a)[:, :, r * HD:(r + 1) * HD], c,
                                                             ey[:, a, :, P:EW] if r == 0 else acc,
                                                             ALU.mult, ALU.add).then_inc(thin_done, 1)
                        dve.wait_ge(z_ps, b + 2)
                        dve.tensor_scalar(zc[:, :, 0:HD], slotted(bank(4)[:, 0:H * HD], HD), minv[:, 1:2], None,
                                          ALU.mult).then_inc(z_done, 1)
                        attention_out(dve, b, xo_ps, dve_step, s, h_done)
                        s.end()

                @block.tensor
                def _(pe):
                    pe.wait_ge(clear, 5)
                    with pe.Fori(0, NB) as b:
                        pe.wait_ge(y_done, b * NT + NT)
                        transpose_y(pe, yT_ps)
                        pe.wait_ge(yT_done, b + 1)
                        project(pe, 0, qkv_ps)
                        pe.wait_ge(q_done, b + 1)
                        pe.wait_ge(k_done, b * G + G)
                        pe.wait_ge(v_done, b * NT + NT)
                        pe.wait_ge(qs_done, b + 1)
                        pe.wait_ge(ks_done, b + 1)

                        def logits(g):
                            for j in range(J):
                                rows, out = slice(SLOT * j, SLOT * (j + 1)), bank(4 * (g % 2) + j)
                                pe.matmul(out[:, 0:L], qs[rows, g, :], kT[rows, g, :], start=True, stop=True)
                                for i in range(NT):
                                    last = pe.matmul(out[:, L + i * P:L + (i + 1) * P], qT[rows, g, i * P:(i + 1) * P],
                                                     ks[rows, g, :], start=True, stop=True)
                            last.then_inc(s_ps, 1)

                        def maxima_to_rows(g):
                            pe.wait_ge(mcol_done, b * G + g + 1)
                            for c in range(3):
                                last = pe.transpose(bank(4 * (g % 2))[:, c * P:(c + 1) * P], mcol[:, g % 2, c, :], ident[:])
                            last.then_inc(mrow_ps, 1)

                        def transposed_logits(g):
                            pe.wait_ge(aug_done, (b * G + g + 1) * 2)
                            for j in range(J):
                                rows, out = slice(SLOT * j, SLOT * (j + 1)), bank(4 * (g % 2) + j)
                                for i in range(NT):
                                    pe.matmul(out[:, i * P:(i + 1) * P], kT[rows, g, i * P:(i + 1) * P], qs[rows, g, :],
                                              start=True, stop=True)
                                last = pe.matmul(out[:, L:2 * L], ks[rows, g, :], qT[rows, g, :], start=True, stop=True)
                            last.then_inc(st_ps, 1)

                        def kernel3_values(g):
                            pe.wait_ge(exp_done, (b * G + g + 1) * 2)
                            for j in range(J):
                                for i in range(NT):
                                    last = pe.matmul(bank(4 * (g % 2) + 1)[:, j * SLOT:j * SLOT + ONE + 1],
                                                     p3[:, g % 2, j, i * P:(i + 1) * P], va[:, i, g * J + j, 0:ONE + 1],
                                                     start=i == 0, stop=i == NT - 1)
                            last.then_inc(yn_ps, 1)

                        logits(0)
                        logits(1)
                        maxima_to_rows(0)
                        transposed_logits(0)
                        maxima_to_rows(1)
                        transposed_logits(1)
                        kernel3_values(0)
                        pe.wait_ge(yn_done, b * G + 1)
                        logits(2)
                        kernel3_values(1)
                        maxima_to_rows(2)
                        transposed_logits(2)
                        pe.wait_ge(yn_done, b * G + 2)
                        logits(3)
                        kernel3_values(2)
                        maxima_to_rows(3)
                        transposed_logits(3)
                        kernel3_values(3)
                        pe.wait_ge(k2_loaded, b * 16 + 16)
                        pe.wait_ge(yn_done, b * G + 3)
                        for g in range(G):
                            for j in range(J):
                                last = pe.transpose(bank(g)[:, j * M:(j + 1) * M], k2[:, j * G + g, :], ident[:])
                            if g % 2:
                                last.then_inc(k2T_ps, 1)
                        pe.wait_ge(yn_done, b * G + G)
                        for half_ in range(2):
                            pe.wait_ge(k2T_done, b * 2 + half_ + 1)
                            for a in range(NU):
                                if half_ == 1:
                                    pe.wait_ge(thin_done, (b * 2) * (3 * NU) + 2 * NU + a + 1)
                                for i in range(U):
                                    kT_h = k2T[:, (half_ * NU + a) * U + i, :]
                                    last = pe.matmul(prod(a)[:, i, 0:P], kT_h, kT_h, start=True, stop=True)
                                last.then_inc(kk_ps, 1)
                            for k in range(LAST):
                                for a in range(NU):
                                    if k == 0:
                                        pe.wait_ge(e0_done, (b * 2 + half_) * NU + a + 1)
                                    else:
                                        pe.wait_ge(cu_dve, turn(b, half_, k - 1) + a + 1)
                                    for i in range(U):
                                        last = pe.matmul(prod(a)[:, i, 0:EW], ey[:, a, i, 0:P], ey[:, a, i, :],
                                                         start=True, stop=True)
                                    last.then_inc(sq_ps, 1)
                                for a in range(NU):
                                    pe.wait_ge(sq_dve, turn(b, half_, k) + a + 1)
                                    for i in range(U):
                                        last = pe.matmul(prod(a)[:, i, 0:EW], e2[:, a, i, 0:P], gu[:, a, i, :],
                                                         start=True, stop=True)
                                    last.then_inc(cu_ps, 1)
                            for r in range(3):
                                for a in range(NU):
                                    if r == 0:
                                        pe.wait_ge(cu_dve, turn(b, half_, LAST - 1) + a + 1)
                                    else:
                                        pe.wait_ge(thin_done, ((b * 2 + half_) * 3 + r - 1) * NU + a + 1)
                                    for i in range(U):
                                        rhs = ey[:, a, i, P:EW] if r == 0 else gu[:, a, i, (r - 1) * HD:r * HD]
                                        last = pe.matmul(prod(a)[:, i, r * HD:(r + 1) * HD], ey[:, a, i, 0:P], rhs,
                                                         start=True, stop=True)
                                    last.then_inc(thin_ps, 1)
                        pe.wait_ge(thin_done, (b + 1) * (6 * NU))
                        for g in range(G):
                            for j in range(J):
                                last = pe.matmul(bank(4)[:, (g * J + j) * HD:(g * J + j + 1) * HD], k2[:, j * G + g, :],
                                                 yn[:, g * J + j, :], start=True, stop=True)
                        last.then_inc(z_ps, 1)
                        pe.wait_ge(z_done, b + 1)
                        for g in range(G):
                            for j in range(J):
                                last = pe.matmul(bank(g // 2)[SLOT * j:SLOT * (j + 1), (g % 2) * L:(g % 2 + 1) * L],
                                                 zc[:, g * J + j, :], p1[:, g * J + j, :], start=True, stop=True)
                        last.then_inc(x_ps, 1)
                        pe.wait_ge(xT_done, b + 1)
                        heads_to_tokens(pe, xo_ps)

        with ExitStack() as tmp:
            W3 = 3 * P
            mcol = sb("mcol1", [P, 2, NT, P], F32, tmp)
            pT = sb("pT", [P, 2, J, W3], F32, tmp)
            res = sb("res", [P, NT, D], F32, tmp)
            names = ("ln_stat", "ln_rstd_done", "y_done", "dve_step", "pool_step", "yT_ps", "yT_done", "ffn_ps",
                     "ffn_done", "qkv_ps", "q_done", "k_done", "v_done", "s_ps", "mcol_done", "mrow_ps",
                     "aug_done", "st_ps", "exp_done", "pv_ps", "xT_done", "xo_ps", "h_done", "clear", "four_ps",
                     "res_done", "stored")
            (ln_stat, ln_rstd_done, y_done, dve_step, pool_step, yT_ps, yT_done, ffn_ps, ffn_done, qkv_ps, q_done,
             k_done, v_done, s_ps, mcol_done, mrow_ps, aug_done, st_ps, exp_done, pv_ps, xT_done, xo_ps, h_done,
             clear, four_ps, res_done, stored) = (sem("tl_" + n) for n in names)
            NLN = 3
            with nc.Block() as block:
                @block.sync
                def _(sp):
                    sp.sem_inc(stored, 16)
                    with sp.Fori(0, NB) as b:
                        sp.wait_ge(res_done, b + 1)
                        sp.dma_start(t["out"][b].rearrange("(t p) d -> p t d", p=P), res[:]).then_inc(stored, 16)
                    sp.wait_ge(stored, 16 * NB + 16)

                @block.gpsimd
                def _(pool):
                    pool.memset(mcol[:], 0.0).then_inc(clear, 1)
                    with pool.Fori(0, NB) as b:
                        for i in range(NLN):
                            ln_rstd(pool, b * NLN + i, ln_stat, pool_step, ln_rstd_done)

                @block.scalar
                def _(act):
                    with act.Fori(0, NB) as b:
                        def copy_yT(i):
                            act.wait_ge(yT_ps, b * NLN + i + 1)
                            act.activation(yT[:].rearrange("p k m -> p (k m)"), bank(4), ACT.Copy).then_inc(yT_done, 1)

                        def exponentials(g):
                            act.wait_ge(st_ps, b * G + g + 1)
                            act.activation(pT[:, g % 2], bank(4 * (g % 2), 4)[:, :, 0:W3], ACT.Exp,
                                           scale=0.25).then_inc(exp_done, 1)

                        def copy_out(g):
                            act.wait_ge(pv_ps, b * G + g + 1)
                            act.activation(xT[:, g, :], bank(4 * (g % 2) + 1)[:, 0:L], ACT.Copy).then_inc(xT_done, 1)

                        copy_yT(0)
                        copy_yT(1)
                        act.wait_ge(qkv_ps, b * 3 + 2)
                        for g in range(G):
                            act.activation(kT[:, g, :], bank(2 + g // 2)[:, (g % 2) * L:(g % 2 + 1) * L], ACT.Identity,
                                           bias=bk[1][:, g:g + 1]).then_inc(k_done, 1)
                        exponentials(0)
                        exponentials(1)
                        copy_out(0)
                        copy_out(1)
                        exponentials(2)
                        copy_out(2)
                        exponentials(3)
                        copy_out(3)
                        copy_yT(2)

                @block.vector
                def _(dve):
                    dve.wait_ge(clear, 1)
                    with dve.Fori(0, NB) as b:
                        s = Steps(3 * NT + 2 + 2)
                        rows = bass.ds(b * NT, NT)
                        ln_statistics(dve, b, dve_step, s, ln_stat)
                        ln_scale(dve, b, b * NLN, ln_rstd_done, y_done)
                        dve.wait_ge(ffn_ps, b + 1)
                        dve.tensor_tensor(h[:, rows, :], h[:, rows, :], bank(5).rearrange("p (t d) -> p t d", t=NT),
                                          ALU.add).then_inc(dve_step, 1)
                        dve.wait_ge(dve_step, s.next(b))
                        dve.tensor_copy(passed[:], half[:])
                        ln_statistics(dve, b, dve_step, s, ln_stat)
                        ln_scale(dve, b, b * NLN + 1, ln_rstd_done, y_done)
                        dve.wait_ge(qkv_ps, b * 3 + 1)
                        dve.tensor_tensor(qT[:], bank(0, 2).rearrange("p a (i n) -> p (a i) n", i=2),
                                          bq[1][:].unsqueeze(2).to_broadcast([P, G, L]), ALU.add).then_inc(q_done, 1)
                        dve.wait_ge(qkv_ps, b * 3 + 3)
                        values(dve, 1, v_done)
                        for g in range(G):
                            a = g % 2
                            dve.wait_ge(s_ps, b * G + g + 1)
                            cols = mcol[:, a].rearrange("p c (j s) -> p j c s", s=SLOT)[:, :, :, ONE]
                            dve.tensor_reduce(cols[:, :, 0], bank(4 * a, 4)[:, :, 0:P], axis=AX.X, op=ALU.max, negate=True)
                            dve.tensor_reduce(cols[:, :, 1], bank(4 * a, 4)[:, :, P:W3], axis=AX.X, op=ALU.max,
                                              negate=True).then_inc(mcol_done, 1)
                            dve.wait_ge(mrow_ps, b * G + g + 1)
                            dve.tensor_tensor(qT[:, g, :], bank(4 * a)[:, 0:L], qT[:, g, :], ALU.add).then_inc(aug_done, 1)
                        attention_out(dve, b, xo_ps, dve_step, s, h_done)
                        dve.wait_ge(h_done, b + 1)
                        dve.tensor_copy(passed[:], half[:])
                        ln_statistics(dve, b, dve_step, s, ln_stat)
                        ln_scale(dve, b, b * NLN + 2, ln_rstd_done, y_done)
                        dve.wait_ge(stored, b * 16 + 16)
                        dve.tensor_tensor(res[:], h[:, rows, :], bf[:].unsqueeze(1).to_broadcast([P, NT, D]),
                                          ALU.add).then_inc(dve_step, 1)
                        dve.wait_ge(dve_step, s.next(b))
                        dve.wait_ge(four_ps, b + 1)
                        dve.tensor_tensor(res[:], res[:], bank(5).rearrange("p (t d) -> p t d", t=NT),
                                          ALU.add).then_inc(res_done, 1)
                        s.end()

                @block.tensor
                def _(pe):
                    pe.wait_ge(clear, 1)
                    with pe.Fori(0, NB) as b:
                        def features(i):
                            pe.wait_ge(y_done, (b * NLN + i + 1) * NT)
                            transpose_y(pe, yT_ps)
                            pe.wait_ge(yT_done, b * NLN + i + 1)

                        def ffn(w, ready):
                            for i in range(NT):
                                for k in range(NK):
                                    last = pe.matmul(bank(5)[:, i * D:(i + 1) * D], yT[:, k, i * P:(i + 1) * P], w[:, k, :],
                                                     start=k == 0, stop=k == NK - 1)
                            last.then_inc(ready, 1)

                        def logits(g, transposed):
                            left, right = (kT, qT) if transposed else (qT, kT)
                            for j in range(J):
                                pe.matmul(bank(4 * (g % 2) + j)[:, 0:2 * P], identb[:], mask[:, int(transposed), :],
                                          start=True, stop=False)
                            for c, (q, k) in enumerate(((0, 0), (1, 1), (1, 0))):
                                l, r = (k, q) if transposed else (q, k)
                                for j in range(J):
                                    rows = slice(SLOT * j, SLOT * (j + 1))
                                    last = pe.matmul(bank(4 * (g % 2) + j)[:, c * P:(c + 1) * P],
                                                     left[rows, g, l * P:(l + 1) * P], right[rows, g, r * P:(r + 1) * P],
                                                     start=False, stop=c == 2)
                            last.then_inc(st_ps if transposed else s_ps, 1)

                        def shifted(g):
                            pe.wait_ge(mcol_done, b * G + g + 1)
                            for c in range(NT):
                                last = pe.transpose(bank(4 * (g % 2))[:, c * P:(c + 1) * P], mcol[:, g % 2, c, :], ident[:])
                            last.then_inc(mrow_ps, 1)
                            pe.wait_ge(aug_done, b * G + g + 1)
                            logits(g, True)

                        def weighted_values(g):
                            pe.wait_ge(exp_done, b * G + g + 1)
                            for j in range(J):
                                out = bank(4 * (g % 2) + 1)[SLOT * j:SLOT * (j + 1), :]
                                pe.matmul(out[:, 0:P], va[:, 0, g * J + j, :], pT[:, g % 2, j, 0:P], start=True, stop=True)
                                pe.matmul(out[:, P:L], va[:, 0, g * J + j, :], pT[:, g % 2, j, 2 * P:W3], start=True, stop=False)
                                last = pe.matmul(out[:, P:L], va[:, 1, g * J + j, :], pT[:, g % 2, j, P:2 * P],
                                                 start=False, stop=True)
                            last.then_inc(pv_ps, 1)

                        features(0)
                        ffn(wt, ffn_ps)
                        features(1)
                        project(pe, 1, qkv_ps)
                        pe.wait_ge(q_done, b + 1)
                        pe.wait_ge(k_done, b * G + G)
                        pe.wait_ge(v_done, b * NT + NT)
                        logits(0, False)
                        logits(1, False)
                        shifted(0)
                        shifted(1)
                        weighted_values(0)
                        pe.wait_ge(xT_done, b * G + 1)
                        logits(2, False)
                        weighted_values(1)
                        shifted(2)
                        pe.wait_ge(xT_done, b * G + 2)
                        logits(3, False)
                        weighted_values(2)
                        shifted(3)
                        weighted_values(3)
                        pe.wait_ge(xT_done, b * G + 4)
                        heads_to_tokens(pe, xo_ps)
                        features(2)
                        ffn(wf, four_ps)




def host_arrays(inputs):
    f = np.float32
    a = {k: np.asarray(v) for k, v in inputs.items()}
    ids = a["x"]
    out = {"ids": ids.reshape(1, NB * L)}
    pos = np.pad(np.arange(L), NFFT // 2, mode="reflect").reshape(NFR, NFFT)
    out["ids_fr"] = np.ascontiguousarray(ids[:, pos].reshape(NB * NFR, NFFT).T)
    out["iota"] = np.arange(V, dtype=f).reshape(1, V)
    out["iota_c"] = np.arange(V, dtype=f).reshape(V, 1)
    ang = 2 * np.pi * np.outer(np.arange(NFFT), np.arange(NFQ)) / NFFT
    out["dft"] = np.stack([np.cos(ang), -np.sin(ang)], 1).astype(f)
    out["window"] = a["L0_tok_window"].reshape(NFFT, 1)
    w = a["L0_tok_proj_w"].reshape(DS, NFQ, V).transpose(2, 1, 0)
    out["wp"] = np.ascontiguousarray(np.concatenate([w, w], 0))
    out["emb"] = a["L0_tok_emb_table"]
    out["proj_b"] = a["L0_tok_proj_b"].reshape(1, DS)
    out["zero"] = np.zeros((1, DS), f)
    coord = np.clip((np.arange(L, dtype=f) + f(0.5)) * f(NFR / L) - f(0.5), 0.0, NFR - 1.0)
    i0 = np.floor(coord).astype(np.int32)
    i1 = np.minimum(i0 + 1, NFR - 1)
    wgt = (coord - i0).astype(f)
    up = np.zeros((NFR, L), f)
    np.add.at(up, (i0, np.arange(L)), 1 - wgt)
    np.add.at(up, (i1, np.arange(L)), wgt)
    full = np.zeros((NB, NFR, NB, L), f)
    for b in range(NB):
        full[b, :, b, :] = up
    full = full.reshape(PAIRS, 2, NB * L)
    interp = np.zeros((PAIRS + 1, 2, NB * L), f)
    interp[:PAIRS] = full
    interp[PAIRS, 0] = 1.0
    out["interp"] = interp
    out["ident"] = np.eye(P, dtype=f)
    out["pairing"] = np.repeat(np.eye(P // 2, dtype=f), 2, 0) * f(0.5)
    out["half"] = np.tile(np.array([-0.5, -0.5, EPS, EPS], f), (P, 1))
    up_m = np.triu(np.full((P, P), NEG, f), 1)
    out["mask"] = np.stack([np.concatenate([m, m], 1) for m in (up_m, up_m.T)], 1)

    def tiles(w):
        return np.ascontiguousarray(w.reshape(NK, P, w.shape[1]).transpose(1, 0, 2))

    def slots(w):
        s = np.zeros(w.shape[:-1] + (H, SLOT), f)
        s[..., :HD] = w.reshape(w.shape[:-1] + (H, HD))
        return s

    for n in range(2):
        for name in "qkv":
            w = a[f"L{n}_attn_W{name}"].reshape(D, D).T
            b = a[f"L{n}_attn_b{name}"].reshape(D)
            if name == "v":
                out[f"wv{n}"], out[f"bv{n}"] = tiles(w), b.reshape(1, D)
                continue
            out[f"w{name}{n}"] = tiles(slots(w).reshape(D, G * P))
            s = slots(b)
            if name == "k":
                s[..., ONE] = 1.0
            out[f"b{name}{n}"] = np.ascontiguousarray(s.reshape(G, P).T)
    out["fw"] = tiles(a["L0_ffn_weight"].T)
    ang = 2 * np.pi * ((np.outer(np.arange(D), np.arange(D))) % D) / D
    out["cs"] = np.ascontiguousarray(np.stack([tiles(m.astype(f)) for m in (np.cos(ang), np.sin(ang), -np.sin(ang))], 1))
    out["wri"] = np.ascontiguousarray(np.stack([tiles(a["L1_ffn_w_freq_real"]), tiles(a["L1_ffn_w_freq_imag"])], 1))
    out["bf"] = a["L1_ffn_bias"].reshape(1, D)
    return {k: np.ascontiguousarray(v) for k, v in out.items()}


def kernel(**inputs):
    import concourse.bacc as bacc
    from concourse.bass_utils import run_bass_kernel_spmd

    nc = bacc.Bacc("TRN2", target_bir_lowering=False, num_devices=1)
    arrays = host_arrays(inputs)
    t = {name: nc.dram_tensor(f"in_{name}", a.shape, mybir.dt.from_np(a.dtype), kind="ExternalInput").ap()
         for name, a in arrays.items()}
    t["out"] = nc.dram_tensor("out", (NB, L, D), F32, kind="ExternalOutput").ap()
    build(nc, t)
    r = run_bass_kernel_spmd(nc, [{f"in_{k}": v for k, v in arrays.items()}], core_ids=[0])
    return r.results[0]["out"]
```

```python
from contextlib import ExitStack

import numpy as np
import concourse.bass as bass
from concourse import mybir

F32 = mybir.dt.float32
BF16 = mybir.dt.bfloat16
I32 = mybir.dt.int32
ALU = mybir.AluOpType
ACT = mybir.ActivationFunctionType
AX = mybir.AxisListType

P = 128
NB, L, D = 16, 256, 256
NT = L // P
NK = D // P
H, HD = 16, 16
HALF = H // 2
J = 4
G = H // J
VW = HD + 1
SLOT = 32
ONE = HD
Q_PARTS = (0, 1, 2, 0, 1, 0)
K_PARTS = (0, 0, 0, 1, 1, 2)
STACK = len(Q_PARTS) * HD
SHIFT = 2
FULL = STACK + SHIFT
M = 128
V, NFFT = 64, 64
NFR = L // NFFT + 1
NFQ = NFFT // 2 + 1
PAIRS = NB * NFR // 2
DE = 179
DS = D - DE
EPS = 1e-5
ITERS = 6
U, NU = 2, 4
EW = P + HD
NEG = -1e30


def build(nc, t):
    ctx = ExitStack()
    with ctx:
        def sb(name, shape, dt=F32, where=None):
            return (where or ctx).enter_context(nc.sbuf_tensor(name, shape, dt))

        def sem(name):
            return ctx.enter_context(nc.semaphore(name))

        def scratch(name, shape, dt=F32):
            return nc.dram_tensor(name, shape, dt, kind="Internal").ap()

        k2_dram = scratch("k2_scratch", [NB, P, H * M])
        tok_parts = [scratch(f"tok_parts{n}", [NB, 2, 3, H * HD, L], BF16) for n in range(2)]
        lm_parts = scratch("lm_parts", [NB, 2, 3, H * HD, M], BF16)
        shift0 = scratch("shift0", [NB, SHIFT, 3, H, P], BF16)
        shift1 = scratch("shift1", [NB, SHIFT, NT, H, P], BF16)

        h = sb("h", [P, NB * NT, D])
        ident = sb("ident", [P, P])
        half = sb("half", [P, 4])
        passed = sb("passed", [P, 4])
        wq = [sb(f"wq{n}", [P, NK, D]) for n in range(2)]
        wk = [sb(f"wk{n}", [P, NK, D]) for n in range(2)]
        wv = [sb(f"wv{n}", [P, NK, D]) for n in range(2)]
        bq = [sb(f"bq{n}", [P, 2]) for n in range(2)]
        bk = [sb(f"bk{n}", [P, 2]) for n in range(2)]
        bv = [sb(f"bv{n}", [P, D]) for n in range(2)]
        wt = sb("wt", [P, NK, D])
        wf = sb("wf", [P, NK, D])
        bf = sb("bf", [P, D])
        mask = sb("mask", [P, 2, 2 * P], BF16)
        identb = sb("identb", [P, P], BF16)
        minv = sb("minv", [P, 2])
        stats = sb("stats", [P, NT, 6])
        mv = sb("mv", [P, NT, 2])
        rstd = sb("rstd", [P, NT])
        y = sb("y", [P, NT, D])
        yT = sb("yT", [P, NK, L])

        ps = ctx.enter_context(nc.psum_tensor("ps", [P, 8, 512], F32))

        def bank(n, k=1):
            return ps[:, n, :] if k == 1 else ps[:, n:n + k, :]

        class Steps:

            def __init__(self, per):
                self.per, self.n = per, 0

            def next(self, b=0):
                self.n += 1
                return b * self.per + self.n

            def end(self):
                assert self.n == self.per, self.n

        with ExitStack() as tmp:
            ids_all = sb("ids_all", [V, NB * L], I32, tmp)
            ids_fr = sb("ids_fr", [NFFT, 2 * PAIRS], I32, tmp)
            iota_c = sb("iota_c", [V, 1], F32, tmp)
            iota_r = sb("iota_r", [NFFT, V], F32, tmp)
            hotT = sb("hotT", [V, NB * L], F32, tmp)
            hot_fr = sb("hot_fr", [NFFT, PAIRS * 2, V], F32, tmp)
            dft = sb("dft", [NFFT, 2, NFQ], F32, tmp)
            dftw = sb("dftw", [NFFT, 2 * NFQ], F32, tmp)
            window = sb("window", [NFFT, 1], F32, tmp)
            sq = sb("sq", [P, PAIRS, 2 * NFQ], F32, tmp)
            mag = sb("mag", [P, PAIRS, NFQ], F32, tmp)
            live = sb("live", [P, PAIRS, NFQ], F32, tmp)
            wp = sb("wp", [P, NFQ, DS], F32, tmp)
            emb = sb("emb", [V, DE], F32, tmp)
            interp = sb("interp", [PAIRS + 1, 2, NB * L], F32, tmp)
            proj = sb("proj", [PAIRS + 1, 2, DS], F32, tmp)
            mask32 = sb("mask32", [P, 2, 2 * P], F32, tmp)
            fw = sb("fw", [P, NK, D], F32, tmp)
            habs = sb("habs", [P, 1], F32, tmp)
            hsum = sb("hsum", [P, 1], F32, tmp)
            hs = sb("hs", [P, 3], F32, tmp)
            neg = sb("neg", [P, NK, D], F32, tmp)
            cs = sb("cs", [P, 3, NK, D], F32, tmp)
            wri = sb("wri", [P, 2, NK, D], F32, tmp)
            prT = sb("prT", [P, 2, NK, D], F32, tmp)

            in_ids, in_tok, in_fft, in_ffn, in_rest = (sem(s) for s in (
                "in_ids", "in_tok", "in_fft", "in_ffn", "in_rest"))
            hot_fr_ready, hotT_ready, dft_ready = sem("hot_fr_ready"), sem("hotT_ready"), sem("dft_ready")
            spec_ready, sq_ready, m2_ready, mag_ready = (sem(s) for s in (
                "spec_ready", "sq_ready", "m2_ready", "mag_ready"))
            root_ready, proj_ps, proj_ready, tok_ps, tok_done = (sem(s) for s in (
                "root_ready", "proj_ps", "proj_ready", "tok_ps", "tok_done"))
            habs_ready, hsum_ready, ffn_step = sem("habs_ready"), sem("hsum_ready"), sem("ffn_step")
            pr_ps, pr_ready, wf_ps, wf_done = sem("pr_ps"), sem("pr_ready"), sem("wf_ps"), sem("wf_done")
            FPB = PAIRS // 8
            NTILE = NB * NT

            with nc.Block() as block:
                @block.sync
                def _(sp):
                    for dst, src in ((ids_fr[:], t["ids_fr"]), (iota_r[:], t["iota"].partition_broadcast(NFFT)),
                                     (iota_c[:], t["iota_c"]), (dft[:], t["dft"]), (window[:], t["window"])):
                        sp.dma_start(dst, src).then_inc(in_ids, 16)
                    for dst, src in ((wp[:], t["wp"]), (emb[:], t["emb"]), (interp[:], t["interp"]),
                                     (proj[PAIRS:PAIRS + 1, 0, :], t["proj_b"]), (proj[PAIRS:PAIRS + 1, 1, :], t["zero"])):
                        sp.dma_start(dst, src).then_inc(in_tok, 16)
                    for dst, src in ((ident[:], t["ident"]), (half[:], t["half"]),
                                     (mask32[:], t["mask"])):
                        sp.dma_start(dst, src).then_inc(in_rest, 16)
                    sp.wait_ge(in_rest, 16 * (3 + 6 * 2 + 1))

                @block.gpsimd
                def _(pool):
                    pool.wait_ge(habs_ready, 1)
                    pool.partition_all_reduce(hsum[:], habs[:], P, bass.bass_isa.ReduceOp.add).then_inc(hsum_ready, 1)

                @block.scalar
                def _(act):
                    act.dma_start(ids_all[:], t["ids"].partition_broadcast(V)).then_inc(in_ids, 16)
                    act.dma_start(fw[:], t["fw"]).then_inc(in_ffn, 16)
                    act.dma_start(cs[:], t["cs"]).then_inc(in_fft, 16)
                    act.dma_start(wri[:], t["wri"]).then_inc(in_fft, 16)
                    for n in range(2):
                        for dst, name in ((wq, "wq"), (wk, "wk"), (wv, "wv"), (bq, "bq"), (bk, "bk")):
                            act.dma_start(dst[n][:], t[f"{name}{n}"]).then_inc(in_rest, 16)
                        act.dma_start(bv[n][:], t[f"bv{n}"].partition_broadcast(P)).then_inc(in_rest, 16)
                    act.dma_start(bf[:], t["bf"].partition_broadcast(P)).then_inc(in_rest, 16)
                    for n in range(8):
                        act.wait_ge(spec_ready, n + 1)
                        act.activation(sq[:, n * FPB:(n + 1) * FPB, :],
                                       bank(n)[:, 0:FPB * 2 * NFQ].rearrange("p (a f) -> p a f", a=FPB),
                                       ACT.Square).then_inc(sq_ready, 1)
                    act.wait_ge(m2_ready, 1)
                    act.activation(mag[:], mag[:], ACT.Sqrt).then_inc(root_ready, 1)
                    act.wait_ge(pr_ps, 1)
                    act.activation(prT[:], bank(0, 4).rearrange("p (a k) n -> p a k n", a=2)[:, :, :, 0:D],
                                   ACT.Copy).then_inc(pr_ready, 1)
                    act.wait_ge(wf_ps, 1)
                    act.activation(wf[:], bank(4, 2)[:, :, 0:D], ACT.Copy, scale=1.0 / D).then_inc(wf_done, 1)

                @block.vector
                def _(dve):
                    s = Steps(7)
                    dve.wait_ge(in_ids, 16 * 6)
                    dve.tensor_scalar(dftw[:], dft[:].rearrange("n a f -> n (a f)"), window[:, 0:1], None,
                                      ALU.mult).then_inc(dft_ready, 1)
                    dve.tensor_tensor(hot_fr[:], ids_fr[:].unsqueeze(2).to_broadcast([NFFT, 2 * PAIRS, V]),
                                      iota_r[:].unsqueeze(1).to_broadcast([NFFT, 2 * PAIRS, V]),
                                      ALU.is_equal).then_inc(hot_fr_ready, 1)
                    dve.tensor_scalar(hotT[:], ids_all[:], iota_c[:, 0:1], None, ALU.is_equal).then_inc(hotT_ready, 1)
                    dve.wait_ge(in_ffn, 16)
                    dve.tensor_reduce(habs[:], fw[:].rearrange("p k n -> p (k n)"), axis=AX.X, op=ALU.add,
                                      apply_absolute_value=True).then_inc(habs_ready, 1)
                    dve.wait_ge(sq_ready, 8)
                    dve.tensor_tensor(mag[:], sq[:, :, 0:NFQ], sq[:, :, NFQ:2 * NFQ], ALU.add).then_inc(ffn_step, 1)
                    dve.wait_ge(ffn_step, s.next())
                    dve.tensor_scalar(live[:], mag[:], 0.0, None, ALU.is_gt).then_inc(ffn_step, 1)
                    dve.wait_ge(ffn_step, s.next())
                    dve.tensor_scalar(mag[:], mag[:], 1e-34, None, ALU.max).then_inc(m2_ready, 1)
                    dve.wait_ge(root_ready, 1)
                    dve.tensor_tensor(mag[:], mag[:], live[:], ALU.mult).then_inc(mag_ready, 1)
                    dve.wait_ge(proj_ps, 1)
                    dve.tensor_copy(proj[0:PAIRS, :, :], bank(0, 2)[0:PAIRS, :, 0:DS]).then_inc(proj_ready, 1)
                    dve.wait_ge(hsum_ready, 1)
                    dve.tensor_scalar(hs[:, 0:1], hsum[:], 1.0 / (D * D), EPS, ALU.mult, ALU.max).then_inc(ffn_step, 1)
                    dve.wait_ge(ffn_step, s.next())
                    dve.tensor_scalar(hs[:, 1:2], hs[:, 0:1], 0.5, None, ALU.mult).then_inc(ffn_step, 1)
                    dve.wait_ge(ffn_step, s.next())
                    dve.tensor_scalar(hs[:, 2:3], hs[:, 0:1], -0.5, None, ALU.mult).then_inc(ffn_step, 1)
                    dve.wait_ge(ffn_step, s.next())
                    dve.tensor_scalar(wt[:], fw[:], hs[:, 1:2], hs[:, 0:1], ALU.is_gt, ALU.mult).then_inc(ffn_step, 1)
                    dve.wait_ge(ffn_step, s.next())
                    dve.tensor_scalar(neg[:], fw[:], hs[:, 2:3], hs[:, 0:1], ALU.is_lt, ALU.mult).then_inc(ffn_step, 1)
                    dve.wait_ge(ffn_step, s.next())
                    dve.tensor_tensor(wt[:], wt[:], neg[:], ALU.subtract)
                    dve.wait_ge(in_rest, 16 * (3 + 6 * 2 + 1))
                    dve.tensor_copy(mask[:], mask32[:])
                    dve.tensor_copy(identb[:], ident[:])
                    for n in range(NTILE // 4):
                        dve.wait_ge(tok_ps, n + 1)
                        b0 = 2 * (n % 2)
                        dve.tensor_copy(h[:, 4 * n:4 * n + 4, :].rearrange("p (a c) d -> p a (c d)", a=2),
                                        bank(4 + b0, 2)).then_inc(tok_done, 1)
                    s.end()

                @block.tensor
                def _(pe):
                    pe.wait_ge(hot_fr_ready, 1)
                    pe.wait_ge(dft_ready, 1)
                    for n in range(8):
                        for i in range(FPB):
                            pair = n * FPB + i
                            last = pe.matmul(bank(n)[:, i * 2 * NFQ:(i + 1) * 2 * NFQ],
                                             hot_fr[:, 2 * pair:2 * pair + 2, :].rearrange("n a v -> n (a v)"),
                                             dftw[:], start=True, stop=True)
                        last.then_inc(spec_ready, 1)
                    pe.wait_ge(mag_ready, 1)
                    pe.wait_ge(in_tok, 16 * 5)
                    for a in range(2):
                        rows = slice(V * a, V * a + V)
                        for f in range(NFQ):
                            last = pe.matmul(bank(a)[0:PAIRS, 0:DS], mag[rows, :, f], wp[rows, f, :],
                                             start=f == 0, stop=f == NFQ - 1)
                    last.then_inc(proj_ps, 1)
                    pe.wait_ge(proj_ready, 1)
                    pe.wait_ge(hotT_ready, 1)
                    for n in range(NTILE // 4):
                        if n >= 2:
                            pe.wait_ge(tok_done, n - 1)
                        for i in range(4):
                            tok = slice((4 * n + i) * P, (4 * n + i + 1) * P)
                            out = bank(4 + 2 * (n % 2) + i // 2)[:, (i % 2) * D:(i % 2 + 1) * D]
                            pe.matmul(out[:, 0:DE], hotT[:, tok], emb[:], start=True, stop=True)
                            for a in range(2):
                                last = pe.matmul(out[:, DE:D], interp[:, a, tok], proj[:, a, :],
                                                 start=a == 0, stop=a == 1)
                        last.then_inc(tok_ps, 1)
                    pe.wait_ge(in_fft, 32)
                    for a in range(2):
                        for o in range(NK):
                            cols = slice(o * P, o * P + P)
                            for k in range(NK):
                                pe.matmul(bank(2 * a + o)[:, 0:D], wri[:, a, k, cols], cs[:, 0, k, :],
                                          start=k == 0, stop=False)
                                last = pe.matmul(bank(2 * a + o)[:, 0:D], wri[:, 1 - a, k, cols],
                                                 cs[:, 1 + a, k, :], start=False, stop=k == NK - 1)
                    last.then_inc(pr_ps, 1)
                    pe.wait_ge(pr_ready, 1)
                    pe.wait_ge(tok_done, NTILE // 4)
                    for o in range(NK):
                        cols = slice(o * P, o * P + P)
                        for k in range(NK):
                            pe.matmul(bank(4 + o)[:, 0:D], prT[:, 0, k, cols], cs[:, 0, k, :],
                                      start=k == 0, stop=False)
                            last = pe.matmul(bank(4 + o)[:, 0:D], prT[:, 1, k, cols], cs[:, 2, k, :],
                                             start=False, stop=k == NK - 1)
                    last.then_inc(wf_ps, 1)

        vall = sb("vall", [P, NB, NT * H * VW])
        qstk = sb("qstk", [P, H, L], BF16)
        kstk = sb("kstk", [P, H, L], BF16)
        xT = sb("xT", [P, G, L])
        xden = sb("xden", [P, NT, H])
        xo = sb("xo", [P, NT, D])

        def ln_statistics(dve, b, q, chain, ready):
            for i in range(NT):
                dve.bn_stats(stats[:, i, :], h[:, b * NT + i, :]).then_inc(chain, 1)
            dve.wait_ge(chain, q * NT + NT)
            dve.tensor_copy(passed[:], half[:])
            for i in range(NT):
                dve.bn_aggr(mv[:, i, :], stats[:, i, :]).then_inc(ready, 1)

        def ln_rstd(pool, q, statistics, chain, ready):
            pool.wait_ge(statistics, q * NT + NT)
            pool.tensor_tensor(rstd[:], mv[:, :, 1], half[:, 2:4], ALU.add).then_inc(chain, 1)
            pool.wait_ge(chain, q + 1)
            pool.tensor_tensor(rstd[:], rstd[:], half[:, 0:2], ALU.pow).then_inc(ready, 1)

        def ln_scale(dve, b, q, rstd_ready, ready):
            dve.wait_ge(rstd_ready, q + 1)
            for i in range(NT):
                dve.tensor_scalar(y[:, i, :], h[:, b * NT + i, :], mv[:, i, 0:1], rstd[:, i:i + 1],
                                  ALU.subtract, ALU.mult).then_inc(ready, 1)

        def transpose_y(pe, ready):
            for k in range(NK):
                for i in range(NT):
                    last = pe.transpose(bank(0)[:, k * L + i * P:k * L + (i + 1) * P], y[:, i, k * P:(k + 1) * P],
                                        ident[:])
            last.then_inc(ready, 1)

        def project(pe, n, vbank, ready):
            for out, w in ((1, wq[n]), (2, wk[n])):
                for a in range(2):
                    for k in range(NK):
                        last = pe.matmul(bank(out)[:, a * L:(a + 1) * L], w[:, k, a * P:(a + 1) * P], yT[:, k, :],
                                         start=k == 0, stop=k == NK - 1)
            last.then_inc(ready, 1)
            for i in range(NT):
                for k in range(NK):
                    last = pe.matmul(bank(vbank)[:, i * D:(i + 1) * D], yT[:, k, i * P:(i + 1) * P], wv[n][:, k, :],
                                     start=k == 0, stop=k == NK - 1)
            last.then_inc(ready, 1)

        def copy_qk(act, n, q32, parts, done):
            for a, bias in ((0, bq[n]), (1, bk[n])):
                for c in range(2):
                    src = bank(1 + a)[:, c * L:(c + 1) * L]
                    act.activation(q32[:, a, c, :], src, ACT.Identity, bias=bias[:, c:c + 1])
                    act.activation(parts[:, a, 0, c, :], src, ACT.Identity, bias=bias[:, c:c + 1]).then_inc(done, 1)

        def split_qk(dve, q, q32, parts, rest, ready, chain, done):
            dve.wait_ge(ready, q * 4 + 4)
            dve.tensor_tensor(rest[:], q32[:], parts[:, :, 0], ALU.subtract)
            dve.tensor_tensor(parts[:, :, 1], q32[:], parts[:, :, 0], ALU.subtract).then_inc(chain, 1)
            dve.wait_ge(chain, q + 1)
            dve.tensor_tensor(parts[:, :, 2], rest[:], parts[:, :, 1], ALU.subtract).then_inc(done, 1)

        def store_parts(sp, dram, tile, stored):
            sp.dma_start(dram.rearrange("a x (c p) l -> p (a x c) l", p=P), tile.rearrange("p a x c l -> p (a x c) l"))\
              .then_inc(stored, 16)

        def load_stack(sp, dram, stack, which, loaded):
            for n, part in enumerate(which):
                sp.dma_start(stack[n * HD:(n + 1) * HD], dram[part].rearrange("(h d) l -> d h l", d=HD)).then_inc(loaded, 16)

        def heads_to_tokens(pe, first, ready):
            for i in range(NT):
                for g in range(G):
                    last = pe.transpose(bank(first + i)[:, g * P:(g + 1) * P], xT[:, g, i * P:(i + 1) * P], ident[:])
            last.then_inc(ready, 1)

        def attention_out(dve, b, first, xo_ps, chain, done):
            dve.wait_ge(xo_ps, b + 1)
            out = bank(first, 2).rearrange("p t (h s) -> p t h s", s=SLOT)
            dve.reciprocal(xden[:], out[:, :, :, ONE]).then_inc(chain, 1)
            dve.wait_ge(chain, b * 2 + 1)
            dve.tensor_tensor(xo[:].rearrange("p t (h d) -> p t h d", d=HD), out[:, :, :, 0:HD],
                              xden[:].unsqueeze(3).to_broadcast([P, NT, H, HD]), ALU.mult).then_inc(chain, 1)
            dve.wait_ge(chain, b * 2 + 2)
            rows = bass.ds(b * NT, NT)
            dve.tensor_tensor(h[:, rows, :], h[:, rows, :], xo[:], ALU.add).then_inc(done, 1)

        def heads(ap, width=HD):
            return ap.rearrange("p (h w) -> p h w", w=width)

        with ExitStack() as tmp:
            q32 = sb("q32a", [P, 2, 2, L], F32, tmp)
            parts = sb("partsa", [P, 2, 3, 2, L], BF16, tmp)
            rest = sb("resta", [P, 2, 2, L], F32, tmp)
            lm32 = sb("lm32", [P, 2, 2, M], F32, tmp)
            lmrest = sb("lmrest", [P, 2, 2, M], F32, tmp)
            lmparts = sb("lmparts", [P, 2, 3, 2, M], BF16, tmp)
            lmstk = sb("lmstk", [P, 2, H, M], BF16, tmp)
            nmax = sb("nmax", [P, H], F32, tmp)
            nbias = sb("nbias", [P, H], F32, tmp)
            rsum = sb("rsum", [P, H], F32, tmp)
            rinv = sb("rinv", [P, H], F32, tmp)
            expo = sb("expo", [P, H, M], F32, tmp)
            k2 = sb("k2", [P, H, M], F32, tmp)
            cmax = sb("cmax", [P, NB], F32, tmp)
            dmax = sb("dmax", [P, P], F32, tmp)
            msum = sb("msum", [P, 1], F32, tmp)
            ones = sb("ones", [P, P], F32, tmp)
            names = ("ln_stat", "ln_rstd_done", "y_done", "ln_step", "pow_step", "yT_ps", "yT_done", "qkv_ps", "qk_done",
                     "v_done", "split_step", "parts_done", "pair_step", "lmparts_done", "parts_stored", "lm_stored",
                     "lm_loaded", "s_ps", "max_step", "max_done", "exp_done", "rinv_done", "k2_done", "k2_stored",
                     "col_ps", "col_done", "ones_done", "dmax_done", "all_ps")
            (ln_stat, ln_rstd_done, y_done, ln_step, pow_step, yT_ps, yT_done, qkv_ps, qk_done, v_done, split_step,
             parts_done, pair_step, lmparts_done, parts_stored, lm_stored, lm_loaded, s_ps, max_step, max_done,
             exp_done, rinv_done, k2_done, k2_stored, col_ps, col_done, ones_done, dmax_done,
             all_ps) = (sem("lm_" + n) for n in names)

            def pipeline(eng, step):
                for b in range(-3, 1):
                    step(b)
                with eng.Fori(1, NB - 3) as b:
                    step(b)
                for b in range(NB - 3, NB + 1):
                    step(b)

            def has(c):
                return not isinstance(c, int) or 0 <= c < NB

            with nc.Block() as block:
                @block.sync
                def _(sp):
                    sp.sem_inc(k2_stored, 16)
                    sp.sem_inc(parts_stored, 16)
                    sp.sem_inc(lm_stored, 16)

                    def step(b):
                        if has(b + 1):
                            c = b + 1
                            sp.wait_ge(parts_done, c + 1)
                            store_parts(sp, tok_parts[0][c], parts[:], parts_stored)
                            sp.wait_ge(lmparts_done, c + 1)
                            store_parts(sp, lm_parts[c], lmparts[:], lm_stored)
                            if has(b):
                                sp.wait_ge(s_ps, c)
                            sp.wait_ge(lm_stored, c * 16 + 32)
                            for a, which in ((0, Q_PARTS), (1, K_PARTS)):
                                load_stack(sp, lm_parts[c, a], lmstk[:, a], which, lm_loaded)
                        if has(b):
                            sp.wait_ge(k2_done, b + 1)
                            sp.dma_start(k2_dram[b], k2[:].rearrange("p h m -> p (h m)")).then_inc(k2_stored, 16)

                    pipeline(sp, step)
                    sp.wait_ge(k2_stored, 16 * NB + 16)
                    sp.wait_ge(parts_stored, 16 * NB + 16)

                @block.gpsimd
                def _(pool):
                    def landmarks(c):
                        pool.wait_ge(qk_done, c * 4 + 4)
                        pair = q32[:].rearrange("p a c (m two) -> p (a c) m two", two=2)
                        flat = [x.rearrange("p a c m -> p (a c) m") for x in (lm32[:], lmrest[:])]
                        part = [lmparts[:, :, n] for n in range(3)]
                        pool.tensor_tensor(flat[0], pair[:, :, :, 0], pair[:, :, :, 1], ALU.add).then_inc(pair_step, 1)
                        pool.wait_ge(lm_stored, c * 16 + 16)
                        for a in range(2):
                            pool.tensor_tensor(part[0][:, a], pair[:, 2 * a:2 * a + 2, :, 0], pair[:, 2 * a:2 * a + 2, :, 1],
                                               ALU.add).then_inc(pair_step, 1)
                        pool.wait_ge(pair_step, c * 5 + 3)
                        pool.tensor_tensor(lmrest[:], lm32[:], part[0], ALU.subtract).then_inc(pair_step, 1)
                        pool.tensor_tensor(part[1], lm32[:], part[0], ALU.subtract).then_inc(pair_step, 1)
                        pool.wait_ge(pair_step, c * 5 + 5)
                        pool.tensor_tensor(part[2], lmrest[:], part[1], ALU.subtract).then_inc(lmparts_done, 1)

                    def step(b):
                        if has(b + 3):
                            ln_rstd(pool, b + 3, ln_stat, pow_step, ln_rstd_done)
                        if has(b + 1):
                            landmarks(b + 1)
                        if has(b):
                            pool.wait_ge(rinv_done, b + 1)
                            pool.wait_ge(k2_stored, b * 16 + 16)
                            pool.tensor_tensor(k2[:], expo[:], rinv[:].unsqueeze(2).to_broadcast([P, H, M]),
                                               ALU.mult).then_inc(k2_done, 1)

                    pipeline(pool, step)

                @block.scalar
                def _(act):
                    def step(b):
                        if has(b + 1):
                            act.wait_ge(qkv_ps, (b + 1) * 2 + 1)
                            act.wait_ge(parts_stored, (b + 1) * 16 + 16)
                            if has(b):
                                act.wait_ge(parts_done, b + 1)
                                act.wait_ge(lmparts_done, b + 1)
                            copy_qk(act, 0, q32, parts, qk_done)
                        if has(b + 2):
                            act.wait_ge(yT_ps, b + 3)
                            act.activation(yT[:].rearrange("p k m -> p (k m)"), bank(0), ACT.Copy).then_inc(yT_done, 1)
                        if has(b):
                            act.wait_ge(max_done, b + 1)
                            if has(b - 1):
                                act.wait_ge(k2_done, b)
                                act.wait_ge(col_ps, b)
                            for i in range(H):
                                act.activation(expo[:, i, :], bank(4 + i // J)[:, (i % J) * M:(i % J + 1) * M], ACT.Exp,
                                               bias=nbias[:, i:i + 1], scale=0.0625,
                                               accum_out=rsum[:, i:i + 1]).then_inc(exp_done, 1)

                    pipeline(act, step)

                @block.vector
                def _(dve):
                    dve.memset(ones[:], 1.0).then_inc(ones_done, 1)
                    dve.memset(vall[:], 1.0).then_inc(ones_done, 1)
                    dve.wait_ge(ones_done, 2)

                    def step(b):
                        if has(b + 3):
                            ln_statistics(dve, b + 3, b + 3, ln_step, ln_stat)
                        if has(b + 1):
                            dve.wait_ge(qkv_ps, (b + 1) * 2 + 2)
                            vb = vall[:, b + 1, :].rearrange("p (t h w) -> p t h w", t=NT, w=VW)
                            for i in range(NT):
                                dve.tensor_tensor(vb[:, i, :, 0:HD], heads(bank(3)[:, i * D:(i + 1) * D]), heads(bv[0][:]),
                                                  ALU.add).then_inc(v_done, 1)
                        if has(b - 1):
                            dve.wait_ge(col_ps, b)
                            dve.tensor_reduce(cmax[:, bass.ds(b - 1, 1)], bank(0)[:, 0:H], axis=AX.X,
                                              op=ALU.max).then_inc(col_done, 1)
                        if has(b + 1):
                            split_qk(dve, b + 1, q32, parts, rest, qk_done, split_step, parts_done)
                        if has(b):
                            dve.wait_ge(s_ps, b + 1)
                            dve.tensor_reduce(nmax[:], bank(4, 4).rearrange("p j (g m) -> p (j g) m", m=M), axis=AX.X,
                                              op=ALU.max, negate=True).then_inc(max_step, 1)
                            dve.wait_ge(max_step, b + 1)
                            dve.tensor_scalar(nbias[:], nmax[:], 0.0625, None, ALU.mult).then_inc(max_done, 1)
                        if has(b + 3):
                            if has(b + 2):
                                dve.wait_ge(yT_ps, b + 3)
                            ln_scale(dve, b + 3, b + 3, ln_rstd_done, y_done)
                        if has(b):
                            dve.wait_ge(exp_done, b * H + H)
                            dve.reciprocal(rinv[:], rsum[:]).then_inc(rinv_done, 1)

                    pipeline(dve, step)
                    dve.wait_ge(col_done, NB)
                    dve.tensor_reduce(msum[:], cmax[:], axis=AX.X, op=ALU.max).then_inc(max_step, 1)
                    dve.wait_ge(max_step, NB + 1)
                    dve.tensor_scalar(dmax[:], ident[:], msum[:, 0:1], None, ALU.mult).then_inc(dmax_done, 1)
                    dve.wait_ge(all_ps, 1)
                    dve.tensor_reduce(msum[:], bank(1)[:, 0:P], axis=AX.X, op=ALU.max).then_inc(max_step, 1)
                    dve.wait_ge(max_step, NB + 2)
                    dve.reciprocal(minv[:, 1:2], msum[:]).then_inc(max_step, 1)
                    dve.wait_ge(max_step, NB + 3)
                    dve.tensor_scalar(minv[:, 0:1], minv[:, 1:2], -1.0, None, ALU.mult)

                @block.tensor
                def _(pe):
                    pe.wait_ge(ones_done, 2)

                    def step(b):
                        if has(b + 1):
                            pe.wait_ge(yT_done, b + 2)
                            if has(b):
                                pe.wait_ge(qk_done, (b + 1) * 4)
                                pe.wait_ge(v_done, (b + 1) * NT)
                            project(pe, 0, 3, qkv_ps)
                        if has(b - 1):
                            pe.wait_ge(rinv_done, b)
                            if has(b - 2):
                                pe.wait_ge(col_done, b - 1)
                            for i in range(H):
                                last = pe.matmul(bank(0)[:, i:i + 1], expo[:, i, :], rinv[:, i:i + 1], start=True, stop=True)
                            last.then_inc(col_ps, 1)
                        if has(b + 2):
                            pe.wait_ge(y_done, (b + 3) * NT)
                            if has(b - 1):
                                pe.wait_ge(col_done, b)
                            transpose_y(pe, yT_ps)
                        if has(b):
                            pe.wait_ge(lm_loaded, (b + 1) * (16 * 2 * len(Q_PARTS)))
                            if has(b - 1):
                                pe.wait_ge(exp_done, b * H)
                            for i in range(H):
                                last = pe.matmul(bank(4 + i // J)[:, (i % J) * M:(i % J + 1) * M], lmstk[0:STACK, 0, i, :],
                                                 lmstk[0:STACK, 1, i, :], start=True, stop=True)
                            last.then_inc(s_ps, 1)

                    pipeline(pe, step)
                    pe.wait_ge(dmax_done, 1)
                    pe.matmul(bank(1)[:, 0:P], ones[:], dmax[:], start=True, stop=True).then_inc(all_ps, 1)

        with ExitStack() as tmp:
            va = sb("va", [P, NT, H, VW], F32, tmp)
            qlstk = sb("qlstk", [P, H, M], BF16, tmp)
            klstk = sb("klstk", [P, H, M], BF16, tmp)
            nmax = sb("nmaxn", [P, 3, H], F32, tmp)
            nparts = sb("nparts", [P, SHIFT, 3, H], BF16, tmp)
            nrow = sb("nrow", [SHIFT * 3 * H, P], BF16, tmp)
            p3 = sb("p3", [P, J, L], F32, tmp)
            p1 = [sb(f"p1{x}", [P, H, L], F32, tmp) for x in range(2)]
            yn = [sb(f"yn{x}", [P, H, HD], F32, tmp) for x in range(2)]
            den = sb("den", [P, H], F32, tmp)
            k2 = [sb(f"k2n{x}", [P, H, M], F32, tmp) for x in range(2)]
            k2T = sb("k2T", [P, H, M], F32, tmp)
            ey = sb("ey", [P, NU, U, EW], F32, tmp)
            gu = sb("gu", [P, NU, U, EW], F32, tmp)
            e2 = sb("e2", [P, NU, U, EW], F32, tmp)
            ya = sb("ya", [P, NU, U, HD], F32, tmp)
            zc = sb("zc", [P, H, SLOT], F32, tmp)
            names = ("stk_loaded", "k2_loaded", "s_ps", "nmax_done", "npart_step", "nparts_done", "nrow_ps", "nrow_done",
                     "nrow_stored", "shift_loaded", "st_ps", "exp_done", "yn_ps", "yn_step", "yn_done",
                     "k2T_ps", "k2T_done", "kk_ps", "e0_done", "sq_ps", "sq_act", "sq_dve", "cu_ps", "cu_act",
                     "cu_dve", "thin_ps", "thin_done", "z_ps", "z_done", "x_ps", "xT_done", "xo_ps", "out_step",
                     "h_done", "clear")
            (stk_loaded, k2_loaded, s_ps, nmax_done, npart_step, nparts_done, nrow_ps, nrow_done, nrow_stored,
             shift_loaded, st_ps, exp_done, yn_ps, yn_step, yn_done, k2T_ps, k2T_done, kk_ps, e0_done, sq_ps,
             sq_act, sq_dve, cu_ps, cu_act, cu_dve, thin_ps, thin_done, z_ps, z_done, x_ps, xT_done, xo_ps,
             out_step, h_done, clear) = (sem("ny_" + n) for n in names)
            LAST = ITERS - 1
            NSTK = 16 * (4 * len(Q_PARTS) + 1)

            def prod(a):
                return bank(4 + a).rearrange("p (i n) -> p i n", i=U)

            def unit(half_, a):
                return slice((half_ * NU + a) * U, (half_ * NU + a + 1) * U)

            def turn(b, half_, k=0):
                return (b * 2 + half_) * (ITERS * NU) + k * NU

            def cube(b, half_, k=0):
                return (b * 2 + half_) * (ITERS * NU) + k * NU

            def batches(eng, ahead_first, both):
                ahead_first()
                with eng.Fori(0, NB // 2 - 1) as pair:
                    both(pair * 2, 0, True)
                    both(pair * 2 + 1, 1, True)
                both(NB - 2, 0, True)
                both(NB - 1, 1, False)

            with nc.Block() as block:
                @block.sync
                def _(sp):
                    def load(b, x):
                        load_stack(sp, tok_parts[0][b, 0], qstk, Q_PARTS, stk_loaded)
                        load_stack(sp, tok_parts[0][b, 1], kstk, K_PARTS, stk_loaded)
                        load_stack(sp, lm_parts[b, 0], qlstk, Q_PARTS, stk_loaded)
                        load_stack(sp, lm_parts[b, 1], klstk, K_PARTS, stk_loaded)
                        sp.dma_start(va[:].rearrange("p t h w -> p (t h w)"), vall[:, b, :]).then_inc(stk_loaded, 16)

                    def load_k2(b, x):
                        sp.dma_start(k2[x][:].rearrange("p h m -> p (h m)"), k2_dram[b]).then_inc(k2_loaded, 16)

                    def shifts(b):
                        sp.wait_ge(nrow_done, b + 1)
                        sp.dma_start(shift0[b].rearrange("x c h l -> (x c h) l"), nrow[:]).then_inc(nrow_stored, 16)
                        sp.wait_ge(nrow_stored, b * 16 + 16)
                        sp.dma_start(qlstk[STACK:FULL], shift0[b, :, 0]).then_inc(shift_loaded, 16)
                        for i in range(NT):
                            sp.dma_start(qstk[STACK:FULL, :, i * P:(i + 1) * P], shift0[b, :, 1 + i]).then_inc(shift_loaded, 16)

                    def first():
                        load(0, 0)
                        load_k2(0, 0)
                        shifts(0)
                        sp.wait_ge(yn_ps, G)
                        load(1, 1)

                    def both(b, x, more):
                        if more:
                            if not isinstance(b, int) or b > 0:
                                sp.wait_ge(z_ps, b + 1)
                            load_k2(b + 1, 1 - x)
                            shifts(b + 1)
                            if not isinstance(b, int) or b + 2 < NB:
                                sp.wait_ge(yn_ps, (b + 2) * G)
                                load(b + 2, x)

                    sp.sem_inc(z_ps, 1)
                    batches(sp, first, both)
                    sp.wait_ge(stk_loaded, NSTK * NB)
                    sp.wait_ge(k2_loaded, 16 * NB)

                @block.scalar
                def _(act):
                    def shift_rows(b):
                        act.wait_ge(nrow_ps, b + 1)
                        act.activation(nrow[:], bank(0)[0:SHIFT * 3 * H, 0:P // 2].bitcast(BF16), ACT.Copy).then_inc(nrow_done, 1)

                    def exponentials3(b, g):
                        act.wait_ge(st_ps, b * G + g + 1)
                        act.activation(p3[:], bank(0, 4)[:, :, 0:L], ACT.Exp, scale=0.125).then_inc(exp_done, 1)

                    def exponentials1(b, x, g):
                        act.activation(p1[x][:, g * J:(g + 1) * J, :], bank(0, 4)[:, :, L:2 * L], ACT.Exp,
                                       scale=0.125).then_inc(exp_done, 1)

                    def copy_k2T(b):
                        act.wait_ge(k2T_ps, b + 1)
                        act.activation(k2T[:], bank(0, 4).rearrange("p a (i m) -> p (a i) m", m=M), ACT.Copy).then_inc(k2T_done, 1)

                    def first():
                        shift_rows(0)
                        for g in range(G):
                            exponentials3(0, g)
                            exponentials1(0, 0, g)
                        copy_k2T(0)

                    def both(b, x, more):
                        for half_ in range(2):
                            for k in range(ITERS):
                                for a in range(NU):
                                    act.wait_ge(sq_ps, turn(b, half_, k) + a + 1)
                                    act.activation(e2[:, a], prod(a)[:, :, 0:EW], ACT.Copy).then_inc(sq_act, 1)
                                if more and half_ == 0 and k == G:
                                    shift_rows(b + 1)
                                if more and half_ == 1 and k < G:
                                    exponentials3(b + 1, k)
                                if more and half_ == 1 and k == LAST:
                                    copy_k2T(b + 1)
                                if k < LAST:
                                    for a in range(NU):
                                        act.wait_ge(cu_ps, cube(b, half_, k) + a + 1)
                                        act.activation(ey[:, a], prod(a)[:, :, 0:EW], ACT.Copy, scale=0.25).then_inc(cu_act, 1)
                                if more and half_ == 1 and k < G:
                                    exponentials1(b + 1, 1 - x, k)
                        act.wait_ge(x_ps, b + 1)
                        act.activation(xT[:], bank(0, 2).rearrange("p a (i n) -> p (a i) n", i=2), ACT.Copy).then_inc(xT_done, 1)

                    batches(act, first, both)

                @block.vector
                def _(dve):
                    def maxima3(b, g):
                        dve.wait_ge(s_ps, b * G + g + 1)
                        dve.tensor_reduce(nmax[:, 0, g * J:(g + 1) * J], bank(0, 4)[:, :, 0:L], axis=AX.X, op=ALU.max,
                                          negate=True)

                    def maxima1(b, g):
                        cols = nmax[:, :, g * J:(g + 1) * J].rearrange("p c j -> p j c")
                        dve.tensor_reduce(cols[:, :, 1:3], bank(0, 4)[:, :, L:2 * L].rearrange("p j (c n) -> p j c n", c=2),
                                          axis=AX.X, op=ALU.max, negate=True).then_inc(nmax_done, 1)

                    def maxima_parts(b):
                        dve.wait_ge(nmax_done, b * G + G)
                        dve.tensor_copy(nparts[:, 0], nmax[:]).then_inc(npart_step, 1)
                        dve.wait_ge(npart_step, b + 1)
                        dve.tensor_tensor(nparts[:, 1], nmax[:], nparts[:, 0], ALU.subtract).then_inc(nparts_done, 1)

                    def norm_y(b, x, g):
                        dve.wait_ge(yn_ps, b * G + g + 1)
                        out = heads(bank(1)[:, 0:J * SLOT], SLOT)
                        dve.reciprocal(den[:, g * J:(g + 1) * J], out[:, :, ONE]).then_inc(yn_step, 1)
                        dve.wait_ge(yn_step, b * G + g + 1)
                        dve.tensor_tensor(yn[x][:, g * J:(g + 1) * J, :], out[:, :, 0:HD],
                                          den[:, g * J:(g + 1) * J].unsqueeze(2).to_broadcast([P, J, HD]),
                                          ALU.mult).then_inc(yn_done, 1)

                    def first():
                        dve.memset(kstk[STACK:P], 1.0)
                        dve.memset(klstk[STACK:P], 1.0)
                        dve.memset(zc[:], 0.0).then_inc(clear, 1)
                        dve.wait_ge(clear, 1)
                        dve.memset(zc[:, :, ONE:ONE + 1], 1.0).then_inc(clear, 1)
                        for g in range(G):
                            maxima3(0, g)
                            maxima1(0, g)
                        maxima_parts(0)
                        for g in range(G):
                            norm_y(0, 0, g)

                    def both(b, x, more):
                        for half_ in range(2):
                            for a in range(NU):
                                dve.wait_ge(kk_ps, (b * 2 + half_) * NU + a + 1)
                                dve.scalar_tensor_tensor(ey[:, a, :, 0:P], prod(a)[:, :, 0:P], minv[:, 0:1],
                                                         ident[:].unsqueeze(1).to_broadcast([P, U, P]), ALU.mult, ALU.add)
                                dve.tensor_copy(ey[:, a, :, P:EW], yn[x][:, unit(half_, a), :]).then_inc(e0_done, 1)
                            for k in range(ITERS):
                                for a in range(NU):
                                    dve.wait_ge(sq_act, turn(b, half_, k) + a + 1)
                                    dve.tensor_tensor(ya[:, a], ey[:, a, :, P:EW], e2[:, a, :, P:EW], ALU.add)
                                    last = dve.scalar_tensor_tensor(gu[:, a, :, P:EW], e2[:, a, :, P:EW], 0.25,
                                                                    ey[:, a, :, P:EW], ALU.mult, ALU.add)
                                    if k < LAST:
                                        last = dve.scalar_tensor_tensor(gu[:, a, :, 0:P], ey[:, a, :, 0:P], 3.0,
                                                                        e2[:, a, :, 0:P], ALU.mult, ALU.add)
                                    last.then_inc(sq_dve, 1)
                                if more and half_ == 0 and k < G:
                                    maxima3(b + 1, k)
                                if more and half_ == 1 and 1 <= k <= G:
                                    norm_y(b + 1, 1 - x, k - 1)
                                for a in range(NU):
                                    if k < LAST:
                                        dve.wait_ge(cu_act, (b * 2 + half_) * (LAST * NU) + k * NU + a + 1)
                                        dve.scalar_tensor_tensor(ey[:, a, :, P:EW], ey[:, a, :, P:EW], 4.0, ya[:, a],
                                                                 ALU.mult, ALU.add).then_inc(cu_dve, 1)
                                    else:
                                        dve.wait_ge(cu_ps, cube(b, half_, k) + a + 1)
                                        dve.tensor_tensor(yn[x][:, unit(half_, a), :], prod(a)[:, :, P:EW], ya[:, a],
                                                          ALU.add).then_inc(thin_done, 1)
                                if more and half_ == 0 and k < G:
                                    maxima1(b + 1, k)
                                if more and half_ == 0 and k == G - 1:
                                    maxima_parts(b + 1)
                        dve.wait_ge(z_ps, b + 2)
                        dve.tensor_scalar(zc[:, :, 0:HD], heads(bank(4)[:, 0:H * HD]), minv[:, 1:2], None,
                                          ALU.mult).then_inc(z_done, 1)
                        attention_out(dve, b, 2, xo_ps, out_step, h_done)

                    batches(dve, first, both)

                @block.tensor
                def _(pe):
                    def logits(b, g):
                        if g > 0:
                            pe.wait_ge(nmax_done, b * G + g)
                        for j in range(J):
                            head = g * J + j
                            pe.matmul(bank(j)[:, 0:L], qlstk[0:STACK, head, :], kstk[0:STACK, head, :], start=True, stop=True)
                            for i in range(NT):
                                last = pe.matmul(bank(j)[:, L + i * P:L + (i + 1) * P],
                                                 qstk[0:STACK, head, i * P:(i + 1) * P], klstk[0:STACK, head, :],
                                                 start=True, stop=True)
                        last.then_inc(s_ps, 1)

                    def maxima_to_rows(b):
                        pe.wait_ge(nparts_done, b + 1)
                        pe.transpose(bank(0)[0:SHIFT * 3 * H, 0:P // 2].bitcast(BF16),
                                     nparts[:].rearrange("p x c h -> p (x c h)"), identb[:]).then_inc(nrow_ps, 1)

                    def transposed_logits(b, g):
                        if g == 0:
                            pe.wait_ge(shift_loaded, (b + 1) * (16 * 3))
                            pe.wait_ge(nrow_done, b + 1)
                        else:
                            pe.wait_ge(exp_done, (b * G + g) * 2)
                        for j in (0, 2, 3, 1):
                            if j == 1 and g > 0:
                                pe.wait_ge(yn_done, b * G + g)
                            head = g * J + j
                            for i in range(NT):
                                pe.matmul(bank(j)[:, i * P:(i + 1) * P], kstk[0:FULL, head, i * P:(i + 1) * P],
                                          qlstk[0:FULL, head, :], start=True, stop=True)
                            last = pe.matmul(bank(j)[:, L:2 * L], klstk[0:FULL, head, :], qstk[0:FULL, head, :],
                                             start=True, stop=True)
                        last.then_inc(st_ps, 1)

                    def kernel3_values(b, g):
                        pe.wait_ge(exp_done, (b * G + g + 1) * 2)
                        for j in range(J):
                            for i in range(NT):
                                last = pe.matmul(bank(1)[:, j * SLOT:j * SLOT + VW], p3[:, j, i * P:(i + 1) * P],
                                                 va[:, i, g * J + j, :], start=i == 0, stop=i == NT - 1)
                        last.then_inc(yn_ps, 1)

                    def kernel2_transposed(b, x):
                        pe.wait_ge(k2_loaded, b * 16 + 16)
                        for i in range(H):
                            last = pe.transpose(bank(i // J)[:, (i % J) * M:(i % J + 1) * M], k2[x][:, i, :], ident[:])
                        last.then_inc(k2T_ps, 1)

                    def first():
                        pe.wait_ge(clear, 2)
                        pe.wait_ge(stk_loaded, NSTK)
                        for g in range(G):
                            logits(0, g)
                        maxima_to_rows(0)
                        for g in range(G):
                            transposed_logits(0, g)
                            kernel3_values(0, g)
                        pe.wait_ge(yn_done, G)
                        kernel2_transposed(0, 0)

                    def both(b, x, more):
                        for half_ in range(2):
                            if half_ == 0:
                                pe.wait_ge(k2T_done, b + 1)
                            for a in range(NU):
                                if half_ == 1:
                                    pe.wait_ge(thin_done, b * (2 * NU) + a + 1)
                                for i in range(U):
                                    kT_h = k2T[:, (half_ * NU + a) * U + i, :]
                                    last = pe.matmul(prod(a)[:, i, 0:P], kT_h, kT_h, start=True, stop=True)
                                last.then_inc(kk_ps, 1)
                            for k in range(ITERS):
                                for a in range(NU):
                                    if k == 0:
                                        pe.wait_ge(e0_done, (b * 2 + half_) * NU + a + 1)
                                    else:
                                        pe.wait_ge(cu_dve, (b * 2 + half_) * (LAST * NU) + (k - 1) * NU + a + 1)
                                    for i in range(U):
                                        last = pe.matmul(prod(a)[:, i, 0:EW], ey[:, a, i, 0:P], ey[:, a, i, :],
                                                         start=True, stop=True)
                                    last.then_inc(sq_ps, 1)
                                if more and half_ == 0 and k < G:
                                    if k == 0:
                                        pe.wait_ge(stk_loaded, (b + 2) * NSTK)
                                    logits(b + 1, k)
                                if more and half_ == 0 and k == G:
                                    maxima_to_rows(b + 1)
                                if more and half_ == 1 and 1 <= k <= G:
                                    kernel3_values(b + 1, k - 1)
                                if more and half_ == 1 and k < G:
                                    transposed_logits(b + 1, k)
                                if more and half_ == 1 and k == LAST:
                                    pe.wait_ge(yn_done, (b + 2) * G)
                                    kernel2_transposed(b + 1, 1 - x)
                                for a in range(NU):
                                    pe.wait_ge(sq_dve, turn(b, half_, k) + a + 1)
                                    cols = slice(0 if k < LAST else P, EW)
                                    for i in range(U):
                                        last = pe.matmul(prod(a)[:, i, cols], e2[:, a, i, 0:P], gu[:, a, i, cols],
                                                         start=True, stop=True)
                                    last.then_inc(cu_ps, 1)
                        pe.wait_ge(thin_done, (b + 1) * (2 * NU))
                        for i in range(H):
                            last = pe.matmul(bank(4)[:, i * HD:(i + 1) * HD], k2[x][:, i, :], yn[x][:, i, :],
                                             start=True, stop=True)
                        last.then_inc(z_ps, 1)
                        pe.wait_ge(z_done, b + 1)
                        if more:
                            pe.wait_ge(k2T_done, b + 2)
                        for i in range(H):
                            g, j = i // J, i % J
                            last = pe.matmul(bank(g // 2)[SLOT * j:SLOT * (j + 1), (g % 2) * L:(g % 2 + 1) * L],
                                             zc[:, i, :], p1[x][:, i, :], start=True, stop=True)
                        last.then_inc(x_ps, 1)
                        pe.wait_ge(xT_done, b + 1)
                        heads_to_tokens(pe, 2, xo_ps)
                        pe.wait_ge(h_done, b + 1)

                    batches(pe, first, both)

        with ExitStack() as tmp:
            q32 = sb("q32b", [P, 2, 2, L], F32, tmp)
            parts = sb("partsb", [P, 2, 3, 2, L], BF16, tmp)
            rest = sb("restb", [P, 2, 2, L], F32, tmp)
            W3 = 3 * P
            va = [sb(f"va1{x}", [P, NT, H, SLOT], F32, tmp) for x in range(2)]
            nmax = sb("nmax1", [P, NT, H], F32, tmp)
            npad = sb("npad", [P, P], BF16, tmp)
            nparts = npad[:, 0:SHIFT * NT * H].rearrange("p (x c h) -> p x c h", x=SHIFT, c=NT)
            nrow = sb("nrow1", [SHIFT * NT * H, P], BF16, tmp)
            pT = sb("pT", [P, 2, J, W3], F32, tmp)
            res = sb("res", [P, NT, D], F32, tmp)
            names = ("ln_stat", "ln_rstd_done", "y_done", "ln_step", "pow_step", "yT_ps", "yT_done", "ffn_ps",
                     "ffn_done", "qkv_ps", "qk_done", "v_done", "split_step", "parts_done", "parts_stored",
                     "stk_loaded", "s_ps", "nmax_done", "npart_step", "nparts_done", "nrow_ps", "nrow_done",
                     "nrow_stored", "shift_loaded", "st_ps", "exp_done", "pv_ps", "xT_done", "xo_ps", "out_step",
                     "h_done", "clear", "four_ps", "bias_done", "res_done", "stored")
            (ln_stat, ln_rstd_done, y_done, ln_step, pow_step, yT_ps, yT_done, ffn_ps, ffn_done, qkv_ps, qk_done,
             v_done, split_step, parts_done, parts_stored, stk_loaded, s_ps, nmax_done, npart_step, nparts_done,
             nrow_ps, nrow_done, nrow_stored, shift_loaded, st_ps, exp_done, pv_ps, xT_done, xo_ps, out_step,
             h_done, clear, four_ps, bias_done, res_done, stored) = (sem("tl_" + n) for n in names)
            NSTK1 = 16 * 2 * len(Q_PARTS)

            def batches(eng, first_half, second_half):
                first_half(None, 0, 0, 0)
                with eng.Fori(0, NB // 2 - 1) as pair:
                    for x in range(2):
                        b = pair * 2 + x
                        first_half(b, b + 1, 1 - x, b * 3 + 2)
                        second_half(b, x, b * 3 + 4)
                first_half(NB - 2, NB - 1, 1, NB * 3 - 4)
                second_half(NB - 2, 0, NB * 3 - 2)
                first_half(NB - 1, None, 0, 0)
                second_half(NB - 1, 1, NB * 3 - 1)

            with nc.Block() as block:
                @block.sync
                def _(sp):
                    sp.sem_inc(stored, 16)
                    sp.sem_inc(parts_stored, 16)

                    def load(c):
                        sp.wait_ge(parts_done, c + 1)
                        store_parts(sp, tok_parts[1][c], parts[:], parts_stored)
                        if not isinstance(c, int) or c > 0:
                            sp.wait_ge(st_ps, c * G)
                        sp.wait_ge(parts_stored, c * 16 + 32)
                        load_stack(sp, tok_parts[1][c, 0], qstk, Q_PARTS, stk_loaded)
                        load_stack(sp, tok_parts[1][c, 1], kstk, K_PARTS, stk_loaded)

                    def first_half(b, c, x, n):
                        if b is not None:
                            sp.wait_ge(nrow_done, b + 1)
                            sp.dma_start(shift1[b].rearrange("x c h l -> (x c h) l"), nrow[:]).then_inc(nrow_stored, 16)
                            sp.wait_ge(nrow_stored, b * 16 + 16)
                            for i in range(NT):
                                sp.dma_start(qstk[STACK:FULL, :, i * P:(i + 1) * P], shift1[b, :, i]).then_inc(shift_loaded, 16)
                        if c is not None:
                            load(c)

                    def second_half(b, x, n):
                        sp.wait_ge(res_done, b + 1)
                        sp.dma_start(t["out"][b].rearrange("(t p) d -> p t d", p=P), res[:]).then_inc(stored, 16)

                    batches(sp, first_half, second_half)
                    sp.wait_ge(stored, 16 * NB + 16)

                @block.gpsimd
                def _(pool):
                    def first_half(b, c, x, n):
                        if c is not None:
                            for i in range(2):
                                ln_rstd(pool, n + i, ln_stat, pow_step, ln_rstd_done)

                    def second_half(b, x, n):
                        ln_rstd(pool, n, ln_stat, pow_step, ln_rstd_done)

                    batches(pool, first_half, second_half)

                @block.scalar
                def _(act):
                    def copy_yT(n):
                        act.wait_ge(yT_ps, n + 1)
                        act.activation(yT[:].rearrange("p k m -> p (k m)"), bank(0), ACT.Copy).then_inc(yT_done, 1)

                    def exponentials(b, g):
                        act.wait_ge(st_ps, b * G + g + 1)
                        act.activation(pT[:, g % 2], bank(4, 4)[:, :, 0:W3], ACT.Exp, scale=0.25).then_inc(exp_done, 1)

                    def copy_out(b, g):
                        act.wait_ge(pv_ps, b * G + g + 1)
                        act.activation(xT[:, g, :], bank(3)[:, 0:L], ACT.Copy).then_inc(xT_done, 1)

                    def first_half(b, c, x, n):
                        if c is not None:
                            copy_yT(n)
                            copy_yT(n + 1)
                        if b is not None:
                            act.wait_ge(nrow_ps, b + 1)
                            act.activation(nrow[:], bank(4)[0:SHIFT * NT * H, 0:P // 2].bitcast(BF16), ACT.Copy).then_inc(nrow_done, 1)
                        if c is not None:
                            act.wait_ge(qkv_ps, c * 2 + 1)
                            act.wait_ge(parts_stored, c * 16 + 16)
                            copy_qk(act, 1, q32, parts, qk_done)

                    def second_half(b, x, n):
                        exponentials(b, 0)
                        for g in range(G):
                            if g + 1 < G:
                                exponentials(b, g + 1)
                            copy_out(b, g)
                        copy_yT(n)

                    batches(act, first_half, second_half)

                @block.vector
                def _(dve):
                    for x in range(2):
                        dve.memset(va[x][:], 0.0).then_inc(clear, 1)
                        dve.wait_ge(clear, x + 1)
                        dve.memset(va[x][:, :, :, ONE:ONE + 1], 1.0)
                    dve.memset(kstk[STACK:P], 1.0)
                    dve.memset(npad[:], 0.0).then_inc(clear, 1)

                    def maxima(b, g):
                        if b is None:
                            return
                        dve.wait_ge(s_ps, b * G + g + 1)
                        cols = nmax[:, :, g * J:(g + 1) * J]
                        dve.tensor_reduce(cols[:, 0, :], bank(4, 4)[:, :, 0:P], axis=AX.X, op=ALU.max, negate=True)
                        dve.tensor_reduce(cols[:, 1, :], bank(4, 4)[:, :, P:W3], axis=AX.X, op=ALU.max,
                                          negate=True).then_inc(nmax_done, 1)

                    def first_half(b, c, x, n):
                        if c is not None:
                            ln_statistics(dve, c, n, ln_step, ln_stat)
                        maxima(b, 0)
                        if c is not None:
                            ln_scale(dve, c, n, ln_rstd_done, y_done)
                        maxima(b, 1)
                        if c is not None:
                            rows = bass.ds(c * NT, NT)
                            dve.wait_ge(ffn_ps, c + 1)
                            dve.tensor_tensor(h[:, rows, :], h[:, rows, :], bank(1).rearrange("p (t d) -> p t d", t=NT),
                                              ALU.add).then_inc(ffn_done, 1)
                            dve.wait_ge(ffn_done, c + 1)
                            dve.tensor_copy(passed[:], half[:])
                            ln_statistics(dve, c, n + 1, ln_step, ln_stat)
                        maxima(b, 2)
                        if c is not None:
                            ln_scale(dve, c, n + 1, ln_rstd_done, y_done)
                        maxima(b, 3)
                        if b is not None:
                            dve.wait_ge(nmax_done, b * G + G)
                            dve.tensor_copy(nparts[:, 0], nmax[:]).then_inc(npart_step, 1)
                            dve.wait_ge(npart_step, b + 1)
                            dve.tensor_tensor(nparts[:, 1], nmax[:], nparts[:, 0], ALU.subtract).then_inc(nparts_done, 1)
                        if c is not None:
                            split_qk(dve, c, q32, parts, rest, qk_done, split_step, parts_done)
                            dve.wait_ge(qkv_ps, c * 2 + 2)
                            for i in range(NT):
                                dve.tensor_tensor(va[x][:, i, :, 0:HD], heads(bank(0)[:, i * D:(i + 1) * D]), heads(bv[1][:]),
                                                  ALU.add).then_inc(v_done, 1)

                    def second_half(b, x, n):
                        rows = bass.ds(b * NT, NT)
                        attention_out(dve, b, 4, xo_ps, out_step, h_done)
                        dve.wait_ge(h_done, b + 1)
                        dve.tensor_copy(passed[:], half[:])
                        ln_statistics(dve, b, n, ln_step, ln_stat)
                        ln_scale(dve, b, n, ln_rstd_done, y_done)
                        dve.wait_ge(stored, b * 16 + 16)
                        dve.tensor_tensor(res[:], h[:, rows, :], bf[:].unsqueeze(1).to_broadcast([P, NT, D]),
                                          ALU.add).then_inc(bias_done, 1)
                        dve.wait_ge(bias_done, b + 1)
                        dve.wait_ge(four_ps, b + 1)
                        dve.tensor_tensor(res[:], res[:], bank(1).rearrange("p (t d) -> p t d", t=NT),
                                          ALU.add).then_inc(res_done, 1)

                    batches(dve, first_half, second_half)

                @block.tensor
                def _(pe):
                    pe.wait_ge(clear, 3)

                    def features(n):
                        pe.wait_ge(y_done, (n + 1) * NT)
                        transpose_y(pe, yT_ps)
                        pe.wait_ge(yT_done, n + 1)

                    def ffn(w, ready):
                        for i in range(NT):
                            for k in range(NK):
                                last = pe.matmul(bank(1)[:, i * D:(i + 1) * D], yT[:, k, i * P:(i + 1) * P], w[:, k, :],
                                                 start=k == 0, stop=k == NK - 1)
                        last.then_inc(ready, 1)

                    def logits(b, g, transposed):
                        left, right = (kstk, qstk) if transposed else (qstk, kstk)
                        rows = slice(0, FULL if transposed else STACK)
                        if transposed:
                            if g == 0:
                                pe.wait_ge(shift_loaded, (b + 1) * (16 * NT))
                                pe.wait_ge(nrow_done, b + 1)
                            else:
                                pe.wait_ge(exp_done, b * G + g)
                        elif g == 0:
                            pe.wait_ge(stk_loaded, (b + 1) * NSTK1)
                        else:
                            pe.wait_ge(nmax_done, b * G + g)
                        for j in range(J):
                            pe.matmul(bank(4 + j)[:, 0:2 * P], identb[:], mask[:, int(transposed), :], start=True, stop=False)
                            for c, (q, k) in enumerate(((0, 0), (1, 1), (1, 0))):
                                l, r = (k, q) if transposed else (q, k)
                                last = pe.matmul(bank(4 + j)[:, c * P:(c + 1) * P], left[rows, g * J + j, l * P:(l + 1) * P],
                                                 right[rows, g * J + j, r * P:(r + 1) * P], start=False, stop=c == 2)
                        last.then_inc(st_ps if transposed else s_ps, 1)

                    def weighted_values(b, g, x):
                        pe.wait_ge(exp_done, b * G + g + 1)
                        if g > 0:
                            pe.wait_ge(xT_done, b * G + g)
                        for j in range(J):
                            out = bank(3)[SLOT * j:SLOT * (j + 1), :]
                            v = [va[x][:, i, g * J + j, :] for i in range(NT)]
                            pe.matmul(out[:, 0:P], v[0], pT[:, g % 2, j, 0:P], start=True, stop=True)
                            pe.matmul(out[:, P:L], v[0], pT[:, g % 2, j, 2 * P:W3], start=True, stop=False)
                            last = pe.matmul(out[:, P:L], v[1], pT[:, g % 2, j, P:2 * P], start=False, stop=True)
                        last.then_inc(pv_ps, 1)

                    def first_half(b, c, x, n):
                        if b is not None:
                            logits(b, 0, False)
                        if c is not None:
                            features(n)
                        if b is not None:
                            logits(b, 1, False)
                        if c is not None:
                            ffn(wt, ffn_ps)
                        if b is not None:
                            logits(b, 2, False)
                        if c is not None:
                            features(n + 1)
                        if b is not None:
                            logits(b, 3, False)
                            pe.wait_ge(nparts_done, b + 1)
                            pe.transpose(bank(4)[:, 0:P // 2].bitcast(BF16), npad[:], identb[:]).then_inc(nrow_ps, 1)
                        if c is not None:
                            project(pe, 1, 0, qkv_ps)

                    def second_half(b, x, n):
                        logits(b, 0, True)
                        for g in range(G):
                            if g + 1 < G:
                                logits(b, g + 1, True)
                            weighted_values(b, g, x)
                        pe.wait_ge(xT_done, b * G + G)
                        heads_to_tokens(pe, 4, xo_ps)
                        features(n)
                        ffn(wf, four_ps)

                    batches(pe, first_half, second_half)


def host_arrays(inputs):
    f = np.float32
    a = {k: np.asarray(v) for k, v in inputs.items()}
    ids = a["x"]
    out = {"ids": ids.reshape(1, NB * L)}
    pos = np.pad(np.arange(L), NFFT // 2, mode="reflect").reshape(NFR, NFFT)
    out["ids_fr"] = np.ascontiguousarray(ids[:, pos].reshape(NB * NFR, NFFT).T)
    out["iota"] = np.arange(V, dtype=f).reshape(1, V)
    out["iota_c"] = np.arange(V, dtype=f).reshape(V, 1)
    ang = 2 * np.pi * np.outer(np.arange(NFFT), np.arange(NFQ)) / NFFT
    out["dft"] = np.stack([np.cos(ang), -np.sin(ang)], 1).astype(f)
    out["window"] = a["L0_tok_window"].reshape(NFFT, 1)
    w = a["L0_tok_proj_w"].reshape(DS, NFQ, V).transpose(2, 1, 0)
    out["wp"] = np.ascontiguousarray(np.concatenate([w, w], 0))
    out["emb"] = a["L0_tok_emb_table"]
    out["proj_b"] = a["L0_tok_proj_b"].reshape(1, DS)
    out["zero"] = np.zeros((1, DS), f)
    coord = np.clip((np.arange(L, dtype=f) + f(0.5)) * f(NFR / L) - f(0.5), 0.0, NFR - 1.0)
    i0 = np.floor(coord).astype(np.int32)
    i1 = np.minimum(i0 + 1, NFR - 1)
    wgt = (coord - i0).astype(f)
    up = np.zeros((NFR, L), f)
    np.add.at(up, (i0, np.arange(L)), 1 - wgt)
    np.add.at(up, (i1, np.arange(L)), wgt)
    full = np.zeros((NB, NFR, NB, L), f)
    for b in range(NB):
        full[b, :, b, :] = up
    full = full.reshape(PAIRS, 2, NB * L)
    interp = np.zeros((PAIRS + 1, 2, NB * L), f)
    interp[:PAIRS] = full
    interp[PAIRS, 0] = 1.0
    out["interp"] = interp
    out["ident"] = np.eye(P, dtype=f)
    out["half"] = np.tile(np.array([-0.5, -0.5, EPS, EPS], f), (P, 1))
    up_m = np.triu(np.full((P, P), NEG, f), 1)
    out["mask"] = np.stack([np.concatenate([m, m], 1) for m in (up_m, up_m.T)], 1)

    def tiles(w):
        return np.ascontiguousarray(w.reshape(NK, P, w.shape[1]).transpose(1, 0, 2))

    for n in range(2):
        for name in "qkv":
            w = a[f"L{n}_attn_W{name}"].reshape(D, D).T
            b = a[f"L{n}_attn_b{name}"].reshape(D)
            if name == "v":
                out[f"wv{n}"], out[f"bv{n}"] = tiles(w), b.reshape(1, D)
                continue
            out[f"w{name}{n}"] = tiles(w)
            out[f"b{name}{n}"] = np.ascontiguousarray(b.reshape(2, P).T)
    out["fw"] = tiles(a["L0_ffn_weight"].T)
    ang = 2 * np.pi * ((np.outer(np.arange(D), np.arange(D))) % D) / D
    out["cs"] = np.ascontiguousarray(np.stack([tiles(m.astype(f)) for m in (np.cos(ang), np.sin(ang), -np.sin(ang))], 1))
    out["wri"] = np.ascontiguousarray(np.stack([tiles(a["L1_ffn_w_freq_real"]), tiles(a["L1_ffn_w_freq_imag"])], 1))
    out["bf"] = a["L1_ffn_bias"].reshape(1, D)
    return {k: np.ascontiguousarray(v) for k, v in out.items()}


def kernel(**inputs):
    import concourse.bacc as bacc
    from concourse.bass_utils import run_bass_kernel_spmd

    nc = bacc.Bacc("TRN2", target_bir_lowering=False, num_devices=1)
    arrays = host_arrays(inputs)
    t = {name: nc.dram_tensor(f"in_{name}", a.shape, mybir.dt.from_np(a.dtype), kind="ExternalInput").ap()
         for name, a in arrays.items()}
    t["out"] = nc.dram_tensor("out", (NB, L, D), F32, kind="ExternalOutput").ap()
    build(nc, t)
    r = run_bass_kernel_spmd(nc, [{f"in_{k}": v for k, v in arrays.items()}], core_ids=[0])
    return r.results[0]["out"]
```

```python
from contextlib import ExitStack

import numpy as np
import concourse.bass as bass
from concourse import mybir

F32 = mybir.dt.float32
BF16 = mybir.dt.bfloat16
I32 = mybir.dt.int32
ALU = mybir.AluOpType
ACT = mybir.ActivationFunctionType
AX = mybir.AxisListType

P = 128
NB, L, D = 16, 256, 256
NT = L // P
NK = D // P
H, HD = 16, 16
J = 4
G = H // J
VW = HD + 1
SLOT = 32
ONE = HD
Q_PARTS = (0, 1, 2, 0, 1, 0)
K_PARTS = (0, 0, 0, 1, 1, 2)
RUNS = ((0, 3), (3, 5), (5, 6))
STACK = len(Q_PARTS) * HD
SHIFT = 2
FULL = STACK + SHIFT
M = 128
V, NFFT = 64, 64
NFR = L // NFFT + 1
NFQ = NFFT // 2 + 1
PAIRS = NB * NFR // 2
DE = 179
DS = D - DE
EPS = 1e-5
ITERS = 6
U, NU = 2, 4
EW = P + HD
NEG = -1e30


def build(nc, t):
    ctx = ExitStack()
    with ctx:
        def sb(name, shape, dt=F32, where=None):
            return (where or ctx).enter_context(nc.sbuf_tensor(name, shape, dt))

        def sem(name):
            return ctx.enter_context(nc.semaphore(name))

        def scratch(name, shape, dt=F32):
            return nc.dram_tensor(name, shape, dt, kind="Internal").ap()

        k2_dram = scratch("k2_scratch", [NB, P, H * M])
        tok_parts = [scratch(f"tok_parts{n}", [NB, 2, 3, P, 2, L], BF16) for n in range(2)]
        lm_parts = scratch("lm_parts", [NB, 2, 3, P, 2, M], BF16)
        shift0 = scratch("shift0", [NB, SHIFT, 3, H, P], BF16)
        shift1 = scratch("shift1", [NB, SHIFT, NT, H, P], BF16)

        h = sb("h", [P, NB * NT, D])
        ident = sb("ident", [P, P])
        half = sb("half", [P, 4])
        passed = sb("passed", [P, 4])
        wq = [sb(f"wq{n}", [P, NK, D]) for n in range(2)]
        wk = [sb(f"wk{n}", [P, NK, D]) for n in range(2)]
        wv = [sb(f"wv{n}", [P, NK, D]) for n in range(2)]
        bq = [sb(f"bq{n}", [P, 2]) for n in range(2)]
        bk = [sb(f"bk{n}", [P, 2]) for n in range(2)]
        bv = [sb(f"bv{n}", [P, D]) for n in range(2)]
        wt = sb("wt", [P, NK, D])
        wf = sb("wf", [P, NK, D])
        bf = sb("bf", [P, D])
        mask = sb("mask", [P, 2, 2 * P], BF16)
        identb = sb("identb", [P, P], BF16)
        minv = sb("minv", [P, 2])
        stats = sb("stats", [P, NT, 6])
        mv = sb("mv", [P, NT, 2])
        rstd = sb("rstd", [P, NT])
        y = sb("y", [P, NT, D])
        yT = sb("yT", [P, NK, L])

        ps = ctx.enter_context(nc.psum_tensor("ps", [P, 8, 512], F32))

        def bank(n, k=1):
            return ps[:, n, :] if k == 1 else ps[:, n:n + k, :]

        class Steps:

            def __init__(self, per):
                self.per, self.n = per, 0

            def next(self, b=0):
                self.n += 1
                return b * self.per + self.n

            def end(self):
                assert self.n == self.per, self.n

        with ExitStack() as tmp:
            ids_all = sb("ids_all", [V, NB * L], I32, tmp)
            ids_fr = sb("ids_fr", [NFFT, 2 * PAIRS], I32, tmp)
            iota_c = sb("iota_c", [V, 1], F32, tmp)
            iota_r = sb("iota_r", [NFFT, V], F32, tmp)
            TOKR = V + PAIRS + 1
            tok_l = sb("tok_l", [TOKR, NB * L], F32, tmp)
            tok_r = sb("tok_r", [TOKR, 2, D], F32, tmp)
            hot_fr = sb("hot_fr", [NFFT, PAIRS * 2, V], F32, tmp)
            dft = sb("dft", [NFFT, 2, NFQ], F32, tmp)
            dftw = sb("dftw", [NFFT, 2 * NFQ], F32, tmp)
            window = sb("window", [NFFT, 1], F32, tmp)
            sq = sb("sq", [P, PAIRS, 2 * NFQ], F32, tmp)
            mag = sb("mag", [P, PAIRS, NFQ], F32, tmp)
            live = sb("live", [P, PAIRS, NFQ], F32, tmp)
            wp = sb("wp", [P, NFQ, DS], F32, tmp)
            mask32 = sb("mask32", [P, 2, 2 * P], F32, tmp)
            fw = sb("fw", [P, NK, D], F32, tmp)
            habs = sb("habs", [P, 1], F32, tmp)
            hsum = sb("hsum", [P, 1], F32, tmp)
            hs = sb("hs", [P, 3], F32, tmp)
            neg = sb("neg", [P, NK, D], F32, tmp)
            cs = sb("cs", [P, 3, NK, D], F32, tmp)
            wri = sb("wri", [P, 2, NK, D], F32, tmp)
            prT = sb("prT", [P, 2, NK, D], F32, tmp)

            in_fr, in_ids, in_tok, in_fft, in_ffn, in_rest, zero_done = (sem(s) for s in (
                "in_fr", "in_ids", "in_tok", "in_fft", "in_ffn", "in_rest", "zero_done"))
            hot_fr_ready, hotT_ready, dft_ready = sem("hot_fr_ready"), sem("hotT_ready"), sem("dft_ready")
            spec_ready, sq_ready, m2_ready, mag_ready = (sem(s) for s in (
                "spec_ready", "sq_ready", "m2_ready", "mag_ready"))
            root_ready, proj_ps, proj_ready, tok_ps, tok_done = (sem(s) for s in (
                "root_ready", "proj_ps", "proj_ready", "tok_ps", "tok_done"))
            habs_ready, hsum_ready, ffn_step = sem("habs_ready"), sem("hsum_ready"), sem("ffn_step")
            pr_ps, pr_ready, wf_ps, wf_done = sem("pr_ps"), sem("pr_ready"), sem("wf_ps"), sem("wf_done")
            FPB = PAIRS // 8
            NTILE = NB * NT

            with nc.Block() as block:
                @block.sync
                def _(sp):
                    for dst, src in ((ids_fr[:], t["ids_fr"]), (iota_r[:], t["iota"].partition_broadcast(NFFT)),
                                     (dft[:], t["dft"]), (window[:], t["window"])):
                        sp.dma_start(dst, src).then_inc(in_fr, 16)
                    sp.dma_start(iota_c[:], t["iota_c"]).then_inc(in_ids, 16)
                    sp.dma_start(ids_all[:], t["ids"].partition_broadcast(V)).then_inc(in_ids, 16)
                    sp.wait_ge(zero_done, 1)
                    for dst, src in [(wp[:], t["wp"]), (tok_l[V:TOKR, :], t["interp"])] + \
                            [(tok_r[0:V, a, 0:DE], t["emb"]) for a in range(2)] + \
                            [(tok_r[TOKR - 1:TOKR, a, DE:D], t["proj_b"]) for a in range(2)]:
                        sp.dma_start(dst, src).then_inc(in_tok, 16)
                    for dst, src in ((ident[:], t["ident"]), (half[:], t["half"]),
                                     (mask32[:], t["mask"])):
                        sp.dma_start(dst, src).then_inc(in_rest, 16)
                    sp.wait_ge(in_rest, 16 * (3 + 6 * 2 + 1))

                @block.gpsimd
                def _(pool):
                    pool.wait_ge(habs_ready, 1)
                    pool.partition_all_reduce(hsum[:], habs[:], P, bass.bass_isa.ReduceOp.add).then_inc(hsum_ready, 1)

                @block.scalar
                def _(act):
                    act.dma_start(cs[:], t["cs"]).then_inc(in_fft, 16)
                    act.dma_start(wri[:], t["wri"]).then_inc(in_fft, 16)
                    act.dma_start(fw[:], t["fw"]).then_inc(in_ffn, 16)
                    for n in range(2):
                        for dst, name in ((wq, "wq"), (wk, "wk"), (wv, "wv"), (bq, "bq"), (bk, "bk")):
                            act.dma_start(dst[n][:], t[f"{name}{n}"]).then_inc(in_rest, 16)
                        act.dma_start(bv[n][:], t[f"bv{n}"].partition_broadcast(P)).then_inc(in_rest, 16)
                    act.dma_start(bf[:], t["bf"].partition_broadcast(P)).then_inc(in_rest, 16)
                    act.wait_ge(pr_ps, 1)
                    act.activation(prT[:], bank(0, 4).rearrange("p (a k) n -> p a k n", a=2)[:, :, :, 0:D],
                                   ACT.Copy).then_inc(pr_ready, 1)
                    for n in range(8):
                        act.wait_ge(spec_ready, n + 1)
                        act.activation(sq[:, n * FPB:(n + 1) * FPB, :],
                                       bank(n)[:, 0:FPB * 2 * NFQ].rearrange("p (a f) -> p a f", a=FPB),
                                       ACT.Square).then_inc(sq_ready, 1)
                    act.wait_ge(m2_ready, 1)
                    act.activation(mag[:], mag[:], ACT.Sqrt).then_inc(root_ready, 1)
                    act.wait_ge(wf_ps, 1)
                    act.activation(wf[:], bank(4, 2)[:, :, 0:D], ACT.Copy, scale=1.0 / D).then_inc(wf_done, 1)

                @block.vector
                def _(dve):
                    s = Steps(7)
                    dve.memset(tok_r[:], 0.0).then_inc(zero_done, 1)
                    dve.wait_ge(in_fr, 16 * 4)
                    dve.tensor_scalar(dftw[:], dft[:].rearrange("n a f -> n (a f)"), window[:, 0:1], None,
                                      ALU.mult).then_inc(dft_ready, 1)
                    for n in range(4):
                        frames = slice(n * PAIRS // 2, (n + 1) * PAIRS // 2)
                        dve.tensor_tensor(hot_fr[:, frames], ids_fr[:, frames].unsqueeze(2).to_broadcast([NFFT, PAIRS // 2, V]),
                                          iota_r[:].unsqueeze(1).to_broadcast([NFFT, PAIRS // 2, V]),
                                          ALU.is_equal).then_inc(hot_fr_ready, 1)
                    dve.wait_ge(in_ids, 16 * 2)
                    dve.tensor_scalar(tok_l[0:V, :], ids_all[:], iota_c[:, 0:1], None, ALU.is_equal).then_inc(hotT_ready, 1)
                    dve.wait_ge(in_ffn, 16)
                    dve.tensor_reduce(habs[:], fw[:].rearrange("p k n -> p (k n)"), axis=AX.X, op=ALU.add,
                                      apply_absolute_value=True).then_inc(habs_ready, 1)
                    dve.wait_ge(sq_ready, 8)
                    dve.tensor_tensor(mag[:], sq[:, :, 0:NFQ], sq[:, :, NFQ:2 * NFQ], ALU.add).then_inc(ffn_step, 1)
                    dve.wait_ge(ffn_step, s.next())
                    dve.tensor_scalar(live[:], mag[:], 0.0, None, ALU.is_gt).then_inc(ffn_step, 1)
                    dve.wait_ge(ffn_step, s.next())
                    dve.tensor_scalar(mag[:], mag[:], 1e-34, None, ALU.max).then_inc(m2_ready, 1)
                    dve.wait_ge(root_ready, 1)
                    dve.tensor_tensor(mag[:], mag[:], live[:], ALU.mult).then_inc(mag_ready, 1)
                    dve.wait_ge(proj_ps, 1)
                    dve.wait_ge(in_tok, 16 * 6)
                    dve.tensor_copy(tok_r[V:V + PAIRS, :, DE:D], bank(0, 2)[V:V + PAIRS, :, 0:DS]).then_inc(proj_ready, 1)
                    dve.wait_ge(hsum_ready, 1)
                    dve.tensor_scalar(hs[:, 0:1], hsum[:], 1.0 / (D * D), EPS, ALU.mult, ALU.max).then_inc(ffn_step, 1)
                    dve.wait_ge(ffn_step, s.next())
                    dve.tensor_scalar(hs[:, 1:2], hs[:, 0:1], 0.5, None, ALU.mult).then_inc(ffn_step, 1)
                    dve.wait_ge(ffn_step, s.next())
                    dve.tensor_scalar(hs[:, 2:3], hs[:, 0:1], -0.5, None, ALU.mult).then_inc(ffn_step, 1)
                    dve.wait_ge(ffn_step, s.next())
                    dve.tensor_scalar(wt[:], fw[:], hs[:, 1:2], hs[:, 0:1], ALU.is_gt, ALU.mult).then_inc(ffn_step, 1)
                    dve.wait_ge(ffn_step, s.next())
                    dve.tensor_scalar(neg[:], fw[:], hs[:, 2:3], hs[:, 0:1], ALU.is_lt, ALU.mult).then_inc(ffn_step, 1)
                    dve.wait_ge(ffn_step, s.next())
                    dve.tensor_tensor(wt[:], wt[:], neg[:], ALU.subtract)
                    dve.wait_ge(in_rest, 16 * (3 + 6 * 2 + 1))
                    dve.tensor_copy(mask[:], mask32[:])
                    dve.tensor_copy(identb[:], ident[:])
                    for n in range(NTILE // 4):
                        dve.wait_ge(tok_ps, n + 1)
                        b0 = 2 * (n % 2)
                        dve.tensor_copy(h[:, 4 * n:4 * n + 4, :].rearrange("p (a c) d -> p a (c d)", a=2),
                                        bank(4 + b0, 2)).then_inc(tok_done, 1)
                    s.end()

                @block.tensor
                def _(pe):
                    pe.wait_ge(in_fft, 32)
                    for a in range(2):
                        for o in range(NK):
                            cols = slice(o * P, o * P + P)
                            for k in range(NK):
                                pe.matmul(bank(2 * a + o)[:, 0:D], wri[:, a, k, cols], cs[:, 0, k, :],
                                          start=k == 0, stop=False)
                                last = pe.matmul(bank(2 * a + o)[:, 0:D], wri[:, 1 - a, k, cols],
                                                 cs[:, 1 + a, k, :], start=False, stop=k == NK - 1)
                    last.then_inc(pr_ps, 1)
                    pe.wait_ge(dft_ready, 1)
                    pe.wait_ge(pr_ready, 1)
                    for n in range(8):
                        if n % 2 == 0:
                            pe.wait_ge(hot_fr_ready, n // 2 + 1)
                        for i in range(FPB):
                            pair = n * FPB + i
                            last = pe.matmul(bank(n)[:, i * 2 * NFQ:(i + 1) * 2 * NFQ],
                                             hot_fr[:, 2 * pair:2 * pair + 2, :].rearrange("n a v -> n (a v)"),
                                             dftw[:], start=True, stop=True)
                        last.then_inc(spec_ready, 1)
                    pe.wait_ge(sq_ready, 8)
                    for o in range(NK):
                        cols = slice(o * P, o * P + P)
                        for k in range(NK):
                            pe.matmul(bank(4 + o)[:, 0:D], prT[:, 0, k, cols], cs[:, 0, k, :],
                                      start=k == 0, stop=False)
                            last = pe.matmul(bank(4 + o)[:, 0:D], prT[:, 1, k, cols], cs[:, 2, k, :],
                                             start=False, stop=k == NK - 1)
                    last.then_inc(wf_ps, 1)
                    pe.wait_ge(mag_ready, 1)
                    pe.wait_ge(in_tok, 16 * 6)
                    for a in range(2):
                        rows = slice(V * a, V * a + V)
                        for f in range(NFQ):
                            last = pe.matmul(bank(a)[V:V + PAIRS, 0:DS], mag[rows, :, f], wp[rows, f, :],
                                             start=f == 0, stop=f == NFQ - 1)
                    last.then_inc(proj_ps, 1)
                    pe.wait_ge(proj_ready, 1)
                    pe.wait_ge(hotT_ready, 1)
                    pe.wait_ge(wf_done, 1)
                    for n in range(NTILE // 4):
                        if n >= 2:
                            pe.wait_ge(tok_done, n - 1)
                        for i in range(4):
                            tile = 4 * n + i
                            out = bank(4 + 2 * (n % 2) + i // 2)[:, (i % 2) * D:(i % 2 + 1) * D]
                            last = pe.matmul(out, tok_l[:, tile * P:(tile + 1) * P], tok_r[:, tile // (NTILE // 2), :],
                                             start=True, stop=True)
                        last.then_inc(tok_ps, 1)

        vall = sb("vall", [P, NB, NT * H * VW])
        qstk = sb("qstk", [P, H, L], BF16)
        kstk = sb("kstk", [P, H, L], BF16)
        xT = sb("xT", [P, G, L])
        xden = sb("xden", [P, NT, H])
        xo = sb("xo", [P, NT, D])

        def ln_statistics(dve, b, q, chain, ready):
            for i in range(NT):
                dve.bn_stats(stats[:, i, :], h[:, b * NT + i, :]).then_inc(chain, 1)
            dve.wait_ge(chain, q * NT + NT)
            dve.tensor_copy(passed[:], half[:])
            for i in range(NT):
                dve.bn_aggr(mv[:, i, :], stats[:, i, :]).then_inc(ready, 1)

        def ln_rstd(pool, q, statistics, chain, ready):
            pool.wait_ge(statistics, q * NT + NT)
            pool.tensor_tensor(rstd[:], mv[:, :, 1], half[:, 2:4], ALU.add).then_inc(chain, 1)
            pool.wait_ge(chain, q + 1)
            pool.tensor_tensor(rstd[:], rstd[:], half[:, 0:2], ALU.pow).then_inc(ready, 1)

        def ln_scale(dve, b, q, rstd_ready, ready):
            dve.wait_ge(rstd_ready, q + 1)
            for i in range(NT):
                dve.tensor_scalar(y[:, i, :], h[:, b * NT + i, :], mv[:, i, 0:1], rstd[:, i:i + 1],
                                  ALU.subtract, ALU.mult).then_inc(ready, 1)

        def transpose_y(pe, ready):
            for k in range(NK):
                for i in range(NT):
                    last = pe.transpose(bank(0)[:, k * L + i * P:k * L + (i + 1) * P], y[:, i, k * P:(k + 1) * P],
                                        ident[:])
            last.then_inc(ready, 1)

        def project_features(pe, out, w):
            for a in range(2):
                for k in range(NK):
                    last = pe.matmul(bank(out)[:, a * L:(a + 1) * L], w[:, k, a * P:(a + 1) * P], yT[:, k, :],
                                     start=k == 0, stop=k == NK - 1)
            return last

        def project_tokens(pe, out, w):
            for i in range(NT):
                for k in range(NK):
                    last = pe.matmul(bank(out)[:, i * D:(i + 1) * D], yT[:, k, i * P:(i + 1) * P], w[:, k, :],
                                     start=k == 0, stop=k == NK - 1)
            return last

        def project(pe, n, vbank, ready):
            project_features(pe, 1, wq[n])
            project_features(pe, 2, wk[n]).then_inc(ready, 1)
            project_tokens(pe, vbank, wv[n]).then_inc(ready, 1)

        def copy_qk(act, n, q32, parts, done, which=(0, 1)):
            for a, bias in [((0, bq[n]), (1, bk[n]))[a] for a in which]:
                for c in range(2):
                    src = bank(1 + a)[:, c * L:(c + 1) * L]
                    act.activation(q32[:, a, c, :], src, ACT.Identity, bias=bias[:, c:c + 1])
                    act.activation(parts[:, a, 0, c, :], src, ACT.Identity, bias=bias[:, c:c + 1]).then_inc(done, 1)

        def split_qk(dve, q, q32, parts, rest, ready, chain, done):
            dve.wait_ge(ready, q * 4 + 4)
            dve.tensor_tensor(rest[:], q32[:], parts[:, :, 0], ALU.subtract)
            dve.tensor_tensor(parts[:, :, 1], q32[:], parts[:, :, 0], ALU.subtract).then_inc(chain, 1)
            dve.wait_ge(chain, q + 1)
            dve.tensor_tensor(parts[:, :, 2], rest[:], parts[:, :, 1], ALU.subtract).then_inc(done, 1)

        def store_parts(sp, dram, tile, stored):
            sp.dma_start(dram.rearrange("a x p c l -> p (a x) (c l)"), tile.rearrange("p a x c l -> p (a x) (c l)"))\
              .then_inc(stored, 16)

        def load_stack(sp, dram, stack, which, loaded):
            for first, end in RUNS:
                src = dram[which[first]:which[end - 1] + 1].rearrange("x (d g) c l -> x d (g c l)", d=HD)
                if which[first] == which[end - 1] and end > first + 1:
                    src = src.to_broadcast([end - first, HD, src.shape[2]])
                else:
                    src = src.rearrange("x d n -> (x d) n")
                sp.dma_start(stack[first * HD:end * HD].rearrange("p h l -> p (h l)"), src).then_inc(loaded, 16)

        def heads_to_tokens(pe, first, ready):
            for i in range(NT):
                for g in range(G):
                    last = pe.transpose(bank(first + i)[:, g * P:(g + 1) * P], xT[:, g, i * P:(i + 1) * P], ident[:])
            last.then_inc(ready, 1)

        def attention_out(dve, b, first, xo_ps, chain, done):
            dve.wait_ge(xo_ps, b + 1)
            out = bank(first, 2).rearrange("p t (h s) -> p t h s", s=SLOT)
            dve.reciprocal(xden[:], out[:, :, :, ONE]).then_inc(chain, 1)
            dve.wait_ge(chain, b * 2 + 1)
            dve.tensor_tensor(xo[:].rearrange("p t (h d) -> p t h d", d=HD), out[:, :, :, 0:HD],
                              xden[:].unsqueeze(3).to_broadcast([P, NT, H, HD]), ALU.mult).then_inc(chain, 1)
            dve.wait_ge(chain, b * 2 + 2)
            rows = bass.ds(b * NT, NT)
            dve.tensor_tensor(h[:, rows, :], h[:, rows, :], xo[:], ALU.add).then_inc(done, 1)

        def heads(ap, width=HD):
            return ap.rearrange("p (h w) -> p h w", w=width)

        with ExitStack() as tmp:
            q32 = sb("q32a", [P, 2, 2, L], F32, tmp)
            parts = sb("partsa", [P, 2, 3, 2, L], BF16, tmp)
            rest = sb("resta", [P, 2, 2, L], F32, tmp)
            lm32 = sb("lm32", [P, 2, 2, M], F32, tmp)
            lmrest = sb("lmrest", [P, 2, 2, M], F32, tmp)
            lmparts = sb("lmparts", [P, 2, 3, 2, M], BF16, tmp)
            lmstk = sb("lmstk", [P, 2, H, M], BF16, tmp)
            nmax = sb("nmax", [P, H], F32, tmp)
            nbias = sb("nbias", [P, H], F32, tmp)
            rsum = sb("rsum", [P, H], F32, tmp)
            rinv = sb("rinv", [P, H], F32, tmp)
            expo = sb("expo", [P, H, M], F32, tmp)
            k2 = sb("k2", [P, H, M], F32, tmp)
            cmax = sb("cmax", [P, NB], F32, tmp)
            dmax = sb("dmax", [P, P], F32, tmp)
            msum = sb("msum", [P, 1], F32, tmp)
            ones = sb("ones", [P, P], F32, tmp)
            names = ("ln_stat", "ln_rstd_done", "y_done", "ln_step", "pow_step", "yT_ps", "yT_done", "qkv_ps", "qk_done",
                     "v_done", "split_step", "parts_done", "pair_step", "lmparts_done", "parts_stored", "lm_stored",
                     "lm_loaded", "s_ps", "max_step", "max_done", "exp_done", "rinv_done", "k2_done", "k2_stored",
                     "col_ps", "col_done", "ones_done", "dmax_done", "all_ps")
            (ln_stat, ln_rstd_done, y_done, ln_step, pow_step, yT_ps, yT_done, qkv_ps, qk_done, v_done, split_step,
             parts_done, pair_step, lmparts_done, parts_stored, lm_stored, lm_loaded, s_ps, max_step, max_done,
             exp_done, rinv_done, k2_done, k2_stored, col_ps, col_done, ones_done, dmax_done,
             all_ps) = (sem("lm_" + n) for n in names)

            def pipeline(eng, step):
                for b in range(-3, 1):
                    step(b)
                with eng.Fori(1, NB - 3) as b:
                    step(b)
                for b in range(NB - 3, NB + 1):
                    step(b)

            def has(c):
                return not isinstance(c, int) or 0 <= c < NB

            with nc.Block() as block:
                @block.sync
                def _(sp):
                    sp.sem_inc(k2_stored, 16)
                    sp.sem_inc(parts_stored, 16)
                    sp.sem_inc(lm_stored, 16)

                    def step(b):
                        if has(b + 1):
                            c = b + 1
                            sp.wait_ge(parts_done, c + 1)
                            store_parts(sp, tok_parts[0][c], parts[:], parts_stored)
                            sp.wait_ge(lmparts_done, c + 1)
                            store_parts(sp, lm_parts[c], lmparts[:], lm_stored)
                            if has(b):
                                sp.wait_ge(s_ps, c)
                            sp.wait_ge(lm_stored, c * 16 + 32)
                            for a, which in ((0, Q_PARTS), (1, K_PARTS)):
                                load_stack(sp, lm_parts[c, a], lmstk[:, a], which, lm_loaded)
                        if has(b):
                            sp.wait_ge(k2_done, b + 1)
                            sp.dma_start(k2_dram[b], k2[:].rearrange("p h m -> p (h m)")).then_inc(k2_stored, 16)

                    pipeline(sp, step)
                    sp.wait_ge(k2_stored, 16 * NB + 16)
                    sp.wait_ge(parts_stored, 16 * NB + 16)

                @block.gpsimd
                def _(pool):
                    def landmarks(c):
                        pool.wait_ge(qk_done, c * 4 + 4)
                        pair = q32[:].rearrange("p a c (m two) -> p (a c) m two", two=2)
                        flat = [x.rearrange("p a c m -> p (a c) m") for x in (lm32[:], lmrest[:])]
                        part = [lmparts[:, :, n] for n in range(3)]
                        pool.tensor_tensor(flat[0], pair[:, :, :, 0], pair[:, :, :, 1], ALU.add).then_inc(pair_step, 1)
                        pool.wait_ge(lm_stored, c * 16 + 16)
                        for a in range(2):
                            pool.tensor_tensor(part[0][:, a], pair[:, 2 * a:2 * a + 2, :, 0], pair[:, 2 * a:2 * a + 2, :, 1],
                                               ALU.add).then_inc(pair_step, 1)
                        pool.wait_ge(pair_step, c * 5 + 3)
                        pool.tensor_tensor(lmrest[:], lm32[:], part[0], ALU.subtract).then_inc(pair_step, 1)
                        pool.tensor_tensor(part[1], lm32[:], part[0], ALU.subtract).then_inc(pair_step, 1)
                        pool.wait_ge(pair_step, c * 5 + 5)
                        pool.tensor_tensor(part[2], lmrest[:], part[1], ALU.subtract).then_inc(lmparts_done, 1)

                    def step(b):
                        if has(b + 3):
                            ln_rstd(pool, b + 3, ln_stat, pow_step, ln_rstd_done)
                        if has(b + 1):
                            landmarks(b + 1)
                        if has(b):
                            pool.wait_ge(rinv_done, b + 1)
                            pool.wait_ge(k2_stored, b * 16 + 16)
                            pool.tensor_tensor(k2[:], expo[:], rinv[:].unsqueeze(2).to_broadcast([P, H, M]),
                                               ALU.mult).then_inc(k2_done, 1)

                    pipeline(pool, step)

                @block.scalar
                def _(act):
                    def step(b):
                        if has(b + 1):
                            act.wait_ge(qkv_ps, (b + 1) * 2 + 1)
                            act.wait_ge(parts_stored, (b + 1) * 16 + 16)
                            if has(b):
                                act.wait_ge(parts_done, b + 1)
                                act.wait_ge(lmparts_done, b + 1)
                            copy_qk(act, 0, q32, parts, qk_done)
                        if has(b + 2):
                            act.wait_ge(yT_ps, b + 3)
                            act.activation(yT[:].rearrange("p k m -> p (k m)"), bank(0), ACT.Copy).then_inc(yT_done, 1)
                        if has(b):
                            act.wait_ge(max_done, b + 1)
                            if has(b - 1):
                                act.wait_ge(k2_done, b)
                                act.wait_ge(col_ps, b)
                            for i in range(H):
                                act.activation(expo[:, i, :], bank(4 + i // J)[:, (i % J) * M:(i % J + 1) * M], ACT.Exp,
                                               bias=nbias[:, i:i + 1], scale=0.0625,
                                               accum_out=rsum[:, i:i + 1]).then_inc(exp_done, 1)

                    pipeline(act, step)

                @block.vector
                def _(dve):
                    dve.memset(ones[:], 1.0).then_inc(ones_done, 1)
                    dve.memset(vall[:].rearrange("p b (n w) -> p (b n) w", w=VW)[:, :, HD:VW], 1.0).then_inc(ones_done, 1)
                    dve.wait_ge(ones_done, 2)

                    def step(b):
                        if has(b + 3):
                            ln_statistics(dve, b + 3, b + 3, ln_step, ln_stat)
                        if has(b + 1):
                            dve.wait_ge(qkv_ps, (b + 1) * 2 + 2)
                            vb = vall[:, b + 1, :].rearrange("p (t h w) -> p t h w", t=NT, w=VW)
                            for i in range(NT):
                                dve.tensor_tensor(vb[:, i, :, 0:HD], heads(bank(3)[:, i * D:(i + 1) * D]), heads(bv[0][:]),
                                                  ALU.add).then_inc(v_done, 1)
                        if has(b - 1):
                            dve.wait_ge(col_ps, b)
                            dve.tensor_reduce(cmax[:, bass.ds(b - 1, 1)], bank(0), axis=AX.X,
                                              op=ALU.max).then_inc(col_done, 1)
                        if has(b + 1):
                            split_qk(dve, b + 1, q32, parts, rest, qk_done, split_step, parts_done)
                        if has(b):
                            dve.wait_ge(s_ps, b + 1)
                            dve.tensor_reduce(nmax[:], bank(4, 4).rearrange("p j (g m) -> p (j g) m", m=M), axis=AX.X,
                                              op=ALU.max, negate=True).then_inc(max_step, 1)
                            dve.wait_ge(max_step, b + 1)
                            dve.tensor_scalar(nbias[:], nmax[:], 0.0625, None, ALU.mult).then_inc(max_done, 1)
                        if has(b + 3):
                            if has(b + 2):
                                dve.wait_ge(yT_ps, b + 3)
                            ln_scale(dve, b + 3, b + 3, ln_rstd_done, y_done)
                        if has(b):
                            dve.wait_ge(exp_done, b * H + H)
                            dve.reciprocal(rinv[:], rsum[:]).then_inc(rinv_done, 1)

                    pipeline(dve, step)
                    dve.wait_ge(col_done, NB)
                    dve.tensor_reduce(msum[:], cmax[:], axis=AX.X, op=ALU.max).then_inc(max_step, 1)
                    dve.wait_ge(max_step, NB + 1)
                    dve.tensor_scalar(dmax[:], ident[:], msum[:, 0:1], None, ALU.mult).then_inc(dmax_done, 1)
                    dve.wait_ge(all_ps, 1)
                    dve.tensor_reduce(msum[:], bank(1)[:, 0:P], axis=AX.X, op=ALU.max).then_inc(max_step, 1)
                    dve.wait_ge(max_step, NB + 2)
                    dve.reciprocal(minv[:, 1:2], msum[:]).then_inc(max_step, 1)
                    dve.wait_ge(max_step, NB + 3)
                    dve.tensor_scalar(minv[:, 0:1], minv[:, 1:2], -1.0, None, ALU.mult)

                @block.tensor
                def _(pe):
                    pe.wait_ge(ones_done, 2)

                    def step(b):
                        if has(b + 1):
                            pe.wait_ge(yT_done, b + 2)
                            if has(b):
                                pe.wait_ge(qk_done, (b + 1) * 4)
                                pe.wait_ge(v_done, (b + 1) * NT)
                            project(pe, 0, 3, qkv_ps)
                        if has(b - 1):
                            pe.wait_ge(rinv_done, b)
                            if has(b - 2):
                                pe.wait_ge(col_done, b - 1)
                            for i in range(H):
                                last = pe.matmul(bank(0)[32 * (i // J):32 * (i // J + 1), (i % J) * M:(i % J + 1) * M],
                                                 rinv[:, i:i + 1].to_broadcast([P, 32]), expo[:, i, :], start=True, stop=True)
                            last.then_inc(col_ps, 1)
                        if has(b):
                            pe.wait_ge(lm_loaded, (b + 1) * (16 * 2 * len(RUNS)))
                            if has(b - 1):
                                pe.wait_ge(exp_done, b * H)
                            for i in range(H):
                                last = pe.matmul(bank(4 + i // J)[:, (i % J) * M:(i % J + 1) * M], lmstk[0:STACK, 0, i, :],
                                                 lmstk[0:STACK, 1, i, :], start=True, stop=True)
                            last.then_inc(s_ps, 1)
                        if has(b + 2):
                            pe.wait_ge(y_done, (b + 3) * NT)
                            if has(b - 1):
                                pe.wait_ge(col_done, b)
                            transpose_y(pe, yT_ps)

                    pipeline(pe, step)
                    pe.wait_ge(dmax_done, 1)
                    pe.matmul(bank(1)[:, 0:P], ones[:], dmax[:], start=True, stop=True).then_inc(all_ps, 1)

        with ExitStack() as tmp:
            va = sb("va", [P, NT, H, VW], F32, tmp)
            qlstk = sb("qlstk", [P, H, M], BF16, tmp)
            klstk = sb("klstk", [P, H, M], BF16, tmp)
            nmax = sb("nmaxn", [P, 3, H], F32, tmp)
            nparts = sb("nparts", [P, SHIFT, 3, H], BF16, tmp)
            nrow = sb("nrow", [SHIFT * 3 * H, P], BF16, tmp)
            p3 = sb("p3", [P, J, L], F32, tmp)
            p1 = [sb(f"p1{x}", [P, H, L], F32, tmp) for x in range(2)]
            yn = [sb(f"yn{x}", [P, H, HD], F32, tmp) for x in range(2)]
            den = sb("den", [P, H], F32, tmp)
            k2 = [sb(f"k2n{x}", [P, H, M], F32, tmp) for x in range(2)]
            k2T = sb("k2T", [P, H, M], F32, tmp)
            ey = sb("ey", [P, NU, U, EW], F32, tmp)
            gu = sb("gu", [P, NU, U, EW], F32, tmp)
            e2 = sb("e2", [P, NU, U, EW], F32, tmp)
            ya = sb("ya", [P, NU, U, HD], F32, tmp)
            zc = sb("zc", [P, H, SLOT], F32, tmp)
            names = ("stk_loaded", "k2_loaded", "s_ps", "nmax_done", "npart_step", "nparts_done", "nrow_ps", "nrow_done",
                     "nrow_stored", "shift_loaded", "st_ps", "exp_done", "yn_ps", "yn_step", "yn_done",
                     "k2T_ps", "k2T_done", "kk_ps", "e0_done", "sq_ps", "sq_act", "sq_dve", "cu_ps", "cu_act",
                     "cu_dve", "thin_ps", "thin_done", "z_ps", "z_done", "x_ps", "xT_done", "xo_ps", "out_step",
                     "h_done", "clear", "ya_done")
            (stk_loaded, k2_loaded, s_ps, nmax_done, npart_step, nparts_done, nrow_ps, nrow_done, nrow_stored,
             shift_loaded, st_ps, exp_done, yn_ps, yn_step, yn_done, k2T_ps, k2T_done, kk_ps, e0_done, sq_ps,
             sq_act, sq_dve, cu_ps, cu_act, cu_dve, thin_ps, thin_done, z_ps, z_done, x_ps, xT_done, xo_ps,
             out_step, h_done, clear, ya_done) = (sem("ny_" + n) for n in names)
            LAST = ITERS - 1
            NSTK = 16 * (4 * len(RUNS) + 1)

            def prod(a):
                return bank(4 + a).rearrange("p (i n) -> p i n", i=U)

            def unit(half_, a):
                return slice((half_ * NU + a) * U, (half_ * NU + a + 1) * U)

            def turn(b, half_, k=0):
                return (b * 2 + half_) * (ITERS * NU) + k * NU

            def cube(b, half_, k=0):
                return (b * 2 + half_) * (ITERS * NU) + k * NU

            def batches(eng, ahead_first, both, output):
                ahead_first()
                both(0, 0, False, True)
                with eng.Fori(0, NB // 2 - 1) as pair:
                    both(pair * 2 + 1, 1, True, True)
                    both(pair * 2 + 2, 0, True, True)
                both(NB - 1, 1, True, False)
                output(NB - 1, 1)

            with nc.Block() as block:
                @block.sync
                def _(sp):
                    def load(b):
                        load_stack(sp, tok_parts[0][b, 0], qstk, Q_PARTS, stk_loaded)
                        load_stack(sp, tok_parts[0][b, 1], kstk, K_PARTS, stk_loaded)
                        load_stack(sp, lm_parts[b, 0], qlstk, Q_PARTS, stk_loaded)
                        load_stack(sp, lm_parts[b, 1], klstk, K_PARTS, stk_loaded)
                        sp.dma_start(va[:].rearrange("p t h w -> p (t h w)"), vall[:, b, :]).then_inc(stk_loaded, 16)

                    def load_k2(b, x):
                        sp.dma_start(k2[x][:].rearrange("p h m -> p (h m)"), k2_dram[b]).then_inc(k2_loaded, 16)

                    def shifts(b):
                        sp.wait_ge(nrow_done, b + 1)
                        sp.dma_start(shift0[b].rearrange("x c h l -> (x c h) l"), nrow[:]).then_inc(nrow_stored, 16)
                        sp.wait_ge(nrow_stored, b * 16 + 16)
                        sp.dma_start(qlstk[STACK:FULL], shift0[b, :, 0]).then_inc(shift_loaded, 16)
                        for i in range(NT):
                            sp.dma_start(qstk[STACK:FULL, :, i * P:(i + 1) * P], shift0[b, :, 1 + i]).then_inc(shift_loaded, 16)

                    def first():
                        load(0)
                        load_k2(0, 0)
                        shifts(0)

                    def both(b, x, past, more):
                        if more:
                            sp.wait_ge(yn_ps, (b + 1) * G)
                            load(b + 1)
                            if past:
                                sp.wait_ge(z_ps, b)
                            load_k2(b + 1, 1 - x)
                            shifts(b + 1)

                    batches(sp, first, both, lambda b, x: None)
                    sp.wait_ge(stk_loaded, NSTK * NB)
                    sp.wait_ge(k2_loaded, 16 * NB)

                @block.gpsimd
                def _(pool):
                    def both(b, x, past, more):
                        for half_ in range(2):
                            for k in range(ITERS):
                                for a in range(NU):
                                    pool.wait_ge(sq_act, turn(b, half_, k) + a + 1)
                                    pool.tensor_tensor(ya[:, a], ey[:, a, :, P:EW], e2[:, a, :, P:EW],
                                                       ALU.add).then_inc(ya_done, 1)

                    batches(pool, lambda: None, both, lambda b, x: None)

                @block.scalar
                def _(act):
                    def shift_rows(b):
                        act.wait_ge(nrow_ps, b + 1)
                        act.activation(nrow[:], bank(0)[0:SHIFT * 3 * H, 0:P // 2].bitcast(BF16), ACT.Copy).then_inc(nrow_done, 1)

                    def exponentials3(b, g):
                        act.wait_ge(st_ps, b * G + g + 1)
                        act.activation(p3[:], bank(0, 4)[:, :, 0:L], ACT.Exp, scale=0.125).then_inc(exp_done, 1)

                    def exponentials1(b, x, g):
                        act.activation(p1[x][:, g * J:(g + 1) * J, :], bank(0, 4)[:, :, L:2 * L], ACT.Exp,
                                       scale=0.125).then_inc(exp_done, 1)

                    def copy_k2T(b):
                        act.wait_ge(k2T_ps, b + 1)
                        act.activation(k2T[:], bank(0, 4).rearrange("p a (i m) -> p (a i) m", m=M), ACT.Copy).then_inc(k2T_done, 1)

                    def copy_out(b):
                        act.wait_ge(x_ps, b + 1)
                        act.activation(xT[:], bank(0, 2).rearrange("p a (i n) -> p (a i) n", i=2), ACT.Copy).then_inc(xT_done, 1)

                    def first():
                        shift_rows(0)
                        for g in range(G):
                            exponentials3(0, g)
                            exponentials1(0, 0, g)
                        copy_k2T(0)

                    def both(b, x, past, more):
                        for half_ in range(2):
                            for k in range(ITERS):
                                for a in range(NU):
                                    act.wait_ge(sq_ps, turn(b, half_, k) + a + 1)
                                    act.activation(e2[:, a], prod(a)[:, :, 0:EW], ACT.Copy).then_inc(sq_act, 1)
                                if past and half_ == 0 and k == 0:
                                    copy_out(b - 1)
                                if more and half_ == 0 and k == LAST:
                                    shift_rows(b + 1)
                                if more and half_ == 1 and k < G:
                                    exponentials3(b + 1, k)
                                if more and half_ == 1 and k == LAST:
                                    copy_k2T(b + 1)
                                if k < LAST:
                                    for a in range(NU):
                                        act.wait_ge(ya_done, turn(b, half_, k) + a + 1)
                                        act.wait_ge(cu_ps, cube(b, half_, k) + a + 1)
                                        act.activation(ey[:, a], prod(a)[:, :, 0:EW], ACT.Copy, scale=0.25).then_inc(cu_act, 1)
                                if more and half_ == 1 and k < G:
                                    exponentials1(b + 1, 1 - x, k)

                    batches(act, first, both, lambda b, x: copy_out(b))

                @block.vector
                def _(dve):
                    def maxima3(b, g):
                        dve.wait_ge(s_ps, b * G + g + 1)
                        dve.tensor_reduce(nmax[:, 0, g * J:(g + 1) * J], bank(0, 4)[:, :, 0:L], axis=AX.X, op=ALU.max,
                                          negate=True)

                    def maxima1(b, g):
                        cols = nmax[:, :, g * J:(g + 1) * J].rearrange("p c j -> p j c")
                        dve.tensor_reduce(cols[:, :, 1:3], bank(0, 4)[:, :, L:2 * L].rearrange("p j (c n) -> p j c n", c=2),
                                          axis=AX.X, op=ALU.max, negate=True).then_inc(nmax_done, 1)

                    def maxima_parts(b):
                        dve.wait_ge(nmax_done, b * G + G)
                        dve.tensor_copy(nparts[:, 0], nmax[:]).then_inc(npart_step, 1)
                        dve.wait_ge(npart_step, b + 1)
                        dve.tensor_tensor(nparts[:, 1], nmax[:], nparts[:, 0], ALU.subtract).then_inc(nparts_done, 1)

                    def norm_y(b, x, g):
                        dve.wait_ge(yn_ps, b * G + g + 1)
                        out = heads(bank(1)[:, 0:J * SLOT], SLOT)
                        dve.reciprocal(den[:, g * J:(g + 1) * J], out[:, :, ONE]).then_inc(yn_step, 1)
                        dve.wait_ge(yn_step, b * G + g + 1)
                        dve.tensor_tensor(yn[x][:, g * J:(g + 1) * J, :], out[:, :, 0:HD],
                                          den[:, g * J:(g + 1) * J].unsqueeze(2).to_broadcast([P, J, HD]),
                                          ALU.mult).then_inc(yn_done, 1)

                    def scale_z(b):
                        dve.wait_ge(z_ps, b + 1)
                        dve.tensor_scalar(zc[:, :, 0:HD], heads(bank(0)[:, 0:H * HD]), minv[:, 1:2], None,
                                          ALU.mult).then_inc(z_done, 1)

                    def first():
                        dve.memset(kstk[STACK:P], 1.0)
                        dve.memset(klstk[STACK:P], 1.0)
                        dve.memset(zc[:], 0.0).then_inc(clear, 1)
                        dve.wait_ge(clear, 1)
                        dve.memset(zc[:, :, ONE:ONE + 1], 1.0).then_inc(clear, 1)
                        for g in range(G):
                            maxima3(0, g)
                            maxima1(0, g)
                        maxima_parts(0)
                        for g in range(G):
                            norm_y(0, 0, g)

                    def both(b, x, past, more):
                        for half_ in range(2):
                            for a in range(NU):
                                dve.wait_ge(kk_ps, (b * 2 + half_) * NU + a + 1)
                                dve.scalar_tensor_tensor(ey[:, a, :, 0:P], prod(a)[:, :, 0:P], minv[:, 0:1],
                                                         ident[:].unsqueeze(1).to_broadcast([P, U, P]), ALU.mult, ALU.add)
                                dve.tensor_copy(ey[:, a, :, P:EW], yn[x][:, unit(half_, a), :]).then_inc(e0_done, 1)
                            if past and half_ == 0:
                                scale_z(b - 1)
                            for k in range(ITERS):
                                for a in range(NU):
                                    dve.wait_ge(sq_act, turn(b, half_, k) + a + 1)
                                    last = dve.scalar_tensor_tensor(gu[:, a, :, P:EW], e2[:, a, :, P:EW], 0.25,
                                                                    ey[:, a, :, P:EW], ALU.mult, ALU.add)
                                    if k < LAST:
                                        last = dve.scalar_tensor_tensor(gu[:, a, :, 0:P], ey[:, a, :, 0:P], 3.0,
                                                                        e2[:, a, :, 0:P], ALU.mult, ALU.add)
                                    last.then_inc(sq_dve, 1)
                                if more and half_ == 0 and 1 <= k <= G:
                                    maxima3(b + 1, k - 1)
                                if more and half_ == 1 and 1 <= k <= G:
                                    norm_y(b + 1, 1 - x, k - 1)
                                for a in range(NU):
                                    dve.wait_ge(ya_done, turn(b, half_, k) + a + 1)
                                    if k < LAST:
                                        dve.wait_ge(cu_act, (b * 2 + half_) * (LAST * NU) + k * NU + a + 1)
                                        dve.scalar_tensor_tensor(ey[:, a, :, P:EW], ey[:, a, :, P:EW], 4.0, ya[:, a],
                                                                 ALU.mult, ALU.add).then_inc(cu_dve, 1)
                                    else:
                                        dve.wait_ge(cu_ps, cube(b, half_, k) + a + 1)
                                        dve.tensor_tensor(yn[x][:, unit(half_, a), :], prod(a)[:, :, P:EW], ya[:, a],
                                                          ALU.add).then_inc(thin_done, 1)
                                if past and half_ == 0 and k == 0:
                                    attention_out(dve, b - 1, 2, xo_ps, out_step, h_done)
                                if more and half_ == 0 and 1 <= k <= G:
                                    maxima1(b + 1, k - 1)
                                if more and half_ == 0 and k == G:
                                    maxima_parts(b + 1)

                    def output(b, x):
                        scale_z(b)
                        attention_out(dve, b, 2, xo_ps, out_step, h_done)

                    batches(dve, first, both, output)

                @block.tensor
                def _(pe):
                    def logits(b, g, past=False):
                        if g > 0:
                            pe.wait_ge(nmax_done, b * G + g)
                        for j in range(J):
                            if j == 2 and g == 0 and past:
                                pe.wait_ge(h_done, b - 1)
                            head = g * J + j
                            pe.matmul(bank(j)[:, 0:L], qlstk[0:STACK, head, :], kstk[0:STACK, head, :], start=True, stop=True)
                            for i in range(NT):
                                last = pe.matmul(bank(j)[:, L + i * P:L + (i + 1) * P],
                                                 qstk[0:STACK, head, i * P:(i + 1) * P], klstk[0:STACK, head, :],
                                                 start=True, stop=True)
                        last.then_inc(s_ps, 1)

                    def maxima_to_rows(b):
                        pe.wait_ge(nparts_done, b + 1)
                        pe.transpose(bank(0)[0:SHIFT * 3 * H, 0:P // 2].bitcast(BF16),
                                     nparts[:].rearrange("p x c h -> p (x c h)"), identb[:]).then_inc(nrow_ps, 1)

                    def transposed_logits(b, g):
                        if g == 0:
                            pe.wait_ge(shift_loaded, (b + 1) * (16 * 3))
                            pe.wait_ge(nrow_done, b + 1)
                        else:
                            pe.wait_ge(exp_done, (b * G + g) * 2)
                        for j in (0, 2, 3, 1):
                            if j == 1 and g > 0:
                                pe.wait_ge(yn_done, b * G + g)
                            head = g * J + j
                            for i in range(NT):
                                pe.matmul(bank(j)[:, i * P:(i + 1) * P], kstk[0:FULL, head, i * P:(i + 1) * P],
                                          qlstk[0:FULL, head, :], start=True, stop=True)
                            last = pe.matmul(bank(j)[:, L:2 * L], klstk[0:FULL, head, :], qstk[0:FULL, head, :],
                                             start=True, stop=True)
                        last.then_inc(st_ps, 1)

                    def kernel3_values(b, g):
                        pe.wait_ge(exp_done, (b * G + g + 1) * 2)
                        for j in range(J):
                            for i in range(NT):
                                last = pe.matmul(bank(1)[:, j * SLOT:j * SLOT + VW], p3[:, j, i * P:(i + 1) * P],
                                                 va[:, i, g * J + j, :], start=i == 0, stop=i == NT - 1)
                        last.then_inc(yn_ps, 1)

                    def kernel2_transposed(b, x):
                        pe.wait_ge(k2_loaded, b * 16 + 16)
                        for i in range(H):
                            last = pe.transpose(bank(i // J)[:, (i % J) * M:(i % J + 1) * M], k2[x][:, i, :], ident[:])
                        last.then_inc(k2T_ps, 1)

                    def z_product(b, x):
                        pe.wait_ge(thin_done, (b + 1) * (2 * NU))
                        for i in range(H):
                            last = pe.matmul(bank(0)[:, i * HD:(i + 1) * HD], k2[x][:, i, :], yn[x][:, i, :],
                                             start=True, stop=True)
                        last.then_inc(z_ps, 1)

                    def x_product(b, x):
                        pe.wait_ge(z_done, b + 1)
                        for i in range(H):
                            g, j = i // J, i % J
                            last = pe.matmul(bank(g // 2)[SLOT * j:SLOT * (j + 1), (g % 2) * L:(g % 2 + 1) * L],
                                             zc[:, i, :], p1[x][:, i, :], start=True, stop=True)
                        last.then_inc(x_ps, 1)

                    def first():
                        pe.wait_ge(clear, 2)
                        pe.wait_ge(stk_loaded, NSTK)
                        for g in range(G):
                            logits(0, g)
                        maxima_to_rows(0)
                        for g in range(G):
                            transposed_logits(0, g)
                            kernel3_values(0, g)
                        pe.wait_ge(yn_done, G)
                        kernel2_transposed(0, 0)

                    def both(b, x, past, more):
                        for half_ in range(2):
                            if half_ == 0:
                                pe.wait_ge(k2T_done, b + 1)
                            for a in range(NU):
                                if half_ == 1 or past:
                                    pe.wait_ge(thin_done, (2 * b + half_) * NU - NU + a + 1)
                                for i in range(U):
                                    kT_h = k2T[:, (half_ * NU + a) * U + i, :]
                                    last = pe.matmul(prod(a)[:, i, 0:P], kT_h, kT_h, start=True, stop=True)
                                last.then_inc(kk_ps, 1)
                            if past and half_ == 0:
                                z_product(b - 1, 1 - x)
                            for k in range(ITERS):
                                for a in range(NU):
                                    if k == 0:
                                        pe.wait_ge(e0_done, (b * 2 + half_) * NU + a + 1)
                                    else:
                                        pe.wait_ge(cu_dve, (b * 2 + half_) * (LAST * NU) + (k - 1) * NU + a + 1)
                                    for i in range(U):
                                        last = pe.matmul(prod(a)[:, i, 0:EW], ey[:, a, i, 0:P], ey[:, a, i, :],
                                                         start=True, stop=True)
                                    last.then_inc(sq_ps, 1)
                                if past and half_ == 0 and k == 0:
                                    x_product(b - 1, 1 - x)
                                if more and half_ == 0 and 1 <= k <= G:
                                    if k == 1:
                                        pe.wait_ge(stk_loaded, (b + 2) * NSTK)
                                    logits(b + 1, k - 1, past)
                                if more and half_ == 0 and k == LAST:
                                    maxima_to_rows(b + 1)
                                if more and half_ == 1 and 1 <= k <= G:
                                    kernel3_values(b + 1, k - 1)
                                if more and half_ == 1 and k < G:
                                    transposed_logits(b + 1, k)
                                if more and half_ == 1 and k == LAST:
                                    pe.wait_ge(yn_done, (b + 2) * G)
                                    kernel2_transposed(b + 1, 1 - x)
                                for a in range(NU):
                                    pe.wait_ge(sq_dve, turn(b, half_, k) + a + 1)
                                    cols = slice(0 if k < LAST else P, EW)
                                    for i in range(U):
                                        last = pe.matmul(prod(a)[:, i, cols], e2[:, a, i, 0:P], gu[:, a, i, cols],
                                                         start=True, stop=True)
                                    last.then_inc(cu_ps, 1)
                                if past and half_ == 0 and k == 0:
                                    pe.wait_ge(xT_done, b)
                                    heads_to_tokens(pe, 2, xo_ps)

                    def output(b, x):
                        z_product(b, x)
                        x_product(b, x)
                        pe.wait_ge(xT_done, b + 1)
                        heads_to_tokens(pe, 2, xo_ps)

                    batches(pe, first, both, output)

        with ExitStack() as tmp:
            q32 = sb("q32b", [P, 2, 2, L], F32, tmp)
            parts = sb("partsb", [P, 2, 3, 2, L], BF16, tmp)
            rest = sb("restb", [P, 2, 2, L], F32, tmp)
            W3 = 3 * P
            PR = H // 2
            va = [sb(f"va1{x}", [P, NT, H, SLOT], F32, tmp) for x in range(2)]
            vst = sb("vst", [P, NT, D], F32, tmp)
            stacks = [(qstk, kstk), (sb("qstkb", [P, H, L], BF16, tmp), sb("kstkb", [P, H, L], BF16, tmp))]
            nmax = sb("nmax1", [P, 3, H], F32, tmp)
            npad = sb("npad", [P, P], BF16, tmp)
            nparts = npad[:, 0:SHIFT * NT * H].rearrange("p (x c h) -> p x c h", x=SHIFT, c=NT)
            nrow = sb("nrow1", [SHIFT * NT * H, P], BF16, tmp)
            pT = sb("pT", [P, 2, 2, W3], F32, tmp)
            res = sb("res", [P, NT, D], F32, tmp)
            names = ("ln_stat", "ln_rstd_done", "y_done", "ln_step", "pow_step", "yT_ps", "yT_done", "ffn_ps",
                     "ffn_done", "qkv_ps", "qk_done", "v_done", "split_step", "parts_done", "parts_stored",
                     "stk_loaded", "s_ps", "nmax_done", "npart_step", "nparts_done", "nrow_ps", "nrow_done",
                     "nrow_stored", "shift_loaded", "st_ps", "exp_done", "pv_ps", "xT_done", "xo_ps", "out_step",
                     "h_done", "clear", "four_ps", "bias_done", "res_done", "stored", "va_done")
            (ln_stat, ln_rstd_done, y_done, ln_step, pow_step, yT_ps, yT_done, ffn_ps, ffn_done, qkv_ps, qk_done,
             v_done, split_step, parts_done, parts_stored, stk_loaded, s_ps, nmax_done, npart_step, nparts_done,
             nrow_ps, nrow_done, nrow_stored, shift_loaded, st_ps, exp_done, pv_ps, xT_done, xo_ps, out_step,
             h_done, clear, four_ps, bias_done, res_done, stored, va_done) = (sem("tl_" + n) for n in names)
            NSTK1 = 16 * 2 * len(RUNS)

            def pipeline(eng, step):
                for b in range(-3, 1):
                    step(b, b % 2)
                with eng.Fori(0, NB // 2 - 2) as pair:
                    step(pair * 2 + 1, 1)
                    step(pair * 2 + 2, 0)
                for b in range(NB - 3, NB + 1):
                    step(b, b % 2)

            def has(c):
                return not isinstance(c, int) or 0 <= c < NB

            def layernorms(b):
                n = 3 * b + 4
                if isinstance(b, int):
                    n = sum(has(s + 2) + has(s - 1) + has(s + 3) for s in range(-3, b))
                four = n + has(b + 2)
                return n - 1, n, four, four + has(b - 1)

            s_banks, st_banks = bank(4, 2), bank(6, 2)

            with nc.Block() as block:
                @block.sync
                def _(sp):
                    sp.sem_inc(stored, 16)
                    sp.sem_inc(parts_stored, 32)

                    def store(c, a):
                        sp.wait_ge(parts_done, c * 2 + a + 1)
                        store_parts(sp, tok_parts[1][c, a:a + 1], parts[:, a:a + 1], parts_stored)

                    def step(b, x):
                        if has(b + 2):
                            store(b + 2, 0)
                        if has(b + 1):
                            c = b + 1
                            sp.wait_ge(nrow_done, c + 1)
                            sp.dma_start(shift1[c].rearrange("x c h l -> (x c h) l"), nrow[:]).then_inc(nrow_stored, 16)
                            sp.wait_ge(nrow_stored, c * 16 + 16)
                            for i in range(NT):
                                sp.dma_start(stacks[1 - x][0][STACK:FULL, :, i * P:(i + 1) * P], shift1[c, :, i])\
                                  .then_inc(shift_loaded, 16)
                        if has(b + 2):
                            c = b + 2
                            store(c, 1)
                            if has(b):
                                sp.wait_ge(st_ps, b * PR + PR)
                            sp.wait_ge(parts_stored, c * 32 + 64)
                            load_stack(sp, tok_parts[1][c, 0], stacks[x][0], Q_PARTS, stk_loaded)
                            load_stack(sp, tok_parts[1][c, 1], stacks[x][1], K_PARTS, stk_loaded)
                        if has(b - 1):
                            sp.wait_ge(res_done, b)
                            sp.dma_start(t["out"][b - 1].rearrange("(t p) d -> p t d", p=P), res[:]).then_inc(stored, 16)

                    pipeline(sp, step)
                    sp.wait_ge(stored, 16 * NB + 16)

                @block.gpsimd
                def _(pool):
                    pool.wait_ge(clear, 3)

                    def step(b, x):
                        _, attn, four, tern = layernorms(b)
                        if has(b + 2):
                            ln_rstd(pool, attn, ln_stat, pow_step, ln_rstd_done)
                        if has(b - 1):
                            ln_rstd(pool, four, ln_stat, pow_step, ln_rstd_done)
                        if has(b + 3):
                            ln_rstd(pool, tern, ln_stat, pow_step, ln_rstd_done)
                        if has(b + 2):
                            pool.wait_ge(v_done, b + 3)
                            if has(b):
                                pool.wait_ge(pv_ps, b * PR + PR)
                            for i in range(NT):
                                pool.tensor_tensor(va[x][:, i, :, 0:HD], heads(vst[:, i, :]), heads(bv[1][:]),
                                                   ALU.add).then_inc(va_done, 1)

                    pipeline(pool, step)

                @block.scalar
                def _(act):
                    def copy_yT(n):
                        act.wait_ge(yT_ps, n + 1)
                        act.activation(yT[:].rearrange("p k m -> p (k m)"), bank(0), ACT.Copy).then_inc(yT_done, 1)

                    def step(b, x):
                        _, attn, four, tern = layernorms(b)
                        for slot in range(PR + 1):
                            if has(b) and slot < PR:
                                act.wait_ge(st_ps, b * PR + slot + 1)
                                act.activation(pT[:, slot % 2], st_banks[:, :, 0:W3], ACT.Exp, scale=0.25).then_inc(exp_done, 1)
                            if slot == 6 and has(b + 2):
                                act.wait_ge(qkv_ps, b * 3 + 9)
                                if has(b + 1):
                                    act.wait_ge(va_done, (b + 2) * NT)
                                act.activation(vst[:].rearrange("p t d -> p (t d)"), bank(0), ACT.Copy).then_inc(v_done, 1)
                            if has(b) and slot % 2 == 0 and slot > 0:
                                act.wait_ge(pv_ps, b * PR + slot)
                                act.activation(xT[:, slot // 2 - 1, :], bank(3)[:, 0:L], ACT.Copy).then_inc(xT_done, 1)
                            if slot == 2 and has(b + 2):
                                copy_yT(attn)
                            if slot in (4, 5) and has(b + 2):
                                act.wait_ge(qkv_ps, b * 3 + slot + 3)
                                if slot == 4:
                                    act.wait_ge(parts_stored, (b + 2) * 32 + 32)
                                copy_qk(act, 1, q32, parts, qk_done, (slot - 4,))
                            if slot == 6 and has(b + 1):
                                act.wait_ge(nrow_ps, b + 2)
                                act.activation(nrow[:], bank(4)[0:SHIFT * NT * H, 0:P // 2].bitcast(BF16),
                                               ACT.Copy).then_inc(nrow_done, 1)
                            if slot == 6 and has(b - 1):
                                copy_yT(four)
                            if slot == 8 and has(b + 3):
                                copy_yT(tern)

                    pipeline(act, step)

                @block.vector
                def _(dve):
                    for x in range(2):
                        dve.memset(va[x][:], 0.0).then_inc(clear, 1)
                        dve.wait_ge(clear, x + 1)
                        dve.memset(va[x][:, :, :, ONE:ONE + 1], 1.0)
                        dve.memset(stacks[x][1][STACK:P], 1.0)
                    dve.memset(npad[:], 0.0).then_inc(clear, 1)

                    def maxima(c, *pairs):
                        if has(c):
                            for u in pairs:
                                dve.wait_ge(s_ps, c * PR + u + 1)
                                dve.tensor_reduce(nmax[:, :, 2 * u:2 * u + 2].rearrange("p c j -> p j c"),
                                                  s_banks[:, :, 0:W3].rearrange("p j (c n) -> p j c n", c=3),
                                                  axis=AX.X, op=ALU.max, negate=True).then_inc(nmax_done, 1)

                    def split(c, a):
                        dve.wait_ge(qk_done, c * 4 + 2 * a + 2)
                        dve.tensor_tensor(parts[:, a, 1], q32[:, a], parts[:, a, 0], ALU.subtract).then_inc(split_step, 1)
                        dve.tensor_tensor(rest[:, a], q32[:, a], parts[:, a, 0], ALU.subtract).then_inc(split_step, 1)
                        dve.wait_ge(split_step, c * 4 + 2 * a + 2)
                        dve.tensor_tensor(parts[:, a, 2], rest[:, a], parts[:, a, 1], ALU.subtract).then_inc(parts_done, 1)

                    def step(b, x):
                        _, attn, four, tern = layernorms(b)
                        if has(b + 2):
                            rows = bass.ds((b + 2) * NT, NT)
                            dve.wait_ge(ffn_ps, b + 3)
                            dve.tensor_tensor(h[:, rows, :], h[:, rows, :], bank(0).rearrange("p (t d) -> p t d", t=NT),
                                              ALU.add).then_inc(ffn_done, 1)
                            dve.wait_ge(ffn_done, b + 3)
                            dve.tensor_copy(passed[:], half[:])
                            ln_statistics(dve, b + 2, attn, ln_step, ln_stat)
                        if has(b - 1):
                            attention_out(dve, b - 1, 1, xo_ps, out_step, h_done)
                        if has(b + 2):
                            ln_scale(dve, b + 2, attn, ln_rstd_done, y_done)
                        maxima(b + 1, 0, 1)
                        if has(b - 1):
                            dve.wait_ge(h_done, b)
                            dve.tensor_copy(passed[:], half[:])
                            ln_statistics(dve, b - 1, four, ln_step, ln_stat)
                        maxima(b + 1, 2)
                        if has(b - 1):
                            dve.wait_ge(stored, b * 16)
                            dve.tensor_tensor(res[:], h[:, bass.ds((b - 1) * NT, NT), :],
                                              bf[:].unsqueeze(1).to_broadcast([P, NT, D]), ALU.add).then_inc(bias_done, 1)
                            if has(b + 2):
                                dve.wait_ge(yT_ps, attn + 1)
                        maxima(b + 1, 3)
                        if has(b - 1):
                            ln_scale(dve, b - 1, four, ln_rstd_done, y_done)
                        maxima(b + 1, 4, 5)
                        if has(b + 3):
                            ln_statistics(dve, b + 3, tern, ln_step, ln_stat)
                        maxima(b + 1, 6)
                        if has(b + 2):
                            split(b + 2, 0)
                        maxima(b + 1, 7)
                        if has(b + 1):
                            c = b + 1
                            dve.wait_ge(nmax_done, c * PR + PR)
                            dve.tensor_tensor(nmax[:, 1], nmax[:, 1], nmax[:, 2], ALU.min).then_inc(npart_step, 1)
                            dve.wait_ge(npart_step, c * 2 + 1)
                            dve.tensor_copy(nparts[:, 0], nmax[:, 0:2]).then_inc(npart_step, 1)
                            dve.wait_ge(npart_step, c * 2 + 2)
                            dve.tensor_tensor(nparts[:, 1], nmax[:, 0:2], nparts[:, 0], ALU.subtract).then_inc(nparts_done, 1)
                        if has(b + 2):
                            split(b + 2, 1)
                        if has(b - 1):
                            dve.wait_ge(bias_done, b)
                            dve.wait_ge(four_ps, b)
                            dve.tensor_tensor(res[:], res[:], bank(0).rearrange("p (t d) -> p t d", t=NT),
                                              ALU.add).then_inc(res_done, 1)
                        if has(b + 3):
                            ln_scale(dve, b + 3, tern, ln_rstd_done, y_done)

                    pipeline(dve, step)

                @block.tensor
                def _(pe):
                    pe.wait_ge(clear, 3)

                    def features(n):
                        pe.wait_ge(y_done, (n + 1) * NT)
                        transpose_y(pe, yT_ps)

                    def ffn(n, w, ready):
                        pe.wait_ge(yT_done, n + 1)
                        project_tokens(pe, 0, w).then_inc(ready, 1)

                    def block_logits(banks, x, u, transposed, ready):
                        q_, k_ = stacks[x]
                        left, right = (k_, q_) if transposed else (q_, k_)
                        rows = slice(0, FULL if transposed else STACK)
                        for j in range(2):
                            out = banks[:, j, :]
                            pe.matmul(out[:, 0:2 * P], identb[:], mask[:, int(transposed), :], start=True, stop=False)
                            for c, (q, k) in enumerate(((0, 0), (1, 1), (1, 0))):
                                l, r = (k, q) if transposed else (q, k)
                                last = pe.matmul(out[:, c * P:(c + 1) * P], left[rows, 2 * u + j, l * P:(l + 1) * P],
                                                 right[rows, 2 * u + j, r * P:(r + 1) * P], start=False, stop=c == 2)
                        last.then_inc(ready, 1)

                    def logits(c, x, u):
                        if has(c):
                            if u > 0:
                                pe.wait_ge(nmax_done, c * PR + u)
                            else:
                                pe.wait_ge(stk_loaded, (c + 1) * NSTK1)
                                if has(c - 1):
                                    pe.wait_ge(nrow_done, c)
                            block_logits(s_banks, x, u, False, s_ps)

                    def transposed_logits(b, x, u):
                        if u == 0:
                            pe.wait_ge(shift_loaded, (b + 1) * (16 * NT))
                        if u > 0 or has(b - 1):
                            pe.wait_ge(exp_done, b * PR + u)
                        block_logits(st_banks, x, u, True, st_ps)

                    def weighted_values(b, x, u):
                        pe.wait_ge(exp_done, b * PR + u + 1)
                        if u == 0:
                            pe.wait_ge(va_done, (b + 1) * NT)
                        if u % 2 == 0 and (u > 0 or has(b - 1)):
                            pe.wait_ge(xT_done, b * G + u // 2)
                        for j in range(2):
                            head = 2 * u + j
                            slot = SLOT * (head % J)
                            out = bank(3)[slot:slot + SLOT, :]
                            v = [va[x][:, i, head, :] for i in range(NT)]
                            pe.matmul(out[:, 0:P], v[0], pT[:, u % 2, j, 0:P], start=True, stop=True)
                            pe.matmul(out[:, P:L], v[0], pT[:, u % 2, j, 2 * P:W3], start=True, stop=False)
                            last = pe.matmul(out[:, P:L], v[1], pT[:, u % 2, j, P:2 * P], start=False, stop=True)
                        last.then_inc(pv_ps, 1)

                    def step(b, x):
                        tern_before, attn, four, tern = layernorms(b)
                        for slot in range(PR + 1):
                            if has(b) and slot < PR:
                                transposed_logits(b, x, slot)
                            if 2 <= slot <= 5:
                                logits(b + 1, 1 - x, 2 * slot - 4)
                            if has(b) and slot > 0:
                                weighted_values(b, x, slot - 1)
                            if slot == 0 and has(b + 2):
                                ffn(tern_before, wt, ffn_ps)
                            if slot == 0 and has(b - 1):
                                pe.wait_ge(xT_done, b * G)
                                if has(b + 1):
                                    pe.wait_ge(qk_done, (b + 2) * 4)
                                else:
                                    pe.wait_ge(h_done, b - 1)
                                heads_to_tokens(pe, 1, xo_ps)
                            if slot == 2 and has(b + 2):
                                features(attn)
                            if slot == 3 and has(b + 2):
                                pe.wait_ge(yT_done, attn + 1)
                                if has(b + 1):
                                    pe.wait_ge(qk_done, (b + 2) * 4)
                                if has(b - 1):
                                    pe.wait_ge(h_done, b)
                                project_features(pe, 1, wq[1]).then_inc(qkv_ps, 1)
                            if slot == 4 and has(b + 2):
                                project_features(pe, 2, wk[1]).then_inc(qkv_ps, 1)
                            if slot == 5 and has(b + 2):
                                project_tokens(pe, 0, wv[1]).then_inc(qkv_ps, 1)
                            if 2 <= slot <= 5:
                                logits(b + 1, 1 - x, 2 * slot - 3)
                            if slot == 6 and has(b + 1):
                                pe.wait_ge(nparts_done, b + 2)
                                pe.transpose(bank(4)[:, 0:P // 2].bitcast(BF16), npad[:], identb[:]).then_inc(nrow_ps, 1)
                            if slot == 6 and has(b - 1):
                                if has(b + 2):
                                    pe.wait_ge(v_done, b + 3)
                                elif has(b - 2):
                                    pe.wait_ge(res_done, b - 1)
                                features(four)
                            if slot == 7 and has(b - 1):
                                ffn(four, wf, four_ps)
                            if slot == 8 and has(b + 3):
                                if has(b + 2):
                                    pe.wait_ge(v_done, b + 3)
                                if has(b - 1):
                                    pe.wait_ge(res_done, b)
                                features(tern)

                    pipeline(pe, step)


def host_arrays(inputs):
    f = np.float32
    a = {k: np.asarray(v) for k, v in inputs.items()}
    ids = a["x"]
    out = {"ids": ids.reshape(1, NB * L)}
    pos = np.pad(np.arange(L), NFFT // 2, mode="reflect").reshape(NFR, NFFT)
    out["ids_fr"] = np.ascontiguousarray(ids[:, pos].reshape(2, PAIRS, NFFT).transpose(2, 1, 0).reshape(NFFT, 2 * PAIRS))
    out["iota"] = np.arange(V, dtype=f).reshape(1, V)
    out["iota_c"] = np.arange(V, dtype=f).reshape(V, 1)
    ang = 2 * np.pi * np.outer(np.arange(NFFT), np.arange(NFQ)) / NFFT
    out["dft"] = np.stack([np.cos(ang), -np.sin(ang)], 1).astype(f)
    out["window"] = a["L0_tok_window"].reshape(NFFT, 1)
    w = a["L0_tok_proj_w"].reshape(DS, NFQ, V).transpose(2, 1, 0)
    out["wp"] = np.ascontiguousarray(np.concatenate([w, w], 0))
    out["emb"] = a["L0_tok_emb_table"]
    out["proj_b"] = a["L0_tok_proj_b"].reshape(1, DS)
    coord = np.clip((np.arange(L, dtype=f) + f(0.5)) * f(NFR / L) - f(0.5), 0.0, NFR - 1.0)
    i0 = np.floor(coord).astype(np.int32)
    i1 = np.minimum(i0 + 1, NFR - 1)
    wgt = (coord - i0).astype(f)
    up = np.zeros((NFR, L), f)
    np.add.at(up, (i0, np.arange(L)), 1 - wgt)
    np.add.at(up, (i1, np.arange(L)), wgt)
    interp = np.zeros((PAIRS + 1, NB, L), f)
    for b in range(NB):
        first = b % (NB // 2) * NFR
        interp[first:first + NFR, b] = up
    interp[PAIRS] = 1.0
    out["interp"] = interp.reshape(PAIRS + 1, NB * L)
    out["ident"] = np.eye(P, dtype=f)
    out["half"] = np.tile(np.array([-0.5, -0.5, EPS, EPS], f), (P, 1))
    up_m = np.triu(np.full((P, P), NEG, f), 1)
    out["mask"] = np.stack([np.concatenate([m, m], 1) for m in (up_m, up_m.T)], 1)

    def tiles(w):
        return np.ascontiguousarray(w.reshape(NK, P, w.shape[1]).transpose(1, 0, 2))

    by_dimension = np.arange(D).reshape(H // 2, 2, HD).transpose(1, 2, 0).reshape(D)
    for n in range(2):
        for name in "qkv":
            w = a[f"L{n}_attn_W{name}"].reshape(D, D).T
            b = a[f"L{n}_attn_b{name}"].reshape(D)
            if name != "v":
                w, b = w[:, by_dimension], b[by_dimension]
            if name == "v":
                out[f"wv{n}"], out[f"bv{n}"] = tiles(w), b.reshape(1, D)
                continue
            out[f"w{name}{n}"] = tiles(w)
            out[f"b{name}{n}"] = np.ascontiguousarray(b.reshape(2, P).T)
    out["fw"] = tiles(a["L0_ffn_weight"].T)
    ang = 2 * np.pi * ((np.outer(np.arange(D), np.arange(D))) % D) / D
    out["cs"] = np.ascontiguousarray(np.stack([tiles(m.astype(f)) for m in (np.cos(ang), np.sin(ang), -np.sin(ang))], 1))
    out["wri"] = np.ascontiguousarray(np.stack([tiles(a["L1_ffn_w_freq_real"]), tiles(a["L1_ffn_w_freq_imag"])], 1))
    out["bf"] = a["L1_ffn_bias"].reshape(1, D)
    return {k: np.ascontiguousarray(v) for k, v in out.items()}


def kernel(**inputs):
    import concourse.bacc as bacc
    from concourse.bass_utils import run_bass_kernel_spmd

    nc = bacc.Bacc("TRN2", target_bir_lowering=False, num_devices=1)
    arrays = host_arrays(inputs)
    t = {name: nc.dram_tensor(f"in_{name}", a.shape, mybir.dt.from_np(a.dtype), kind="ExternalInput").ap()
         for name, a in arrays.items()}
    t["out"] = nc.dram_tensor("out", (NB, L, D), F32, kind="ExternalOutput").ap()
    build(nc, t)
    r = run_bass_kernel_spmd(nc, [{f"in_{k}": v for k, v in arrays.items()}], core_ids=[0])
    return r.results[0]["out"]
```
